# Optimizing a Trainium2 kernel written in Bass

```python
import numpy as np
import jax
import jax.numpy as jnp

def _softmax(x, axis=-1):
    return jax.nn.softmax(x, axis=axis)

def _gelu(x):
    return jax.nn.gelu(x, approximate=True)

def _silu(x):
    return jax.nn.silu(x)

def _sigmoid(x):
    return jax.nn.sigmoid(x)

def _layernorm(x, axis=-1, eps=1e-05):
    m = jnp.mean(x, axis=axis, keepdims=True)
    v = jnp.var(x, axis=axis, keepdims=True)
    return (x - m) / jnp.sqrt(v + eps)

def _scatter_add(tgt, idx, src, axis=0):
    return tgt.at[idx].add(src)

def _segment_sum(src, seg, n):
    return jax.ops.segment_sum(src, seg, n)
kernel_name = 'mk_perceiver_d1_seqx_r2_6349e6'

def setup_inputs(seed: int=0):
    np.random.seed(seed)
    _w = jnp.asarray

    def _rec_inputs():
        import jax
        import jax.numpy as jnp
        _rk = jax.random.key(seed)
        x = -0.000125 + 0.9999 * jax.random.normal(jax.random.fold_in(_rk, 1), (16, 64, 512), jnp.float32)
        _lenS = 64 - jax.random.randint(jax.random.fold_in(_rk, 7), (16,), 0, max(1, 64 // 4) + 1, jnp.int32)
        _lenS2 = 1601 - jax.random.randint(jax.random.fold_in(_rk, 8), (16,), 0, max(1, 1601 // 4) + 1, jnp.int32)
        _ctx_1024P = jax.random.normal(jax.random.fold_in(_rk, 11), (16, 16, 512), jnp.float32)
        _ctx_1024c = jax.random.dirichlet(jax.random.fold_in(_rk, 511), 0.3 * jnp.ones((16,), jnp.float32), (16, 1601))
        _ctx_1024t = jnp.einsum('bsk,bkd->bsd', _ctx_1024c, _ctx_1024P)
        _ctx_1024t = _ctx_1024t * jax.lax.rsqrt(jnp.mean(jnp.square(_ctx_1024t)) + 1e-12) * 0.953939
        ctx_1024 = -1.52775e-05 + 0.999936 * (_ctx_1024t + 0.3 * jax.random.normal(jax.random.fold_in(_rk, 611), (16, 1601, 512), jnp.float32))
        return (x, ctx_1024)
    x, ctx_1024 = _rec_inputs()

    def _L0_xattn_setup():
        import jax, jax.numpy as jnp
        import numpy as np
        key = jax.random.key(seed)
        k1, k2 = jax.random.split(key)
        B, Tq, Ts, H = (16, 1024, 1024, 512)
        hidden = jax.random.normal(k1, (B, Tq, H), dtype=jnp.float32)
        encoder_outputs = jax.random.normal(k2, (B, Ts, H), dtype=jnp.float32)
        return {'hidden': hidden, 'encoder_outputs': encoder_outputs}
    _L0_xattn_all = _L0_xattn_setup()
    _L0_xattn_in = {k: v for k, v in _L0_xattn_all.items() if k in ()}
    del _L0_xattn_all

    def _L0_attn_setup():
        import math
        import jax, jax.numpy as jnp
        import numpy as np
        SEQ, BATCH, D_MODEL, NHEAD, FEAT = (1024, 2, 512, 8, 128)

        def _sinusoid_pe(length, d_model, dtype):
            pos = jnp.arange(length, dtype=dtype)[:, None]
            div = jnp.exp(jnp.arange(0, d_model, 2, dtype=dtype) * (-math.log(10000.0) / d_model))
            ang = pos * div
            return jnp.stack([jnp.sin(ang), jnp.cos(ang)], axis=-1).reshape(length, d_model)

        def _left_shift(x):
            I, J, B, N = x.shape
            zero = jnp.zeros((I, 1, B, N), x.dtype)
            padded = jnp.concatenate([zero, x], axis=1)
            padded = padded.reshape(J + 1, I, B, N)[1:]
            x = padded.reshape(I, J, B, N)
            return jnp.tril(x)
        key = jax.random.key(seed)
        ks = jax.random.split(key, 8)
        s = 0.02
        return {'x': jax.random.normal(ks[0], (SEQ, BATCH, D_MODEL), dtype=jnp.float32), 'gamma': jnp.ones((D_MODEL,), jnp.float32), 'beta': jnp.zeros((D_MODEL,), jnp.float32), 'Wq': jax.random.normal(ks[1], (D_MODEL, NHEAD * FEAT), jnp.float32) * s, 'Wv': jax.random.normal(ks[2], (D_MODEL, NHEAD * FEAT), jnp.float32) * s, 'Wr': jax.random.normal(ks[3], (D_MODEL, NHEAD * FEAT), jnp.float32) * s, 'u_bias': jax.random.normal(ks[4], (NHEAD, FEAT), jnp.float32) * s, 'v_bias': jax.random.normal(ks[5], (NHEAD, FEAT), jnp.float32) * s, 'Wout': jax.random.normal(ks[6], (NHEAD * FEAT, D_MODEL), jnp.float32) * s, 'bout': jnp.zeros((D_MODEL,), jnp.float32)}
    _L0_attn_all = _L0_attn_setup()
    _L0_attn_in = {k: v for k, v in _L0_attn_all.items() if k in ('gamma', 'beta', 'Wq', 'Wv', 'Wr', 'u_bias', 'v_bias', 'Wout', 'bout')}
    del _L0_attn_all

    def _L0_ffn_setup():
        import jax, jax.numpy as jnp
        import numpy as np
        H = 512
        NH = 16
        HD = H // NH
        HH = HD // 2
        L = H // 4
        I = int(H * 1.0)
        ER = 7
        TOPK = 2
        BASE = 10000.0
        EPS = 1e-05

        def rmsnorm(x, w):
            norm = jnp.sqrt(jnp.mean(x * x, axis=-1, keepdims=True)) + EPS
            return x / norm * w

        def rope_tables(seq_len):
            inv_freq = 1.0 / BASE ** (jnp.arange(0, HH, 2, dtype=jnp.float32) / HH)
            t = jnp.arange(seq_len, dtype=jnp.float32)
            freqs = jnp.einsum('i,j->ij', t, inv_freq)
            emb = jnp.concatenate([freqs, freqs], axis=-1)
            cos = jnp.cos(emb)[None, :, None, :]
            sin = jnp.sin(emb)[None, :, None, :]
            return (cos, sin)

        def rotate_half(x):
            x1, x2 = jnp.split(x, 2, axis=-1)
            return jnp.concatenate([-x2, x1], axis=-1)

        def silu(x):
            return x * jax.nn.sigmoid(x)

        def mla(xn, W_kvd, W_qd, W_ku, W_qu, W_vu, W_ropeq, W_ropek, W_o):
            B, S, _ = xn.shape
            kv_lat = xn @ W_kvd
            q_lat = xn @ W_qd
            k = (kv_lat @ W_ku).reshape(B, S, NH, HH)
            q = (q_lat @ W_qu).reshape(B, S, NH, HH)
            v = (kv_lat @ W_vu).reshape(B, S, NH, HD)
            q_rope = (q_lat @ W_ropeq).reshape(B, S, NH, HH)
            k_rope = (xn @ W_ropek).reshape(B, S, NH, HH)
            cos, sin = rope_tables(S)
            k_rope = k_rope * cos + rotate_half(k_rope) * sin
            q_rope = q_rope * cos + rotate_half(q_rope) * sin
            kk = jnp.concatenate([k, k_rope], axis=-1)
            qq = jnp.concatenate([q, q_rope], axis=-1)
            scale = 1.0 / jnp.sqrt(jnp.float32(HD))
            scores = jnp.einsum('bqhd,bkhd->bhqk', qq, kk) * scale
            causal = jnp.tril(jnp.ones((S, S), dtype=bool))
            scores = jnp.where(causal[None, None], scores, jnp.finfo(scores.dtype).min)
            probs = jax.nn.softmax(scores, axis=-1)
            y = jnp.einsum('bhqk,bkhd->bqhd', probs, v).reshape(B, S, H)
            return y @ W_o

        def moe(xn, Wg_s, Wu_s, Wd_s, Wg_r, Wu_r, Wd_r, W_router, routing_bias):
            B, S, _ = xn.shape
            xt = xn.reshape(B * S, H)
            shared = silu(xt @ Wg_s) * (xt @ Wu_s) @ Wd_s
            logits = xt @ W_router + routing_bias
            probs = jax.nn.sigmoid(logits)
            scores, idx = jax.lax.top_k(probs, TOPK)
            scores = scores / jnp.sum(scores, axis=-1, keepdims=True)
            wts = jnp.sum(jax.nn.one_hot(idx, ER, dtype=xt.dtype) * scores[..., None], axis=1)
            g = jnp.einsum('th,ehi->tei', xt, Wg_r)
            u = jnp.einsum('th,ehi->tei', xt, Wu_r)
            hmid = silu(g) * u
            combined = jnp.einsum('tei,eih,te->th', hmid, Wd_r, wts)
            return (shared + combined).reshape(B, S, H)
        key = jax.random.key(seed)
        ks = jax.random.split(key, 20)
        s = 0.02
        r = lambda k, shp: jax.random.normal(k, shp, dtype=jnp.float32) * s
        return {'x': jax.random.normal(ks[0], (4, 512, H), dtype=jnp.float32), 'w_ln1': jnp.ones((H,), jnp.float32), 'w_ln2': jnp.ones((H,), jnp.float32), 'W_kvd': r(ks[1], (H, L)), 'W_qd': r(ks[2], (H, L)), 'W_ku': r(ks[3], (L, NH * HH)), 'W_qu': r(ks[4], (L, NH * HH)), 'W_vu': r(ks[5], (L, H)), 'W_ropeq': r(ks[6], (L, H // 2)), 'W_ropek': r(ks[7], (H, H // 2)), 'W_o': r(ks[8], (H, H)), 'Wg_s': r(ks[9], (H, I)), 'Wu_s': r(ks[10], (H, I)), 'Wd_s': r(ks[11], (I, H)), 'Wg_r': r(ks[12], (ER, H, I)), 'Wu_r': r(ks[13], (ER, H, I)), 'Wd_r': r(ks[14], (ER, I, H)), 'W_router': r(ks[15], (H, ER)), 'routing_bias': jnp.zeros((ER,), jnp.float32)}
    _L0_ffn_all = _L0_ffn_setup()
    _L0_ffn_in = {k: v for k, v in _L0_ffn_all.items() if k in ('w_ln1', 'w_ln2', 'W_kvd', 'W_qd', 'W_ku', 'W_qu', 'W_vu', 'W_ropeq', 'W_ropek', 'W_o', 'Wg_s', 'Wu_s', 'Wd_s', 'Wg_r', 'Wu_r', 'Wd_r', 'W_router', 'routing_bias')}
    del _L0_ffn_all
    return {'x': x, 'ctx_1024': ctx_1024, 'L0_attn_gamma': _L0_attn_in['gamma'], 'L0_attn_beta': _L0_attn_in['beta'], 'L0_attn_Wq': _L0_attn_in['Wq'], 'L0_attn_Wv': _L0_attn_in['Wv'], 'L0_attn_Wr': _L0_attn_in['Wr'], 'L0_attn_u_bias': _L0_attn_in['u_bias'], 'L0_attn_v_bias': _L0_attn_in['v_bias'], 'L0_attn_Wout': _L0_attn_in['Wout'], 'L0_attn_bout': _L0_attn_in['bout'], 'L0_ffn_w_ln1': _L0_ffn_in['w_ln1'], 'L0_ffn_w_ln2': _L0_ffn_in['w_ln2'], 'L0_ffn_W_kvd': _L0_ffn_in['W_kvd'], 'L0_ffn_W_qd': _L0_ffn_in['W_qd'], 'L0_ffn_W_ku': _L0_ffn_in['W_ku'], 'L0_ffn_W_qu': _L0_ffn_in['W_qu'], 'L0_ffn_W_vu': _L0_ffn_in['W_vu'], 'L0_ffn_W_ropeq': _L0_ffn_in['W_ropeq'], 'L0_ffn_W_ropek': _L0_ffn_in['W_ropek'], 'L0_ffn_W_o': _L0_ffn_in['W_o'], 'L0_ffn_Wg_s': _L0_ffn_in['Wg_s'], 'L0_ffn_Wu_s': _L0_ffn_in['Wu_s'], 'L0_ffn_Wd_s': _L0_ffn_in['Wd_s'], 'L0_ffn_Wg_r': _L0_ffn_in['Wg_r'], 'L0_ffn_Wu_r': _L0_ffn_in['Wu_r'], 'L0_ffn_Wd_r': _L0_ffn_in['Wd_r'], 'L0_ffn_W_router': _L0_ffn_in['W_router'], 'L0_ffn_routing_bias': _L0_ffn_in['routing_bias']}

def reference(x, ctx_1024, L0_attn_gamma, L0_attn_beta, L0_attn_Wq, L0_attn_Wv, L0_attn_Wr, L0_attn_u_bias, L0_attn_v_bias, L0_attn_Wout, L0_attn_bout, L0_ffn_w_ln1, L0_ffn_w_ln2, L0_ffn_W_kvd, L0_ffn_W_qd, L0_ffn_W_ku, L0_ffn_W_qu, L0_ffn_W_vu, L0_ffn_W_ropeq, L0_ffn_W_ropek, L0_ffn_W_o, L0_ffn_Wg_s, L0_ffn_Wu_s, L0_ffn_Wd_s, L0_ffn_Wg_r, L0_ffn_Wu_r, L0_ffn_Wd_r, L0_ffn_W_router, L0_ffn_routing_bias):
    import jax
    import jax.numpy as jnp

    def _L0_xattn_ref(hidden, encoder_outputs):
        import jax, jax.numpy as jnp
        import numpy as np
        scores = jnp.einsum('bsh,bqh->bsq', encoder_outputs, hidden)
        attn_weights = jax.nn.softmax(scores, axis=1)
        context = jnp.einsum('bsq,bsh->bqh', attn_weights, encoder_outputs)
        return context

    def _L0_attn_ref(x, gamma, beta, Wq, Wv, Wr, u_bias, v_bias, Wout, bout):
        import math
        import jax, jax.numpy as jnp
        import numpy as np
        SEQ, BATCH, D_MODEL, NHEAD, FEAT = (1024, 2, 512, 8, 128)

        def _sinusoid_pe(length, d_model, dtype):
            pos = jnp.arange(length, dtype=dtype)[:, None]
            div = jnp.exp(jnp.arange(0, d_model, 2, dtype=dtype) * (-math.log(10000.0) / d_model))
            ang = pos * div
            return jnp.stack([jnp.sin(ang), jnp.cos(ang)], axis=-1).reshape(length, d_model)

        def _left_shift(x):
            I, J, B, N = x.shape
            zero = jnp.zeros((I, 1, B, N), x.dtype)
            padded = jnp.concatenate([zero, x], axis=1)
            padded = padded.reshape(J + 1, I, B, N)[1:]
            x = padded.reshape(I, J, B, N)
            return jnp.tril(x)
        I, B, D = x.shape
        H, F = u_bias.shape
        sqrt_d = jnp.asarray(math.sqrt(D), x.dtype)
        mu = jnp.mean(x, axis=-1, keepdims=True)
        var = jnp.mean((x - mu) ** 2, axis=-1, keepdims=True)
        h = (x - mu) * jax.lax.rsqrt(var + 1e-05) * gamma + beta
        pe = _sinusoid_pe(I, D, x.dtype)[::-1]
        q = (h @ Wq).reshape(I, B, H, F)
        k = (h @ Wq).reshape(I, B, H, F)
        v = (h @ Wv).reshape(I, B, H, F)
        r = (pe @ Wr).reshape(I, H, F)
        content = jnp.einsum('ibnf,jbnf->ijbn', q + u_bias, k)
        pos = jnp.einsum('ibnf,jnf->ijbn', q + v_bias, r)
        pos = _left_shift(pos)
        attn = jax.nn.softmax((content + pos) / sqrt_d, axis=1)
        o = jnp.einsum('ijbn,jbnf->ibnf', attn, v).reshape(I, B, H * F)
        return o @ Wout + bout

    def _L0_ffn_ref(x, w_ln1, w_ln2, W_kvd, W_qd, W_ku, W_qu, W_vu, W_ropeq, W_ropek, W_o, Wg_s, Wu_s, Wd_s, Wg_r, Wu_r, Wd_r, W_router, routing_bias):
        import jax, jax.numpy as jnp
        import numpy as np
        H = 512
        NH = 16
        HD = H // NH
        HH = HD // 2
        L = H // 4
        I = int(H * 1.0)
        ER = 7
        TOPK = 2
        BASE = 10000.0
        EPS = 1e-05

        def rmsnorm(x, w):
            norm = jnp.sqrt(jnp.mean(x * x, axis=-1, keepdims=True)) + EPS
            return x / norm * w

        def rope_tables(seq_len):
            inv_freq = 1.0 / BASE ** (jnp.arange(0, HH, 2, dtype=jnp.float32) / HH)
            t = jnp.arange(seq_len, dtype=jnp.float32)
            freqs = jnp.einsum('i,j->ij', t, inv_freq)
            emb = jnp.concatenate([freqs, freqs], axis=-1)
            cos = jnp.cos(emb)[None, :, None, :]
            sin = jnp.sin(emb)[None, :, None, :]
            return (cos, sin)

        def rotate_half(x):
            x1, x2 = jnp.split(x, 2, axis=-1)
            return jnp.concatenate([-x2, x1], axis=-1)

        def silu(x):
            return x * jax.nn.sigmoid(x)

        def mla(xn, W_kvd, W_qd, W_ku, W_qu, W_vu, W_ropeq, W_ropek, W_o):
            B, S, _ = xn.shape
            kv_lat = xn @ W_kvd
            q_lat = xn @ W_qd
            k = (kv_lat @ W_ku).reshape(B, S, NH, HH)
            q = (q_lat @ W_qu).reshape(B, S, NH, HH)
            v = (kv_lat @ W_vu).reshape(B, S, NH, HD)
            q_rope = (q_lat @ W_ropeq).reshape(B, S, NH, HH)
            k_rope = (xn @ W_ropek).reshape(B, S, NH, HH)
            cos, sin = rope_tables(S)
            k_rope = k_rope * cos + rotate_half(k_rope) * sin
            q_rope = q_rope * cos + rotate_half(q_rope) * sin
            kk = jnp.concatenate([k, k_rope], axis=-1)
            qq = jnp.concatenate([q, q_rope], axis=-1)
            scale = 1.0 / jnp.sqrt(jnp.float32(HD))
            scores = jnp.einsum('bqhd,bkhd->bhqk', qq, kk) * scale
            causal = jnp.tril(jnp.ones((S, S), dtype=bool))
            scores = jnp.where(causal[None, None], scores, jnp.finfo(scores.dtype).min)
            probs = jax.nn.softmax(scores, axis=-1)
            y = jnp.einsum('bhqk,bkhd->bqhd', probs, v).reshape(B, S, H)
            return y @ W_o

        def moe(xn, Wg_s, Wu_s, Wd_s, Wg_r, Wu_r, Wd_r, W_router, routing_bias):
            B, S, _ = xn.shape
            xt = xn.reshape(B * S, H)
            shared = silu(xt @ Wg_s) * (xt @ Wu_s) @ Wd_s
            logits = xt @ W_router + routing_bias
            probs = jax.nn.sigmoid(logits)
            scores, idx = jax.lax.top_k(probs, TOPK)
            scores = scores / jnp.sum(scores, axis=-1, keepdims=True)
            wts = jnp.sum(jax.nn.one_hot(idx, ER, dtype=xt.dtype) * scores[..., None], axis=1)
            g = jnp.einsum('th,ehi->tei', xt, Wg_r)
            u = jnp.einsum('th,ehi->tei', xt, Wu_r)
            hmid = silu(g) * u
            combined = jnp.einsum('tei,eih,te->th', hmid, Wd_r, wts)
            return (shared + combined).reshape(B, S, H)
        x = x + mla(rmsnorm(x, w_ln1), W_kvd, W_qd, W_ku, W_qu, W_vu, W_ropeq, W_ropek, W_o)
        x = x + moe(rmsnorm(x, w_ln2), Wg_s, Wu_s, Wd_s, Wg_r, Wu_r, Wd_r, W_router, routing_bias)
        return x
    x = x + _L0_xattn_ref(_layernorm(x, axis=-1), ctx_1024)
    x = x + _L0_attn_ref(_layernorm(x, axis=-1), L0_attn_gamma, L0_attn_beta, L0_attn_Wq, L0_attn_Wv, L0_attn_Wr, L0_attn_u_bias, L0_attn_v_bias, L0_attn_Wout, L0_attn_bout)
    x = x + _L0_ffn_ref(_layernorm(x, axis=-1), L0_ffn_w_ln1, L0_ffn_w_ln2, L0_ffn_W_kvd, L0_ffn_W_qd, L0_ffn_W_ku, L0_ffn_W_qu, L0_ffn_W_vu, L0_ffn_W_ropeq, L0_ffn_W_ropek, L0_ffn_W_o, L0_ffn_Wg_s, L0_ffn_Wu_s, L0_ffn_Wd_s, L0_ffn_Wg_r, L0_ffn_Wu_r, L0_ffn_Wd_r, L0_ffn_W_router, L0_ffn_routing_bias)
    return x

_drawn_inputs = setup_inputs


def setup_inputs(seed=0):
    import zlib

    import numpy as np

    out = dict(_drawn_inputs(seed))
    spreads = {'L0_attn_gamma': (1.0, 0.6),
     'L0_attn_beta': (0.0, 0.517),
     'L0_attn_bout': (0.0, 0.1),
     'L0_ffn_w_ln1': (1.0, 0.6),
     'L0_ffn_w_ln2': (1.0, 0.6),
     'L0_ffn_routing_bias': (0.0, 0.8)}
    factors = {'L0_attn_Wq': 8.0,
     'L0_attn_Wr': 8.0,
     'L0_attn_u_bias': 8.0,
     'L0_attn_v_bias': 8.0,
     'L0_ffn_W_kvd': 7.955,
     'L0_ffn_W_qd': 8.0,
     'L0_ffn_W_ku': 8.0,
     'L0_ffn_W_qu': 8.0,
     'L0_ffn_W_vu': 7.763,
     'L0_ffn_W_ropeq': 8.0,
     'L0_ffn_W_ropek': 8.0,
     'L0_ffn_W_o': 7.983,
     'L0_ffn_Wg_s': 2.97,
     'L0_ffn_Wu_s': 2.881,
     'L0_ffn_Wd_s': 2.895,
     'L0_ffn_Wg_r': 4.176,
     'L0_ffn_Wu_r': 4.082,
     'L0_ffn_Wd_r': 4.08,
     'L0_ffn_W_router': 4.794}
    for name, (base, spread) in spreads.items():
        noise = np.random.default_rng([zlib.crc32(name.encode()), seed]).standard_normal(out[name].shape)
        drawn = base * np.exp(spread * noise) if base else spread * noise
        out[name] = jnp.asarray(drawn.astype(out[name].dtype))
    for name, factor in factors.items():
        out[name] = (out[name] * factor).astype(out[name].dtype)
    return out
```

```python
from contextlib import ExitStack

import numpy as np

import concourse.bass as bass
from concourse import mybir
from concourse.alu_op_type import AluOpType as ALU

F32 = mybir.dt.float32
F32R = mybir.dt.float32r
BF16 = mybir.dt.bfloat16
I32 = mybir.dt.int32
ACT = mybir.ActivationFunctionType
AX = mybir.AxisListType.X
ds = bass.ds

P = 128
D = 512
HC = D // P
TOK = 16 * 64
NT = TOK // P
SQ = 64
SK = 1601
JM = SK // P
TAIL = SK - JM * P
JT = JM + 1
S_CHUNKS = [(0, 401), (401, 400), (801, 400), (1201, 400)]
RING = 3
T_FILLS = 2 * JT
P_FILLS = -(-JT // 4)
BLOCK = T_FILLS + P_FILLS
assert BLOCK % RING == 0 and BLOCK % 2 == 0
NG, GB, NH, F, SEQ = 8, 8, 8, 128, 16
BATCH = NG * GB
ATT_SCALE = D ** -0.5
LN_EPS = 1e-5
V_GAMMA, V_BETA, V_W1, V_W2, V_U, V_V, V_END = 0, 4, 8, 12, 16, 24, 32
NEG = -1e30

HEADS, HD, RD, LAT = 16, 32, 16, 128
QUADS = HEADS // 4
SELF_SCALE = HD ** -0.5
RMS_EPS = 1e-5
NE = 8
NR = NE - 1
HALF = TOK // 2
NJ = 2 * HC
C_IDENT, C_PE, C_BLOCK, C_CAUSAL, C_COS, C_SIN, C_TRIL, C_RANK, C_END = np.cumsum(
    [0, P, HC * 16, P, P, 16, 16, 8, 8]).tolist()


def shape_constants():
    c = np.zeros((P, C_END), np.float32)
    c[:, C_IDENT:C_IDENT + P] = np.eye(P)
    pos = np.arange(16, dtype=np.float32)[:, None]
    div = np.exp(np.arange(0, D, 2, dtype=np.float32) * np.float32(-np.log(10000.0) / D))
    ang = pos * div
    pe = np.stack([np.sin(ang), np.cos(ang)], axis=-1).reshape(16, D)[::-1]
    c[:, C_PE:C_PE + HC * 16] = pe.T.reshape(HC, P, 16).transpose(1, 0, 2).reshape(P, HC * 16)
    p, q = np.arange(P)[:, None], np.arange(P)[None, :]
    c[:, C_BLOCK:C_BLOCK + P] = np.where(p % 8 == q % 8, 0.0, NEG)
    c[:, C_CAUSAL:C_CAUSAL + P] = np.where((p // 64 == q // 64) & (q <= p), 0.0, NEG)
    inv = (1.0 / np.float32(10000.0) ** (np.arange(0, 16, 2, dtype=np.float32) / np.float32(16))).astype(np.float32)
    f = (np.arange(P) % 64).astype(np.float32)[:, None] * inv[None, :]
    c[:, C_COS:C_COS + 16] = np.concatenate([np.cos(f), np.cos(f)], 1)
    c[:, C_SIN:C_SIN + 16] = np.concatenate([-np.sin(f), np.sin(f)], 1)
    c[:, C_TRIL:C_TRIL + 8] = (np.arange(8)[None, :] <= p % 64)
    c[:, C_RANK:C_RANK + 8] = 8 - np.arange(8)
    return c


class Steps:

    def __init__(self, eng, sem):
        self.eng, self.sem, self.base, self.n = eng, sem, 0, 0

    def mark(self, ins):
        ins.then_inc(self.sem, 1)
        self.n += 1

    def wait(self):
        self.eng.wait_ge(self.sem, self.base + self.n)

    def __call__(self, ins):
        self.mark(ins)
        self.wait()

    def enter(self):
        self.start, self.n = self.base + self.n, 0

    def turn(self, i, per):
        self.base, self.n, self.per = self.start + i * per, 0, per

    def leave(self, turns):
        assert self.n == self.per, self.n
        self.base, self.n = self.start + turns * self.per, 0


def perceiver_kernel(nc, x, ctx_keys, consts, vecs, rows, Wq, Wv, Wr, Wout, Wkvd, Wqd, Wku, Wqu, Wvu, Wropeq, Wropek,
                     Wo, Wexp, Wrouter, out):
    with ExitStack() as ctx:
        def sem(name):
            return ctx.enter_context(nc.semaphore(name))

        def sbuf(scope, name, shape, dt=F32):
            return scope.enter_context(nc.sbuf_tensor(name, shape, dt))

        bank = [ctx.enter_context(nc.psum_tensor(f"bank{i}", [P, 512], F32)) for i in range(8)]

        y = sbuf(ctx, "y", [P, NT, D])
        cst = sbuf(ctx, "cst", [P, C_END])
        ident = cst[:, C_IDENT:C_IDENT + P]
        stats = sbuf(ctx, "stats", [P, NT, 6])
        mv = sbuf(ctx, "mv", [P, NT, 2])
        mean, var = mv[:, :, 0], mv[:, :, 1]
        rstd = sbuf(ctx, "rstd", [P, NT])
        rs_v = sbuf(ctx, "rs_v", [P, NT])
        rs_h = sbuf(ctx, "rs_h", [P, NT])
        rs_t = sbuf(ctx, "rs_t", [P, NT])
        rs_r = sbuf(ctx, "rs_r", [P, NT])

        vec = sbuf(ctx, "vec", [P, V_END])
        ident_bf = sbuf(ctx, "ident_bf", [P, P], BF16)

        scope = ExitStack()
        nat = [sbuf(scope, f"nat{i}", [P, 2, JT, D]) for i in range(2)]
        ctxT = [sbuf(scope, f"ctxT{i}", [P, HC, SK]) for i in range(2)]
        prob = sbuf(scope, "prob", [P, SK])
        probT = sbuf(scope, "probT", [P, JT, P])
        qn = sbuf(scope, "qn", [P, D])
        qT = sbuf(scope, "qT", [P, HC, P])
        mx = sbuf(scope, "mx", [P, 4])
        nmax = sbuf(scope, "nmax", [P, 1])
        sums = sbuf(scope, "sums", [P, 4])
        total = sbuf(scope, "total", [P, 1])
        rinv = sbuf(scope, "rinv", [P, 1])
        scope.close()

        scope = ExitStack()
        wq_sb = sbuf(scope, "wq_sb", [P, HC, NH * F])
        wv_sb = sbuf(scope, "wv_sb", [P, HC, NH * F])
        oT = sbuf(scope, "oT", [P, NH, TOK])
        wr_sb = oT[:, 0:HC, :]
        wout_sb = wq_sb[:].rearrange("p a b -> p (a b)").rearrange("p (n d) -> p n d", n=NH)
        hT = sbuf(scope, "hT", [P, HC, TOK])
        kT = sbuf(scope, "kT", [P, NH, TOK])
        rpad = [sbuf(scope, f"rpad{i}", [P, NH, 2 * SEQ]) for i in range(2)]
        kv_n = [sbuf(scope, f"kv_n{i}", [P, TOK]) for i in range(2)]
        pos_b = sbuf(scope, "pos_b", [BATCH, SEQ, NH, SEQ])
        pos_g = sbuf(scope, "pos_g", [P, NG, NH, SEQ])
        hn = [sbuf(scope, f"hn{i}", [P, D]) for i in range(2)]
        hT_g = [sbuf(scope, f"hT_g{i}", [P, HC, SEQ, GB]) for i in range(2)]
        ku_g = [sbuf(scope, f"ku_g{i}", [P, NH, SEQ, GB]) for i in range(2)]
        v_g = [sbuf(scope, f"v_g{i}", [P, NH * F]) for i in range(2)]
        att = [sbuf(scope, f"att{i}", [P, NH, P]) for i in range(2)]
        attT = sbuf(scope, "attT", [P, NH, P])
        a_max = [sbuf(scope, f"a_max{i}", [P, NH]) for i in range(2)]
        a_bias = [sbuf(scope, f"a_bias{i}", [P, NH]) for i in range(2)]
        a_sum = [sbuf(scope, f"a_sum{i}", [P, NH]) for i in range(2)]
        a_inv = [sbuf(scope, f"a_inv{i}", [P, NH]) for i in range(2)]
        bout_sb = sbuf(scope, "bout_sb", [P, D])
        block_bf = sbuf(scope, "block_bf", [P, 4, P], BF16)
        scope.close()
        scope = ExitStack()
        w_raw = [sbuf(scope, f"w_raw{i}", [P, HC, D]) for i in range(3)]
        w_hi = [sbuf(scope, f"w_hi{i}", [P, HC, D], F32R) for i in range(3)]
        w_lo = [sbuf(scope, f"w_lo{i}", [P, HC, D], F32R) for i in range(3)]
        xx = sbuf(scope, "xx", [P, NT, D])
        r_p = sbuf(scope, "r_p", [P, NT, NE])
        r_eq = sbuf(scope, "r_eq", [P, NT, NE])
        r_sel = [sbuf(scope, f"r_sel{i}", [P, NT, NE]) for i in range(2)]
        r_max = [sbuf(scope, f"r_max{i}", [P, NT]) for i in range(2)]
        r_key = sbuf(scope, "r_key", [P, NT])
        wts = sbuf(scope, "wts", [P, NT, NE])
        rbias_sb = sbuf(scope, "rbias_sb", [P, NR])
        wrout_sb = sbuf(scope, "wrout_sb", [P, HC, NR])
        own = ExitStack()
        wkvd_sb = sbuf(own, "wkvd_sb", [P, HC, LAT])
        wqd_sb = sbuf(own, "wqd_sb", [P, HC, LAT])
        wku_sb = sbuf(own, "wku_sb", [LAT, HEADS * RD])
        wvu_sb = sbuf(own, "wvu_sb", [LAT, D])
        wq_up = sbuf(own, "wq_up", [LAT, 2, HEADS * RD])
        wrk_sb = sbuf(own, "wrk_sb", [P, HC, HEADS * RD])
        wo_sb = sbuf(own, "wo_sb", [P, HC, D])
        xn = [sbuf(own, f"xn{i}", [P, D]) for i in range(2)]
        xnT = [sbuf(own, f"xnT{i}", [P, HC, P]) for i in range(2)]
        latT = [sbuf(own, f"latT{i}", [LAT, 2, P]) for i in range(2)]
        raw = sbuf(own, "raw", [P, 2 * HEADS, RD])
        turned = sbuf(own, "turned", [P, 2 * HEADS, RD])
        kq = [sbuf(own, f"kq{i}", [P, 2 * HEADS, HD]) for i in range(2)]
        v_t = [sbuf(own, f"v_t{i}", [P, D]) for i in range(2)]
        qT_h = [sbuf(own, f"qT_h{i}", [P, QUADS, P]) for i in range(2)]
        kT_h = [sbuf(own, f"kT_h{i}", [P, QUADS, 4, P]) for i in range(2)]
        sp_ = [sbuf(own, f"sp{i}", [P, HEADS, P]) for i in range(2)]
        spT = sbuf(own, "spT", [P, HEADS, P])
        yT = sbuf(own, "yT", [P, HC, P])
        s_max = [sbuf(own, f"s_max{i}", [P, HEADS]) for i in range(2)]
        s_bias = [sbuf(own, f"s_bias{i}", [P, HEADS]) for i in range(2)]
        s_sum = [sbuf(own, f"s_sum{i}", [P, HEADS]) for i in range(2)]
        s_inv = [sbuf(own, f"s_inv{i}", [P, HEADS]) for i in range(2)]
        rms_x = sbuf(own, "rms_x", [P, NT])
        causal_bf = sbuf(own, "causal_bf", [P, 4, P], BF16)
        own.close()
        own = ExitStack()
        xT_hi = sbuf(own, "xT_hi", [P, HC, TOK], F32R)
        xT_lo = sbuf(own, "xT_lo", [P, HC, TOK], F32R)
        xn2 = [sbuf(own, f"xn2{i}", [P, D]) for i in range(2)]
        xf = [sbuf(own, f"xf{i}", [P, HC, P]) for i in range(2)]
        hm_hi = sbuf(own, "hm_hi", [P, HC, TOK], F32R)
        hm_lo = sbuf(own, "hm_lo", [P, HC, TOK], F32R)
        act_g = [sbuf(own, f"act_g{i}", [P, HALF]) for i in range(2)]
        hm = [sbuf(own, f"hm{i}", [P, HALF]) for i in range(2)]
        rms_f = sbuf(own, "rms_f", [P, NT])
        own.close()
        scope.close()
        pos_dram = nc.dram_tensor("pos_dram", (BATCH, SEQ, NH * SEQ), F32).ap()
        kT_t = kT[:].rearrange("p n (i b) -> p n i b", b=BATCH)
        hT_t = hT[:].rearrange("p c (i b) -> p c i b", b=BATCH)
        oT_t = oT[:].rearrange("p n (i b) -> p n i b", b=BATCH)

        w_loaded = {n: sem(f"{n}_loaded") for n in ("wr", "wq", "wv", "wout", "bout")}
        consts_cast = sem("consts_cast")
        stats_done, hn_ready, hT_full, hT_act, hT_dve = sem("stats_done"), sem("hn_ready"), sem("hT_full"), sem("hT_act"), sem("hT_dve")
        rT_full, rpad_ready, kT_full, kT_act, kT_dve = sem("rT_full"), sem("rpad_ready"), sem("kT_full"), sem("kT_act"), sem("kT_dve")
        kv_ready, pos_full, pos_out, pos_stored, pos_loaded = sem("kv_ready"), sem("pos_full"), sem("pos_out"), sem("pos_stored"), sem("pos_loaded")
        hg_ready, ku_ready, v_full, v_out, con_full, con_out = (sem(n) for n in ("hg_ready", "ku_ready", "v_full", "v_out", "con_full", "con_out"))
        abias_ready, exp_ready, ainv_ready, att_ready = (sem(n) for n in ("abias_ready", "exp_ready", "ainv_ready", "att_ready"))
        attT_full, attT_act, attT_dve, o_full, o_act, o_dve = (sem(n) for n in ("attT_full", "attT_act", "attT_dve", "o_full", "o_act", "o_dve"))
        bout_added, y2_full, y2_ready = sem("bout_added"), sem("y2_full"), sem("y2_ready")

        mla_loaded, router_loaded, raw_loaded = sem("mla_loaded"), sem("router_loaded"), [sem(f"raw_loaded{i}") for i in range(3)]
        causal_ready, kT_zero, xn_ready, xnT_full, xnT_ready = (sem(n) for n in ("causal_ready", "kT_zero", "xn_ready", "xnT_full", "xnT_ready"))
        lat_full, lat_ready, k_full, vv_full, q_full = (sem(n) for n in ("lat_full", "lat_ready", "k_full", "vv_full", "q_full"))
        raw_ready, vv_ready, kq_ready, qTh_full, kTh_full = (sem(n) for n in ("raw_ready", "vv_ready", "kq_ready", "qTh_full", "kTh_full"))
        qTh_ready, kTh_ready, self_full, sbias_ready, sexp_ready = (sem(n) for n in ("qTh_ready", "kTh_ready", "self_full", "sbias_ready", "sexp_ready"))
        sinv_ready, sp_ready, spT_full, spT_act, spT_dve = (sem(n) for n in ("sinv_ready", "sp_ready", "spT_full", "spT_act", "spT_dve"))
        yT_full, yT_ready, wo_full, xx_ready, y_summed = (sem(n) for n in ("yT_full", "yT_ready", "wo_full", "xx_ready", "y_summed"))
        xn2_ready, xfT_full, xf_ready, logit_full, logit_ready, gate_ready = (sem(n) for n in ("xn2_ready", "xfT_full", "xf_ready", "logit_full", "logit_ready", "gate_ready"))
        xhi_ready, xlo_ready, wts_ready = sem("xhi_ready"), sem("xlo_ready"), sem("wts_ready")
        whi_ready, wlo_ready = [sem(f"whi_ready{i}") for i in range(3)], [sem(f"wlo_ready{i}") for i in range(3)]
        gu_full, silu_ready, hm_ready, hhi_ready, hlo_ready = (sem(n) for n in ("gu_full", "silu_ready", "hm_ready", "hhi_ready", "hlo_ready"))
        down_free, down_full = sem("down_free"), sem("down_full")

        PIECES = [(0, JM // 2), (JM // 2, JM), (JM, JT)]
        x_loaded, cst_loaded, stored = sem("x_loaded"), sem("cst_loaded"), sem("stored")
        keys_loaded = [[[sem(f"keys_loaded{i}{b}{p}") for p in range(3)] for b in range(2)] for i in range(2)]
        ring_full, evac_act, evac_dve = sem("ring_full"), sem("evac_act"), sem("evac_dve")
        qn_ready, qT_full, qT_ready = sem("qn_ready"), sem("qT_full"), sem("qT_ready")
        scores_full, nmax_ready, prob_ready = sem("scores_full"), sem("nmax_ready"), sem("prob_ready")
        context_full, y1_ready = sem("context_full"), sem("y1_ready")
        dve_step = sem("dve_step")

        def evacs(block, g):
            return BLOCK // 2 * block + g // 2 - 1

        def row(t, k):
            return t[:, ds(k, 1), :].rearrange("p a d -> p (a d)")

        block = ctx.enter_context(nc.Block())

        @block.sync
        def _(sp):
            def load_keys(k, par):
                for b in range(2):
                    keys = ctx_keys[ds(2 * k + b, 1)]
                    main = keys[:, 0:JM * P, :].rearrange("a (p j) d -> p (a j) d", j=JM)
                    for p, (j0, j1) in enumerate(PIECES[:2]):
                        sp.dma_start(nat[par][:, b, j0:j1, :], main[:, j0:j1, :]).then_inc(keys_loaded[par][b][p], 16)
                    tail = keys[:, JM * P:SK, :].rearrange("a p d -> p (a d)")
                    sp.dma_start(nat[par][0:TAIL, b, JM, :], tail).then_inc(keys_loaded[par][b][2], 16)

            sp.dma_start(y[:], x.rearrange("(k p) d -> p k d", p=P)).then_inc(x_loaded, 16)
            sp.dma_start(cst[:], consts).then_inc(cst_loaded, 16)
            sp.dma_start(vec[:], vecs).then_inc(cst_loaded, 16)
            load_keys(0, 0)
            load_keys(1, 1)
            with sp.Fori(0, NT // 2 - 1) as i:
                for par in range(2):
                    sp.wait_ge(context_full, 2 * i + par + 1)
                    load_keys(2 * i + par + 2, par)
            sp.wait_ge(context_full, NT - 1)
            sp.dma_start(wr_sb, Wr.rearrange("(c p) n -> p c n", p=P)).then_inc(w_loaded["wr"], 16)
            sp.dma_start(wq_sb[:], Wq.rearrange("(c p) n -> p c n", p=P)).then_inc(w_loaded["wq"], 16)
            sp.dma_start(wv_sb[:], Wv.rearrange("(c p) n -> p c n", p=P)).then_inc(w_loaded["wv"], 16)
            sp.wait_ge(y1_ready, NT)
            sp.dma_start(bout_sb[:], rows[0, 0:D].partition_broadcast(P)).then_inc(w_loaded["bout"], 16)
            sp.wait_ge(kT_full, 2 * NH)
            sp.dma_start(wout_sb, Wout.rearrange("(n p) d -> p n d", p=P)).then_inc(w_loaded["wout"], 16)
            sp.wait_ge(pos_out, NH)
            sp.dma_start(pos_dram, pos_b[:].rearrange("b i n j -> b i (n j)")).then_inc(pos_stored, 16)
            sp.wait_ge(pos_stored, 16)
            for i in range(SEQ):
                sp.dma_start(pos_g[GB * i:GB * i + GB, :, :, :].rearrange("b g n j -> b g (n j)"),
                             pos_dram[:, i, :].rearrange("(g b) f -> b g f", b=GB)).then_inc(pos_loaded, 16)
            sp.wait_ge(y2_ready, NT)
            for dst, src in ((wkvd_sb[:], Wkvd.rearrange("(c p) n -> p c n", p=P)), (wqd_sb[:], Wqd.rearrange("(c p) n -> p c n", p=P)),
                             (wrk_sb[:], Wropek.rearrange("(c p) n -> p c n", p=P)), (wku_sb[:], Wku), (wvu_sb[:], Wvu),
                             (wq_up[:, 0, :], Wqu), (wq_up[:, 1, :], Wropeq), (wo_sb[:], Wo.rearrange("(c p) n -> p c n", p=P))):
                sp.dma_start(dst, src).then_inc(mla_loaded, 16)
            sp.dma_start(wrout_sb[:], Wrouter.rearrange("(c p) n -> p c n", p=P)).then_inc(router_loaded, 16)
            sp.dma_start(rbias_sb[:], rows[0, D:D + NR].partition_broadcast(P)).then_inc(router_loaded, 16)

            def load_expert(e):
                for m in range(3):
                    src = Wexp[m, ds(e, 1)].rearrange("a (c p) n -> p (a c) n", p=P)
                    sp.dma_start(w_raw[m][:], src).then_inc(raw_loaded[m], 16)

            load_expert(0)
            with sp.Fori(0, NE - 1) as e:
                for m in range(3):
                    sp.wait_ge(whi_ready[m], e + 1)
                    sp.wait_ge(wlo_ready[m], e + 1)
                    sp.dma_start(w_raw[m][:], Wexp[m, ds(e + 1, 1)].rearrange("a (c p) n -> p (a c) n", p=P)).then_inc(
                        raw_loaded[m], 16)
            sp.wait_ge(down_free, NE * NT + 4)
            sp.dma_start(out.rearrange("(k p) d -> p k d", p=P), y[:]).then_inc(stored, 16)
            sp.wait_ge(stored, 16)

        @block.tensor
        def _(pe):
            def ring_free(blk, g):
                v = evacs(blk, g - RING)
                if not (isinstance(v, int) and v <= 0):
                    pe.wait_ge(evac_act if (g - RING) % 2 == 0 else evac_dve, v)

            def key_transposes(k, par, blk, g0):
                turn = 16 * (k // 2 + 1) if isinstance(k, int) else k
                for b in range(2):
                    for j in range(JT):
                        for p, (j0, _) in enumerate(PIECES):
                            if j == j0:
                                pe.wait_ge(keys_loaded[par][b][p], turn)
                        g = g0 + b * JT + j
                        n = P if j < JM else TAIL
                        ring_free(blk, g)
                        for c in range(HC):
                            last = nc.tensor.transpose(bank[4 + g % RING][:, c * P:c * P + n],
                                                       nat[par][0:n, b, j, c * P:(c + 1) * P], ident[0:n, 0:n])
                        last.then_inc(ring_full, 1)

            def query_transposes(k):
                pe.wait_ge(qn_ready, k + 1)
                for c in range(HC):
                    last = nc.tensor.transpose(bank[7][:, c * P:(c + 1) * P], qn[:, c * P:(c + 1) * P], ident)
                last.then_inc(qT_full, 1)

            def scores(k, blk, g_last):
                pe.wait_ge(qT_ready, k + 1)
                for g in (g_last - 1, g_last):
                    pe.wait_ge(evac_act if g % 2 == 0 else evac_dve, evacs(blk, g))
                if not (isinstance(k, int) and k == 0):
                    pe.wait_ge(prob_ready, 4 * k)
                for n, (s0, w) in enumerate(S_CHUNKS):
                    for c in range(HC):
                        for b in range(2):
                            last = nc.tensor.matmul(bank[n][64 * b:64 * b + 64, 0:w], qT[:, c, 64 * b:64 * b + 64],
                                                    ctxT[b][:, c, s0:s0 + w], start=c == 0, stop=c == HC - 1,
                                                    skip_group_check=True)
                    last.then_inc(scores_full, 1)

            def prob_transposes(k, blk, g0):
                pe.wait_ge(prob_ready, 4 * k + 4)
                for f in range(P_FILLS):
                    g = g0 + f
                    ring_free(blk, g)
                    for j in range(4 * f, min(4 * f + 4, JT)):
                        n = P if j < JM else TAIL
                        last = nc.tensor.transpose(bank[4 + g % RING][0:n, (j % 4) * P:(j % 4 + 1) * P],
                                                   prob[:, j * P:j * P + n], ident)
                    last.then_inc(ring_full, 1)

            def context(k, par, blk, g_last):
                for g in (g_last - 1, g_last):
                    pe.wait_ge(evac_act if g % 2 == 0 else evac_dve, evacs(blk, g))
                for j in range(JT):
                    n = P if j < JM else TAIL
                    for b in range(2):
                        last = nc.tensor.matmul(bank[7][64 * b:64 * b + 64, :], probT[0:n, j, 64 * b:64 * b + 64],
                                                nat[par][0:n, b, j, :], start=j == 0, stop=j == JT - 1,
                                                skip_group_check=True)
                last.then_inc(context_full, 1)

            def step(k, par, turn):
                if not (isinstance(k, int) and k == 0):
                    pe.wait_ge(y1_ready, k)
                query_transposes(k + 1)
                key_transposes(turn, 1 - par, k + 1, 0)
                prob_transposes(k, k + 1, T_FILLS)
                pe.wait_ge(qT_ready, k + 2)
                context(k, par, k + 1, BLOCK - 1)
                scores(k + 1, k + 1, T_FILLS - 1)

            pe.wait_ge(cst_loaded, 32)
            query_transposes(0)
            key_transposes(0, 0, 0, BLOCK - T_FILLS)
            scores(0, 0, BLOCK - 1)
            step(0, 0, 1)
            with pe.Fori(0, NT // 2 - 1) as i:
                step(2 * i + 1, 1, 16 * i + 32)
                step(2 * i + 2, 0, 16 * i + 32)
            prob_transposes(NT - 1, NT, 0)
            context(NT - 1, 1, NT, P_FILLS - 1)

            pe.wait_ge(w_loaded["wr"], 16)
            pe.wait_ge(prob_ready, 4 * NT)
            for n in range(NH):
                for c in range(HC):
                    last = nc.tensor.matmul(bank[0][:, n * SEQ:(n + 1) * SEQ], wr_sb[:, c, n * F:(n + 1) * F],
                                            cst[:, C_PE + c * SEQ:C_PE + (c + 1) * SEQ], start=c == 0, stop=c == HC - 1)
            last.then_inc(rT_full, 1)
            for k in range(NT):
                pe.wait_ge(hn_ready, k + 1)
                if k == 0:
                    pe.wait_ge(rpad_ready, 1)
                for c in range(HC):
                    last = nc.tensor.transpose(bank[k][:, c * P:(c + 1) * P], hn[k % 2][:, c * P:(c + 1) * P], ident)
                last.then_inc(hT_full, 1)
            pe.wait_ge(w_loaded["wq"], 16)
            pe.wait_ge(hT_act, NT // 2)
            pe.wait_ge(hT_dve, NT // 2)
            for n in range(NH):
                for half in range(2):
                    m = 2 * n + half
                    if m >= 4:
                        pe.wait_ge(kT_act if half == 0 else kT_dve, (m - 4) // 2 + 1)
                    for c in range(HC):
                        last = nc.tensor.matmul(bank[m % 4][:], wq_sb[:, c, n * F:(n + 1) * F],
                                                hT[:, c, half * 512:half * 512 + 512], start=c == 0, stop=c == HC - 1)
                    last.then_inc(kT_full, 1)

            def positions(n, par):
                pe.wait_ge(kv_ready, n + 1)
                for i in range(SEQ):
                    o = bank[4 + par][0:BATCH, i * SEQ:(i + 1) * SEQ]
                    at = SEQ - 1 - i
                    last = nc.tensor.matmul(o, kv_n[par][:, i * BATCH:(i + 1) * BATCH],
                                            rpad[0][:, ds(n, 1), at:at + SEQ].rearrange("p a j -> p (a j)"),
                                            start=True, stop=i == SEQ - 1)
                    if i < SEQ - 1:
                        last = nc.tensor.matmul(o, kv_n[par][:, (i + 1) * BATCH:(i + 2) * BATCH],
                                                rpad[1][:, ds(n, 1), at:at + SEQ].rearrange("p a j -> p (a j)"),
                                                start=False, stop=True)
                last.then_inc(pos_full, 1)

            positions(0, 0)
            positions(1, 1)
            with pe.Fori(0, NH // 2 - 1) as i:
                for par in range(2):
                    pe.wait_ge(pos_out, 2 * i + par + 1)
                    positions(2 * i + par + 2, par)

            def group_scores(g, par):
                pe.wait_ge(hg_ready, g + 1)
                if not (isinstance(g, int) and g == 0):
                    pe.wait_ge(v_out, 2 * g)
                for h in range(2):
                    for c in range(HC):
                        last = nc.tensor.matmul(bank[h][:], hT_g[par][:, c, :, :].rearrange("p i b -> p (i b)"),
                                                wv_sb[:, c, h * 512:(h + 1) * 512], start=c == 0, stop=c == HC - 1)
                    last.then_inc(v_full, 1)
                pe.wait_ge(ku_ready, g + 1)
                if not (isinstance(g, int) and g == 0):
                    pe.wait_ge(con_out, 2 * g)
                for h in range(2):
                    nc.tensor.matmul(bank[2 + h][:], ident_bf[:], block_bf[:].rearrange("p n q -> p (n q)"),
                                     start=True, stop=True)
                    for n in range(4 * h, 4 * h + 4):
                        last = nc.tensor.matmul(bank[2 + h][:, (n % 4) * P:(n % 4 + 1) * P],
                                                ku_g[par][:, n, :, :].rearrange("p i b -> p (i b)"),
                                                kT_t[:, n, :, ds(GB * g, GB)], start=False, stop=True,
                                                skip_group_check=True)
                    last.then_inc(con_full, 1)

            def group_output(g, par):
                pe.wait_ge(att_ready, g + 1)
                for n in range(NH):
                    last = nc.tensor.transpose(bank[4 + n // 4][:, (n % 4) * P:(n % 4 + 1) * P], att[par][:, n, :], ident)
                    if n % 4 == 3:
                        last.then_inc(attT_full, 1)
                pe.wait_ge(v_out, 2 * g + 2)
                pe.wait_ge(attT_act, g + 1)
                pe.wait_ge(attT_dve, g + 1)
                for n in range(NH):
                    last = nc.tensor.matmul(bank[6 + n // 4][:, (n % 4) * P:(n % 4 + 1) * P],
                                            v_g[par][:, n * F:(n + 1) * F], attT[:, n, :], start=True, stop=True)
                    if n % 4 == 3:
                        last.then_inc(o_full, 1)

            def output_free(g):
                pe.wait_ge(o_act, g + 1)
                pe.wait_ge(o_dve, g + 1)

            pe.wait_ge(kT_act, NH)
            pe.wait_ge(kT_dve, NH)
            pe.wait_ge(w_loaded["wv"], 16)
            pe.wait_ge(consts_cast, 2)
            group_scores(0, 0)
            group_scores(1, 1)
            pe.wait_ge(pos_out, NH)
            with pe.Fori(0, NG // 2 - 1) as i:
                for par in range(2):
                    group_output(2 * i + par, par)
                    group_scores(2 * i + par + 2, par)
                    output_free(2 * i + par)
            group_output(NG - 2, 0)
            output_free(NG - 2)
            group_output(NG - 1, 1)
            output_free(NG - 1)
            pe.wait_ge(w_loaded["wout"], 16)
            for k in range(NT):
                for n in range(NH):
                    last = nc.tensor.matmul(bank[k][:], oT[:, n, k * P:(k + 1) * P], wout_sb[:, n, :], start=n == 0,
                                            stop=n == NH - 1)
                last.then_inc(y2_full, 1)

            def project(k, par):
                pe.wait_ge(xn_ready, k + 1)
                for c in range(HC):
                    last = nc.tensor.transpose(bank[0][:, c * P:(c + 1) * P], xn[par][:, c * P:(c + 1) * P], ident)
                last.then_inc(xnT_full, 1)
                pe.wait_ge(xnT_ready, k + 1)
                for i, w in enumerate((wkvd_sb, wqd_sb)):
                    for c in range(HC):
                        last = nc.tensor.matmul(bank[1][:, i * P:(i + 1) * P], w[:, c, :], xnT[par][:, c, :], start=c == 0,
                                                stop=c == HC - 1)
                last.then_inc(lat_full, 1)
                for c in range(HC):
                    nc.tensor.matmul(bank[2][:, 0:256], xnT[par][:, c, :], wrk_sb[:, c, :], start=c == 0, stop=c == HC - 1)
                pe.wait_ge(lat_ready, k + 1)
                nc.tensor.matmul(bank[2][:, 256:512], latT[par][:, 0, :], wku_sb[:], start=True, stop=True).then_inc(k_full, 1)
                nc.tensor.matmul(bank[0][:], latT[par][:, 1, :], wq_up[:].rearrange("l a n -> l (a n)"), start=True,
                                 stop=True).then_inc(q_full, 1)
                if not (isinstance(k, int) and k == 0):
                    pe.wait_ge(vv_ready, k)
                nc.tensor.matmul(bank[3][:], latT[par][:, 0, :], wvu_sb[:], start=True, stop=True).then_inc(vv_full, 1)

            def head_transposes(k, par):
                pe.wait_ge(kq_ready, k + 1)
                for first, b, full in ((HEADS, 0, qTh_full), (0, 1, kTh_full)):
                    for c in range(QUADS):
                        last = nc.tensor.transpose(
                            bank[b][:, c * P:(c + 1) * P],
                            kq[par][:, first + 4 * c:first + 4 * c + 4, :].rearrange("p h d -> p (h d)"), ident)
                    last.then_inc(full, 1)

            def self_scores(k, par):
                pe.wait_ge(qTh_ready, k + 1)
                pe.wait_ge(kTh_ready, k + 1)
                for c in range(QUADS):
                    if c == 3 and not (isinstance(k, int) and k == 0):
                        pe.wait_ge(xx_ready, k)
                    nc.tensor.matmul(bank[4 + c][:], ident_bf[:], causal_bf[:].rearrange("p n q -> p (n q)"), start=True,
                                     stop=False)
                    nc.tensor.matmul(bank[4 + c][:], qT_h[par][:, c, :], kT_h[par][:, c, :, :].rearrange("p n q -> p (n q)"),
                                     start=False, stop=True).then_inc(self_full, 1)

            def weight_transposes(k, par):
                for c in range(QUADS):
                    pe.wait_ge(sp_ready, 4 * k + c + 1)
                    for n in range(4):
                        last = nc.tensor.transpose(bank[4 + c][:, n * P:(n + 1) * P], sp_[par][:, 4 * c + n, :], ident)
                    last.then_inc(spT_full, 1)

            def self_output(k, par):
                pe.wait_ge(spT_act, 2 * k + 2)
                pe.wait_ge(spT_dve, 2 * k + 2)
                pe.wait_ge(vv_ready, k + 1)
                for h in range(HEADS):
                    last = nc.tensor.matmul(bank[4][HD * (h % 4):HD * (h % 4 + 1), h // 4 * P:(h // 4 + 1) * P],
                                            v_t[par][:, HD * h:HD * (h + 1)], spT[:, h, :], start=True, stop=True,
                                            skip_group_check=True)
                last.then_inc(yT_full, 1)
                pe.wait_ge(yT_ready, k + 1)
                for c in range(HC):
                    last = nc.tensor.matmul(bank[7][:], yT[:, c, :], wo_sb[:, c, :], start=c == 0, stop=c == HC - 1)
                last.then_inc(wo_full, 1)

            def self_step(k, par):
                project(k + 1, 1 - par)
                weight_transposes(k, par)
                head_transposes(k + 1, 1 - par)
                self_output(k, par)
                self_scores(k + 1, 1 - par)

            pe.wait_ge(mla_loaded, 16 * 8)
            pe.wait_ge(causal_ready, 1)
            project(0, 0)
            head_transposes(0, 0)
            self_scores(0, 0)
            self_step(0, 0)
            with pe.Fori(0, NT // 2 - 1) as i:
                self_step(2 * i + 1, 1)
                self_step(2 * i + 2, 0)
            weight_transposes(NT - 1, 1)
            self_output(NT - 1, 1)

            pe.wait_ge(router_loaded, 32)
            for k in range(NT):
                pe.wait_ge(xn2_ready, k + 1)
                for c in range(HC):
                    last = nc.tensor.transpose(bank[k % 2][:, c * P:(c + 1) * P], xn2[k % 2][:, c * P:(c + 1) * P], ident)
                last.then_inc(xfT_full, 1)
                pe.wait_ge(xf_ready, k + 1)
                for c in range(HC):
                    last = nc.tensor.matmul(bank[2][:, NE * k:NE * k + NR], xf[k % 2][:, c, :], wrout_sb[:, c, :],
                                            start=c == 0, stop=c == HC - 1)
                last.then_inc(logit_full, 1)
            pe.wait_ge(xhi_ready, NT)
            pe.wait_ge(xlo_ready, NT)
            gate, up, down = range(3)
            with pe.Fori(0, NE) as e:
                for m in (gate, up):
                    pe.wait_ge(whi_ready[m], e + 1)
                    pe.wait_ge(wlo_ready[m], e + 1)
                for j in range(NJ):
                    half, ic = divmod(j, HC)
                    pe.wait_ge(hm_ready, NJ * e + j + 1)
                    for m, b in ((gate, j % 2), (up, 2 + j % 2)):
                        for c in range(HC):
                            lo, hi = (w[m][:, c, ic * P:(ic + 1) * P] for w in (w_lo, w_hi))
                            xl, xh = (t[:, c, half * HALF:(half + 1) * HALF] for t in (xT_lo, xT_hi))
                            nc.tensor.matmul(bank[b][:], lo, xh, start=c == 0, stop=False)
                            nc.tensor.matmul(bank[b][:], hi, xl, start=False, stop=False)
                            last = nc.tensor.matmul(bank[b][:], hi, xh, start=False, stop=c == HC - 1)
                    last.then_inc(gu_full, 1)
                pe.wait_ge(whi_ready[down], e + 1)
                pe.wait_ge(wlo_ready[down], e + 1)
                for k in range(NT):
                    if k % 4 == 0:
                        pe.wait_ge(hhi_ready, NJ * e + HC * (k // 4 + 1))
                        pe.wait_ge(hlo_ready, NJ * e + HC * (k // 4 + 1))
                    pe.wait_ge(down_free, NT * e + k + 1)
                    for c in range(HC):
                        hl, hh = (t[:, c, k * P:(k + 1) * P] for t in (hm_lo, hm_hi))
                        nc.tensor.matmul(bank[4 + k % 4][:], hl, w_hi[down][:, c, :], start=c == 0, stop=False)
                        nc.tensor.matmul(bank[4 + k % 4][:], hh, w_lo[down][:, c, :], start=False, stop=False)
                        last = nc.tensor.matmul(bank[4 + k % 4][:], hh, w_hi[down][:, c, :], start=False, stop=c == HC - 1)
                    last.then_inc(down_full, 1)

        @block.gpsimd
        def _(pool):
            def columns(g, par):
                nc.gpsimd.tensor_copy(hT_g[par][:], hT_t[:, :, :, ds(GB * g, GB)]).then_inc(hg_ready, 1)

            def normalise(g, par):
                pool.wait_ge(ainv_ready, g + 1)
                nc.gpsimd.tensor_tensor(att[par][:], att[par][:], a_inv[par][:].unsqueeze(2).broadcast_to([P, NH, P]),
                                        ALU.mult).then_inc(att_ready, 1)

            pool.wait_ge(hT_act, NT // 2)
            pool.wait_ge(hT_dve, NT // 2)
            columns(0, 0)
            columns(1, 1)
            pool.wait_ge(w_loaded["bout"], 16)
            nc.gpsimd.tensor_tensor(y[:], y[:], bout_sb[:].unsqueeze(1).broadcast_to([P, NT, D]),
                                    ALU.add).then_inc(bout_added, 1)
            normalise(0, 0)
            with pool.Fori(0, NG // 2 - 1) as i:
                for par in range(2):
                    pool.wait_ge(v_full, 2 * (2 * i + par) + 2)
                    columns(2 * i + par + 2, par)
                    normalise(2 * i + par + 1, 1 - par)
            normalise(NG - 1, 1)

            pool.wait_ge(y2_ready, NT)
            for t in kT_h:
                nc.gpsimd.memset(t[:], 0.0).then_inc(kT_zero, 1)

            def self_normalise(k, par):
                for c in range(QUADS):
                    pool.wait_ge(sinv_ready, 4 * k + c + 1)
                    nc.gpsimd.tensor_tensor(sp_[par][:, 4 * c:4 * c + 4, :], sp_[par][:, 4 * c:4 * c + 4, :],
                                            s_inv[par][:, 4 * c:4 * c + 4].unsqueeze(2).broadcast_to([P, 4, P]),
                                            ALU.mult).then_inc(sp_ready, 1)

            def add_up(k):
                pool.wait_ge(xx_ready, k + 1)
                nc.gpsimd.tensor_tensor(row(y, k), row(y, k), row(xx, k), ALU.add).then_inc(y_summed, 1)

            self_normalise(0, 0)
            with pool.Fori(0, NT // 2 - 1) as i:
                for par in range(2):
                    self_normalise(2 * i + 1 + par, 1 - par)
                    add_up(2 * i + par)
            self_normalise(NT - 1, 1)
            add_up(NT - 2)
            add_up(NT - 1)

            gate, up, down = range(3)

            def low_part(m, turn):
                pool.wait_ge(whi_ready[m], turn)
                nc.gpsimd.tensor_tensor(w_lo[m][:], w_raw[m][:], w_hi[m].bitcast(F32)[:], ALU.subtract).then_inc(wlo_ready[m], 1)

            def hidden_low(e):
                for j in range(NJ):
                    half, ic = divmod(j, HC)
                    at = slice(half * HALF, (half + 1) * HALF)
                    pool.wait_ge(hhi_ready, NJ * e + j + 1)
                    nc.gpsimd.tensor_tensor(hm_lo[:, ic, at], hm[j % 2][:], hm_hi.bitcast(F32)[:, ic, at],
                                            ALU.subtract).then_inc(hlo_ready, 1)

            for m in (gate, up, down):
                low_part(m, 1)
            with pool.Fori(0, NE - 1) as e:
                hidden_low(e)
                low_part(gate, e + 2)
                low_part(up, e + 2)
                low_part(down, e + 2)
            hidden_low(NE - 1)

        def ring_out(copy, blk, g, g_keys, sem_done):
            if g >= g_keys and g < g_keys + T_FILLS:
                b, j = divmod(g - g_keys, JT)
                n = P if j < JM else TAIL
                src = bank[4 + g % RING][:].rearrange("p (c s) -> p c s", c=HC)[:, :, 0:n]
                copy(ctxT[b][:, :, j * P:j * P + n], src).then_inc(sem_done, 1)

        def prob_out(copy, g, f, sem_done):
            j0, j1 = 4 * f, min(4 * f + 4, JT)
            n = P if j1 <= JM else TAIL
            src = bank[4 + g % RING][0:n, 0:(j1 - j0) * P]
            copy(probT[0:n, j0:j1, :].rearrange("p j q -> p (j q)"), src).then_inc(sem_done, 1)

        @block.scalar
        def _(act):
            def keys_out(blk, g, g_keys):
                act.wait_ge(ring_full, BLOCK * blk + g - 3)
                ring_out(nc.scalar.copy, blk, g, g_keys, evac_act)

            def exps(n):
                s0, w = S_CHUNKS[n]
                nc.scalar.activation(prob[:, s0:s0 + w], bank[n][:, 0:w], ACT.Exp, bias=nmax[:, 0:1],
                                     accum_out=sums[:, n:n + 1]).then_inc(prob_ready, 1)

            def probs_out(blk, g0):
                for f in range(P_FILLS):
                    if (g0 + f) % 2 == 0:
                        act.wait_ge(ring_full, BLOCK * blk + g0 + f - 3)
                        prob_out(nc.scalar.copy, g0 + f, f, evac_act)

            def step(k):
                mine = list(range(0, T_FILLS, 2))
                keys_out(k + 1, mine[0], 0)
                act.wait_ge(nmax_ready, k + 1)
                for n in range(4):
                    exps(n)
                    keys_out(k + 1, mine[n + 1], 0)
                for g in mine[5:]:
                    keys_out(k + 1, g, 0)
                probs_out(k + 1, T_FILLS)

            for g in range(BLOCK - T_FILLS, BLOCK, 2):
                keys_out(0, g, BLOCK - T_FILLS)
            step(0)
            with act.Fori(0, NT // 2 - 1) as i:
                step(2 * i + 1)
                step(2 * i + 2)
            act.wait_ge(nmax_ready, NT)
            for n in range(4):
                exps(n)
            probs_out(NT, 0)

            act.wait_ge(cst_loaded, 32)
            for k in range(0, NT, 2):
                act.wait_ge(hT_full, k + 1)
                for c in range(HC):
                    last = nc.scalar.activation(hT[:, c, k * P:(k + 1) * P], bank[k][:, c * P:(c + 1) * P], ACT.Identity,
                                                bias=vec[:, V_BETA + c:V_BETA + c + 1],
                                                scale=vec[:, V_GAMMA + c:V_GAMMA + c + 1])
                last.then_inc(hT_act, 1)
            for n in range(NH):
                act.wait_ge(kT_full, 2 * n + 1)
                nc.scalar.copy(kT[:, n, 0:512], bank[2 * n % 4][:]).then_inc(kT_act, 1)

            def positions_out(n, par):
                act.wait_ge(pos_full, n + 1)
                nc.scalar.activation(pos_b[:, :, ds(n, 1), :].rearrange("b i a j -> b i (a j)"),
                                     bank[4 + par][0:BATCH, 0:SEQ * SEQ].rearrange("b (i j) -> b i j", j=SEQ), ACT.Copy,
                                     scale=cst[0:BATCH, ds(C_TRIL + n, 1)]).then_inc(pos_out, 1)

            with act.Fori(0, NH // 2) as i:
                positions_out(2 * i, 0)
                positions_out(2 * i + 1, 1)

            def values_out(g, par):
                for h in range(2):
                    act.wait_ge(v_full, 2 * g + h + 1)
                    nc.scalar.copy(v_g[par][:, h * 512:(h + 1) * 512], bank[h][:]).then_inc(v_out, 1)

            def group_exps(g, par):
                act.wait_ge(abias_ready, g + 1)
                for n in range(NH):
                    last = nc.scalar.activation(att[par][:, n, :], att[par][:, n, :], ACT.Exp, bias=a_bias[par][:, n:n + 1],
                                                scale=ATT_SCALE, accum_out=a_sum[par][:, n:n + 1])
                last.then_inc(exp_ready, 1)

            def group_out(g):
                act.wait_ge(attT_full, 2 * g + 1)
                nc.scalar.copy(attT[:, 0:4, :].rearrange("p n q -> p (n q)"), bank[4][:]).then_inc(attT_act, 1)
                act.wait_ge(o_full, 2 * g + 1)
                nc.scalar.copy(oT_t[:, 0:4, :, ds(GB * g, GB)],
                               bank[6][:].rearrange("p (n i b) -> p n i b", n=4, i=SEQ)).then_inc(o_act, 1)

            for g in range(2):
                values_out(g, g)
                group_exps(g, g)
            with act.Fori(0, NG // 2 - 1) as i:
                for par in range(2):
                    group_out(2 * i + par)
                    values_out(2 * i + par + 2, par)
                    group_exps(2 * i + par + 2, par)
            group_out(NG - 2)
            group_out(NG - 1)

            def heads_out(k, par):
                act.wait_ge(k_full, k + 1)
                kr = bank[2][:].rearrange("p (a h d) -> p a h d", a=2, d=RD)
                if not (isinstance(k, int) and k == 0):
                    act.wait_ge(kq_ready, k)
                nc.scalar.copy(raw[:, 0:HEADS, :], kr[:, 0])
                nc.scalar.copy(kq[par][:, 0:HEADS, 0:RD], kr[:, 1])
                act.wait_ge(q_full, k + 1)
                qr = bank[0][:].rearrange("p (a h d) -> p a h d", a=2, d=RD)
                nc.scalar.copy(kq[par][:, HEADS:, 0:RD], qr[:, 0])
                nc.scalar.copy(raw[:, HEADS:, :], qr[:, 1]).then_inc(raw_ready, 1)
                act.wait_ge(vv_full, k + 1)
                nc.scalar.copy(v_t[par][:], bank[3][:]).then_inc(vv_ready, 1)

            def keys_spread(k, par):
                act.wait_ge(kTh_full, k + 1)
                for h in range(4):
                    rows_h = slice(HD * h, HD * (h + 1))
                    last = nc.scalar.copy(kT_h[par][rows_h, :, h, :], bank[1][rows_h, :].rearrange("p (c q) -> p c q", c=QUADS))
                last.then_inc(kTh_ready, 1)

            def self_exps(k, par):
                for c in range(QUADS):
                    act.wait_ge(sbias_ready, 4 * k + c + 1)
                    for n in range(4):
                        h = 4 * c + n
                        last = nc.scalar.activation(sp_[par][:, h, :], bank[4 + c][:, n * P:(n + 1) * P], ACT.Exp,
                                                    bias=s_bias[par][:, h:h + 1], scale=SELF_SCALE,
                                                    accum_out=s_sum[par][:, h:h + 1])
                    last.then_inc(sexp_ready, 1)

            def weights_out(k):
                for c in range(0, QUADS, 2):
                    act.wait_ge(spT_full, 4 * k + c + 1)
                    nc.scalar.copy(spT[:, 4 * c:4 * c + 4, :].rearrange("p n q -> p (n q)"), bank[4 + c][:]).then_inc(spT_act, 1)

            def self_step(k, par):
                self_exps(k, par)
                heads_out(k + 1, 1 - par)
                weights_out(k)
                keys_spread(k + 1, 1 - par)

            act.wait_ge(kT_zero, 2)
            heads_out(0, 0)
            keys_spread(0, 0)
            self_step(0, 0)
            with act.Fori(0, NT // 2 - 1) as i:
                self_step(2 * i + 1, 1)
                self_step(2 * i + 2, 0)
            self_exps(NT - 1, 1)
            weights_out(NT - 1)

            gate, up, down = range(3)

            def high_part(m, turn):
                act.wait_ge(raw_loaded[m], turn)
                nc.scalar.copy(w_hi[m][:], w_raw[m][:]).then_inc(whi_ready[m], 1)

            act.wait_ge(raw_loaded[gate], 16)
            for m in (gate, up, down):
                high_part(m, 16)
            for k in range(NT):
                act.wait_ge(xf_ready, k + 1)
                nc.scalar.copy(xT_hi[:, :, k * P:(k + 1) * P], xf[k % 2][:]).then_inc(xhi_ready, 1)
            act.wait_ge(logit_ready, 1)
            nc.scalar.activation(r_p[:, :, 0:NR], r_p[:, :, 0:NR], ACT.Exp, scale=-1.0).then_inc(gate_ready, 1)

            def silus(e):
                for j in range(NJ):
                    half, ic = divmod(j, HC)
                    act.wait_ge(gu_full, NJ * e + j + 1)
                    nc.scalar.activation(act_g[j % 2][:], bank[j % 2][:], ACT.Silu).then_inc(silu_ready, 1)
                    act.wait_ge(hm_ready, NJ * e + j + 1 + 2)
                    nc.scalar.copy(hm_hi[:, ic, half * HALF:(half + 1) * HALF], hm[j % 2][:]).then_inc(hhi_ready, 1)

            with act.Fori(0, NE - 1) as e:
                silus(e)
                for m in (gate, up):
                    act.wait_ge(gu_full, NJ * e + NJ)
                    high_part(m, 16 * e + 32)
                act.wait_ge(down_full, NT * e + NT)
                high_part(down, 16 * e + 32)
            silus(NE - 1)

        @block.vector
        def _(dve):
            chain = Steps(dve, dve_step)

            def row_stats(t):
                for k in range(NT):
                    chain.mark(dve.bn_stats(stats[:, k, :], t[:, k, :]))
                chain.wait()
                for k in range(NT):
                    chain.mark(dve.bn_aggr(mv[:, k, :], stats[:, k, :]))
                chain.wait()

            def rsqrt(dst, v):
                chain(dve.tensor_scalar(rs_h[:], v, -0.5, None, ALU.mult))
                chain(dve.tensor_scalar(rs_t.bitcast(I32)[:], v.bitcast(I32), 1, None, ALU.arith_shift_right))
                chain(dve.tensor_scalar(dst.bitcast(I32), rs_t.bitcast(I32)[:], -1.0, float(0x5F3759DF), ALU.mult, ALU.add))
                for _ in range(3):
                    chain(dve.tensor_tensor(rs_t[:], dst, dst, ALU.mult))
                    chain(dve.tensor_tensor(rs_t[:], rs_t[:], rs_h[:], ALU.mult))
                    chain(dve.scalar_tensor_tensor(dst, rs_t[:], 1.5, dst, ALU.add, ALU.mult))

            def double_norm():
                chain(dve.tensor_scalar(rs_v[:], var, LN_EPS, None, ALU.add))
                rsqrt(rstd[:], rs_v[:])
                chain(dve.tensor_tensor(rs_v[:], rstd[:], rstd[:], ALU.mult))
                chain(dve.tensor_tensor(rs_v[:], rs_v[:], var, ALU.mult))
                chain(dve.tensor_scalar(rs_v[:], rs_v[:], LN_EPS, None, ALU.add))
                rsqrt(rs_r[:], rs_v[:])
                chain(dve.tensor_tensor(rstd[:], rstd[:], rs_r[:], ALU.mult))

            def queries(k):
                dve.tensor_scalar(qn[:], row(y, k), mean[:, ds(k, 1)], rstd[:, ds(k, 1)], ALU.subtract,
                                  ALU.mult).then_inc(qn_ready, 1)

            def queries_out(k):
                dve.wait_ge(qT_full, k + 1)
                dve.tensor_copy(qT[:].rearrange("p c q -> p (c q)"), bank[7][:]).then_inc(qT_ready, 1)

            def maxima(k):
                for n, (s0, w) in enumerate(S_CHUNKS):
                    dve.wait_ge(scores_full, 4 * k + n + 1)
                    chain.mark(dve.tensor_reduce(mx[:, n:n + 1], bank[n][:, 0:w], AX, ALU.max))
                chain.wait()
                dve.tensor_reduce(nmax[:], mx[:], AX, ALU.max, negate=True).then_inc(nmax_ready, 1)

            def keys_out(blk, g, g_keys):
                dve.wait_ge(ring_full, BLOCK * blk + g - 3)
                ring_out(dve.tensor_copy, blk, g, g_keys, evac_dve)

            def finish(k, blk, g0):
                dve.wait_ge(prob_ready, 4 * k + 4)
                chain(dve.tensor_reduce(total[:], sums[:], AX, ALU.add))
                chain(dve.reciprocal(rinv[:], total[:]))
                for f in range(P_FILLS):
                    if (g0 + f) % 2 == 1:
                        dve.wait_ge(ring_full, BLOCK * blk + g0 + f - 3)
                        prob_out(dve.tensor_copy, g0 + f, f, evac_dve)
                dve.wait_ge(context_full, k + 1)
                dve.scalar_tensor_tensor(row(y, k), bank[7][:], rinv[:, 0:1], row(y, k), ALU.mult,
                                         ALU.add).then_inc(y1_ready, 1)

            def step(k):
                queries(k + 1)
                maxima(k)
                queries_out(k + 1)
                for g in range(1, T_FILLS, 2):
                    keys_out(k + 1, g, 0)
                finish(k, k + 1, T_FILLS)

            dve.wait_ge(x_loaded, 16)
            row_stats(y)
            chain(dve.tensor_scalar(rs_v[:], var, LN_EPS, None, ALU.add))
            rsqrt(rstd[:], rs_v[:])
            queries(0)
            queries_out(0)
            for g in range(BLOCK - T_FILLS + 1, BLOCK, 2):
                keys_out(0, g, BLOCK - T_FILLS)
            step(0)
            chain.enter()
            with dve.Fori(0, NT // 2 - 1) as i:
                chain.turn(i, 12)
                step(2 * i + 1)
                step(2 * i + 2)
            chain.leave(NT // 2 - 1)
            maxima(NT - 1)
            finish(NT - 1, NT, 0)

            dve.wait_ge(y1_ready, NT)
            row_stats(y)
            double_norm()
            dve.wait_ge(cst_loaded, 32)
            dve.tensor_copy(ident_bf[:], ident).then_inc(consts_cast, 1)
            dve.tensor_copy(block_bf[:], cst[:, C_BLOCK:C_BLOCK + P].unsqueeze(1).broadcast_to([P, 4, P])).then_inc(consts_cast, 1)
            for t in rpad:
                chain.mark(dve.memset(t[:], 0.0))
            chain.wait()
            dve.wait_ge(rT_full, 1)
            rT = bank[0][:, 0:NH * SEQ].rearrange("p (n j) -> p n j", j=SEQ)
            chain(dve.tensor_copy(rpad[0][:, :, 0:SEQ], rT))
            dve.tensor_copy(rpad[1][:, :, SEQ + 1:2 * SEQ], rT[:, :, 0:SEQ - 1]).then_inc(rpad_ready, 1)
            dve.wait_ge(rpad_ready, 1)
            for k in range(NT + 1):
                if k < NT:
                    if k >= 2:
                        dve.wait_ge(hT_full, k - 1)
                    dve.tensor_scalar(hn[k % 2][:], y[:, k, :], mean[:, k:k + 1], rstd[:, k:k + 1], ALU.subtract,
                                      ALU.mult).then_inc(hn_ready, 1)
                if k % 2 == 0 and k > 0:
                    dve.wait_ge(hT_full, k)
                    for c in range(HC):
                        last = dve.tensor_scalar(hT[:, c, (k - 1) * P:k * P], bank[k - 1][:, c * P:(c + 1) * P],
                                                 vec[:, V_GAMMA + c:V_GAMMA + c + 1], vec[:, V_BETA + c:V_BETA + c + 1],
                                                 ALU.mult, ALU.add)
                    last.then_inc(hT_dve, 1)
            for n in range(NH):
                dve.wait_ge(kT_full, 2 * n + 2)
                dve.tensor_copy(kT[:, n, 512:1024], bank[(2 * n + 1) % 4][:]).then_inc(kT_dve, 1)
            dve.wait_ge(kT_act, NH)
            dve.wait_ge(kT_dve, NH)

            def pos_queries(n, par):
                dve.tensor_scalar(kv_n[par][:], row(kT, n), vec[:, ds(V_V + n, 1)], None, ALU.add).then_inc(kv_ready, 1)

            pos_queries(0, 0)
            pos_queries(1, 1)
            with dve.Fori(0, NH // 2 - 1) as i:
                for par in range(2):
                    dve.wait_ge(pos_full, 2 * i + par + 1)
                    pos_queries(2 * i + par + 2, par)

            def group_queries(g, par):
                dve.tensor_tensor(ku_g[par][:], kT_t[:, :, :, ds(GB * g, GB)],
                                  vec[:, V_U:V_U + NH].unsqueeze(2).unsqueeze(3).broadcast_to([P, NH, SEQ, GB]),
                                  ALU.add).then_inc(ku_ready, 1)

            def group_max(g, par):
                for h in range(2):
                    dve.wait_ge(con_full, 2 * g + h + 1)
                    pos = pos_g[:, ds(g, 1), 4 * h:4 * h + 4, :].rearrange("p a n j -> p (a n j)").unsqueeze(2)
                    dve.tensor_tensor(att[par][:, 4 * h:4 * h + 4, :].rearrange("p n (j b) -> p (n j) b", b=GB),
                                      bank[2 + h][:].rearrange("p (n j b) -> p (n j) b", n=4, b=GB),
                                      pos.broadcast_to([P, 4 * SEQ, GB]), ALU.add).then_inc(con_out, 1)
                dve.wait_ge(con_out, 2 * g + 2)
                chain(dve.tensor_reduce(a_max[par][:], att[par][:], AX, ALU.max, negate=True))
                dve.tensor_scalar(a_bias[par][:], a_max[par][:], ATT_SCALE, None, ALU.mult).then_inc(abias_ready, 1)

            def group_inv(g, par):
                dve.wait_ge(exp_ready, g + 1)
                dve.reciprocal(a_inv[par][:], a_sum[par][:]).then_inc(ainv_ready, 1)

            def groupT_out(g):
                dve.wait_ge(attT_full, 2 * g + 2)
                dve.tensor_copy(attT[:, 4:8, :].rearrange("p n q -> p (n q)"), bank[5][:]).then_inc(attT_dve, 1)

            def group_out(g):
                dve.wait_ge(o_full, 2 * g + 2)
                dve.tensor_copy(oT_t[:, 4:8, :, ds(GB * g, GB)],
                                bank[7][:].rearrange("p (n i b) -> p n i b", n=4, i=SEQ)).then_inc(o_dve, 1)

            group_queries(0, 0)
            group_queries(1, 1)
            dve.wait_ge(pos_loaded, 16 * SEQ)
            group_max(0, 0)
            group_max(1, 1)
            group_inv(0, 0)
            chain.enter()
            with dve.Fori(0, NG // 2 - 1) as i:
                chain.turn(i, 2)
                for par in range(2):
                    g = 2 * i + par
                    dve.wait_ge(con_full, 2 * g + 2)
                    group_queries(g + 2, par)
                    groupT_out(g)
                    group_inv(g + 1, 1 - par)
                    group_out(g)
                    group_max(g + 2, par)
            chain.leave(NG // 2 - 1)
            groupT_out(NG - 2)
            group_inv(NG - 1, 1)
            group_out(NG - 2)
            groupT_out(NG - 1)
            group_out(NG - 1)
            dve.wait_ge(bout_added, 1)
            for k in range(NT):
                dve.wait_ge(y2_full, k + 1)
                dve.tensor_tensor(y[:, k, :], bank[k][:], y[:, k, :], ALU.add).then_inc(y2_ready, 1)

            dve.wait_ge(y2_ready, NT)
            dve.tensor_copy(causal_bf[:], cst[:, C_CAUSAL:C_CAUSAL + P].unsqueeze(1).broadcast_to([P, 4, P])).then_inc(causal_ready, 1)
            row_stats(y)
            chain(dve.tensor_scalar(rs_v[:], var, LN_EPS, None, ALU.add))
            rsqrt(rstd[:], rs_v[:])
            chain(dve.tensor_tensor(rs_v[:], rstd[:], rstd[:], ALU.mult))
            chain(dve.tensor_tensor(rs_v[:], rs_v[:], var, ALU.mult))

            def rms_inverse(dst):
                rsqrt(rs_r[:], rs_v[:])
                chain(dve.tensor_tensor(rs_r[:], rs_r[:], rs_v[:], ALU.mult))
                chain(dve.tensor_scalar(rs_r[:], rs_r[:], RMS_EPS, None, ALU.add))
                chain(dve.reciprocal(dst, rs_r[:]))

            rms_inverse(rms_x[:])
            chain(dve.tensor_tensor(rms_x[:], rms_x[:], rstd[:], ALU.mult))

            def self_norm(k, par):
                dve.tensor_scalar(xn[par][:], row(y, k), mean[:, ds(k, 1)], rms_x[:, ds(k, 1)], ALU.subtract,
                                  ALU.mult).then_inc(xn_ready, 1)
                chain.mark(dve.tensor_scalar(row(xx, k), row(y, k), mean[:, ds(k, 1)], rstd[:, ds(k, 1)], ALU.subtract,
                                             ALU.mult))

            def normT_out(k, par):
                dve.wait_ge(xnT_full, k + 1)
                for c in range(HC):
                    last = dve.tensor_scalar(xnT[par][:, c, :], bank[0][:, c * P:(c + 1) * P], vec[:, V_W1 + c:V_W1 + c + 1],
                                             None, ALU.mult)
                last.then_inc(xnT_ready, 1)
                dve.wait_ge(lat_full, k + 1)
                dve.tensor_copy(latT[par][:].rearrange("l a t -> l (a t)"), bank[1][:, 0:2 * P]).then_inc(lat_ready, 1)

            def rotate(k, par):
                dve.wait_ge(raw_ready, k + 1)
                cos = cst[:, C_COS:C_COS + RD].unsqueeze(1).broadcast_to([P, 2 * HEADS, RD])
                sin = cst[:, C_SIN:C_SIN + RD].unsqueeze(1).broadcast_to([P, 2 * HEADS, RD])
                half = RD // 2
                chain.mark(dve.tensor_tensor(kq[par][:, :, RD:HD], raw[:], cos, ALU.mult))
                chain.mark(dve.tensor_tensor(turned[:, :, 0:half], raw[:, :, half:RD], sin[:, :, 0:half], ALU.mult))
                chain(dve.tensor_tensor(turned[:, :, half:RD], raw[:, :, 0:half], sin[:, :, half:RD], ALU.mult))
                dve.tensor_tensor(kq[par][:, :, RD:HD], kq[par][:, :, RD:HD], turned[:], ALU.add).then_inc(kq_ready, 1)

            def headsT_out(k, par):
                dve.wait_ge(qTh_full, k + 1)
                dve.tensor_copy(qT_h[par][:].rearrange("p c q -> p (c q)"), bank[0][:]).then_inc(qTh_ready, 1)

            def self_max(k, par, c):
                dve.wait_ge(self_full, 4 * k + c + 1)
                at = slice(4 * c, 4 * c + 4)
                chain(dve.tensor_reduce(s_max[par][:, at], bank[4 + c][:].rearrange("p (n q) -> p n q", n=4), AX, ALU.max,
                                        negate=True))
                dve.tensor_scalar(s_bias[par][:, at], s_max[par][:, at], SELF_SCALE, None, ALU.mult).then_inc(sbias_ready, 1)

            def self_inv(k, par):
                for c in range(QUADS):
                    dve.wait_ge(sexp_ready, 4 * k + c + 1)
                    dve.reciprocal(s_inv[par][:, 4 * c:4 * c + 4], s_sum[par][:, 4 * c:4 * c + 4]).then_inc(sinv_ready, 1)

            def weights_out(k):
                for c in range(1, QUADS, 2):
                    dve.wait_ge(spT_full, 4 * k + c + 1)
                    dve.tensor_copy(spT[:, 4 * c:4 * c + 4, :].rearrange("p n q -> p (n q)"), bank[4 + c][:]).then_inc(spT_dve, 1)

            def self_out(k):
                dve.wait_ge(yT_full, k + 1)
                dve.tensor_copy(yT[:].rearrange("p c q -> p (c q)"), bank[4][:]).then_inc(yT_ready, 1)
                dve.wait_ge(wo_full, k + 1)
                dve.tensor_tensor(row(xx, k), bank[7][:], row(xx, k), ALU.add).then_inc(xx_ready, 1)

            def self_step(k, par, norm=True):
                self_max(k, par, 0)
                self_max(k, par, 1)
                normT_out(k + 1, 1 - par)
                self_max(k, par, 2)
                self_max(k, par, 3)
                self_inv(k, par)
                if norm:
                    self_norm(k + 2, par)
                rotate(k + 1, 1 - par)
                weights_out(k)
                headsT_out(k + 1, 1 - par)
                self_out(k)

            self_norm(0, 0)
            normT_out(0, 0)
            rotate(0, 0)
            headsT_out(0, 0)
            self_norm(1, 1)
            self_step(0, 0)
            chain.enter()
            with dve.Fori(0, NT // 2 - 2) as i:
                chain.turn(i, 16)
                self_step(2 * i + 1, 1)
                self_step(2 * i + 2, 0)
            chain.leave(NT // 2 - 2)
            self_step(NT - 3, 1)
            self_step(NT - 2, 0, norm=False)
            for c in range(QUADS):
                self_max(NT - 1, 1, c)
            self_inv(NT - 1, 1)
            weights_out(NT - 1)
            self_out(NT - 1)

            dve.wait_ge(xx_ready, NT)
            row_stats(xx)
            chain(dve.tensor_tensor(rs_v[:], mean, mean, ALU.mult))
            chain(dve.tensor_tensor(rs_v[:], rs_v[:], var, ALU.add))
            rms_inverse(rms_f[:])
            for k in range(NT + 1):
                if k < NT:
                    if k >= 2:
                        dve.wait_ge(xfT_full, k - 1)
                    dve.tensor_scalar(xn2[k % 2][:], xx[:, k, :], rms_f[:, k:k + 1], None, ALU.mult).then_inc(xn2_ready, 1)
                if k >= 1:
                    m, t = k - 1, slice((k - 1) * P, k * P)
                    dve.wait_ge(xfT_full, k)
                    if m >= 2:
                        dve.wait_ge(logit_full, m - 1)
                        dve.wait_ge(xhi_ready, m - 1)
                    for c in range(HC):
                        last = dve.tensor_scalar(xf[m % 2][:, c, :], bank[m % 2][:, c * P:(c + 1) * P],
                                                 vec[:, V_W2 + c:V_W2 + c + 1], None, ALU.mult)
                    last.then_inc(xf_ready, 1)
                    dve.wait_ge(xhi_ready, k)
                    dve.tensor_tensor(xT_lo[:, :, t], xf[m % 2][:], xT_hi.bitcast(F32)[:, :, t], ALU.subtract).then_inc(xlo_ready, 1)
            dve.wait_ge(logit_full, NT)
            dve.wait_ge(router_loaded, 32)
            dve.tensor_tensor(r_p[:, :, 0:NR], bank[2][:, 0:NT * NE].rearrange("p (k e) -> p k e", e=NE)[:, :, 0:NR],
                              rbias_sb[:].unsqueeze(1).broadcast_to([P, NT, NR]), ALU.add).then_inc(logit_ready, 1)
            dve.wait_ge(gate_ready, 1)
            chain(dve.tensor_scalar(r_p[:, :, 0:NR], r_p[:, :, 0:NR], 1.0, None, ALU.add))
            chain(dve.reciprocal(r_p[:, :, 0:NR], r_p[:, :, 0:NR]))
            chain(dve.memset(r_p[:, :, NR:NE], -1.0))

            def spread(t):
                return t[:].unsqueeze(2).broadcast_to([P, NT, NE])

            rank = cst[:, C_RANK:C_RANK + NE].unsqueeze(1).broadcast_to([P, NT, NE])
            for i in range(2):
                chain(dve.tensor_reduce(r_max[i][:], r_p[:], AX, ALU.max))
                chain(dve.tensor_tensor(r_eq[:], r_p[:], spread(r_max[i]), ALU.is_equal))
                chain(dve.tensor_tensor(r_eq[:], r_eq[:], rank, ALU.mult))
                chain(dve.tensor_reduce(r_key[:], r_eq[:], AX, ALU.max))
                chain(dve.tensor_tensor(r_sel[i][:], r_eq[:], spread(r_key), ALU.is_equal))
                if i == 0:
                    chain(dve.scalar_tensor_tensor(r_p[:], r_sel[0][:], -4.0, r_p[:], ALU.mult, ALU.add))
            chain(dve.tensor_tensor(r_key[:], r_max[0][:], r_max[1][:], ALU.add))
            chain(dve.reciprocal(r_key[:], r_key[:]))
            for i in range(2):
                chain(dve.tensor_tensor(r_max[i][:], r_max[i][:], r_key[:], ALU.mult))
                chain(dve.tensor_tensor(r_sel[i][:], r_sel[i][:], spread(r_max[i]), ALU.mult))
            chain(dve.memset(wts[:, :, 0:1], 1.0))
            chain(dve.tensor_tensor(wts[:, :, 1:NE], r_sel[0][:, :, 0:NR], r_sel[1][:, :, 0:NR], ALU.add))
            dve.wait_ge(y_summed, NT)
            dve.wait_ge(logit_ready, 1)
            dve.wait_ge(xf_ready, NT)
            dve.sem_inc(hm_ready, 2)
            dve.sem_inc(down_free, 4)
            with dve.Fori(0, NE) as e:
                for j in range(NJ):
                    dve.wait_ge(silu_ready, NJ * e + j + 1)
                    if j >= 2:
                        dve.wait_ge(hlo_ready, NJ * e + j - 1)
                    dve.tensor_tensor(hm[j % 2][:], act_g[j % 2][:], bank[2 + j % 2][:], ALU.mult).then_inc(hm_ready, 1)
                for k in range(NT):
                    dve.wait_ge(down_full, NT * e + k + 1)
                    dve.scalar_tensor_tensor(y[:, k, :], bank[4 + k % 4][:], wts[:, k, ds(e, 1)], y[:, k, :], ALU.mult,
                                             ALU.add).then_inc(down_free, 1)


def kernel(x, ctx_1024, L0_attn_gamma, L0_attn_beta, L0_attn_Wq, L0_attn_Wv, L0_attn_Wr, L0_attn_u_bias, L0_attn_v_bias,
           L0_attn_Wout, L0_attn_bout, L0_ffn_w_ln1, L0_ffn_w_ln2, L0_ffn_W_kvd, L0_ffn_W_qd, L0_ffn_W_ku, L0_ffn_W_qu,
           L0_ffn_W_vu, L0_ffn_W_ropeq, L0_ffn_W_ropek, L0_ffn_W_o, L0_ffn_Wg_s, L0_ffn_Wu_s, L0_ffn_Wd_s, L0_ffn_Wg_r,
           L0_ffn_Wu_r, L0_ffn_Wd_r, L0_ffn_W_router, L0_ffn_routing_bias):
    import concourse.bacc as bacc
    from concourse.bass_utils import run_bass_kernel_spmd

    def columns(v):
        return np.asarray(v).reshape(-1, P).T

    arrays = {
        "x": np.asarray(x).reshape(TOK, D),
        "ctx_keys": np.asarray(ctx_1024),
        "consts": shape_constants(),
        "vecs": np.concatenate([columns(v) for v in (L0_attn_gamma, L0_attn_beta, L0_ffn_w_ln1, L0_ffn_w_ln2,
                                                     L0_attn_u_bias, L0_attn_v_bias)], axis=1),
        "rows": np.concatenate([np.asarray(L0_attn_bout), np.asarray(L0_ffn_routing_bias)])[None, :],
        "Wq": L0_attn_Wq, "Wv": L0_attn_Wv, "Wr": L0_attn_Wr, "Wout": L0_attn_Wout,
        "Wkvd": L0_ffn_W_kvd, "Wqd": L0_ffn_W_qd, "Wku": L0_ffn_W_ku, "Wqu": L0_ffn_W_qu, "Wvu": L0_ffn_W_vu,
        "Wropeq": L0_ffn_W_ropeq, "Wropek": L0_ffn_W_ropek, "Wo": L0_ffn_W_o,
        "Wexp": np.stack([np.concatenate([np.asarray(s)[None], np.asarray(r)]) for s, r in (
            (L0_ffn_Wg_s, L0_ffn_Wg_r), (L0_ffn_Wu_s, L0_ffn_Wu_r), (L0_ffn_Wd_s, L0_ffn_Wd_r))]),
        "Wrouter": L0_ffn_W_router,
    }
    arrays = {f"in_{n}": np.ascontiguousarray(a) for n, a in arrays.items()}
    nc = bacc.Bacc("TRN2", target_bir_lowering=False, num_devices=1)
    args = [nc.dram_tensor(n, a.shape, mybir.dt.from_np(a.dtype), kind="ExternalInput").ap() for n, a in arrays.items()]
    args.append(nc.dram_tensor("out", (TOK, D), F32, kind="ExternalOutput").ap())
    perceiver_kernel(nc, *args)
    r = run_bass_kernel_spmd(nc, [arrays], core_ids=[0])
    return np.asarray(r.results[0]["out"]).reshape(16, 64, D)
```

```python
from contextlib import ExitStack

import numpy as np

import concourse.bass as bass
from concourse import mybir
from concourse.alu_op_type import AluOpType as ALU

F32 = mybir.dt.float32
F32R = mybir.dt.float32r
BF16 = mybir.dt.bfloat16
I32 = mybir.dt.int32
U32 = mybir.dt.uint32
ACT = mybir.ActivationFunctionType
AX = mybir.AxisListType.X
ds = bass.ds

P = 128
D = 512
HC = D // P
TOK = 16 * 64
NT = TOK // P
SQ = 64
SK = 1601
JM = SK // P
TAIL = SK - JM * P
JT = JM + 1
S_CHUNKS = [(0, 401), (401, 400), (801, 400), (1201, 400)]
RING = 3
T_FILLS = 2 * JT
P_FILLS = -(-JT // 4)
BLOCK = T_FILLS + P_FILLS
assert BLOCK % RING == 0 and BLOCK % 2 == 0
NG, GB, NH, F, SEQ = 8, 8, 8, 128, 16
BATCH = NG * GB
PADDED = SEQ + 1
ATT_SCALE = D ** -0.5
LN_EPS = 1e-5
V_GAMMA, V_BETA, V_W1, V_W2, V_U, V_V, V_END = 0, 4, 8, 12, 16, 24, 32
NEG = -1e30

HEADS, HD, RD, LAT = 16, 32, 16, 128
QUADS = HEADS // 4
SELF_SCALE = HD ** -0.5
RMS_EPS = 1e-5
NE = 8
NR = NE - 1
HALF = TOK // 2
NJ = 2 * HC
PICKS = 2 * TOK
TILES = PICKS // P + NR - 1
PLACES = [3, 2, 0, 1, 4, 5, 6]
C_IDENT, C_PE, C_BLOCK, C_CAUSAL, C_COS, C_SIN, C_TRIL, C_RANK, C_BELOW, C_TILE, C_FILL, C_EARLIER, C_PLACE, \
    C_NEED, C_END = np.cumsum([0, P, HC * 16, P, P, 16, 16, NG * NH, NE, P, TILES, NE, NE * NE, NE, NE]).tolist()


def shape_constants():
    c = np.zeros((P, C_END), np.float32)
    c[:, C_IDENT:C_IDENT + P] = np.eye(P)
    pos = np.arange(16, dtype=np.float32)[:, None]
    div = np.exp(np.arange(0, D, 2, dtype=np.float32) * np.float32(-np.log(10000.0) / D))
    ang = pos * div
    pe = np.stack([np.sin(ang), np.cos(ang)], axis=-1).reshape(16, D)[::-1]
    c[:, C_PE:C_PE + HC * 16] = pe.T.reshape(HC, P, 16).transpose(1, 0, 2).reshape(P, HC * 16)
    p, q = np.arange(P)[:, None], np.arange(P)[None, :]
    c[:, C_BLOCK:C_BLOCK + P] = np.where(p % 8 == q % 8, 0.0, NEG)
    c[:, C_CAUSAL:C_CAUSAL + P] = np.where((p // 64 == q // 64) & (q <= p), 0.0, NEG)
    inv = (1.0 / np.float32(10000.0) ** (np.arange(0, 16, 2, dtype=np.float32) / np.float32(16))).astype(np.float32)
    f = (np.arange(P) % 64).astype(np.float32)[:, None] * inv[None, :]
    c[:, C_COS:C_COS + 16] = np.concatenate([np.cos(f), np.cos(f)], 1)
    c[:, C_SIN:C_SIN + 16] = np.concatenate([-np.sin(f), np.sin(f)], 1)
    batch = np.arange(NG)[None, :, None] * GB + (p % GB)[:, :, None]
    c[:, C_TRIL:C_TRIL + NG * NH] = (np.arange(NH)[None, None, :] <= batch).reshape(P, NG * NH)
    c[:, C_RANK:C_RANK + NE] = NE - np.arange(NE)
    c[:, C_BELOW:C_BELOW + P] = p < q
    c[:, C_TILE:C_TILE + TILES] = np.arange(TILES)
    c[:, C_FILL:C_FILL + NE] = P * np.arange(NE)
    c[:, C_EARLIER:C_EARLIER + NE * NE] = (np.arange(NE)[None, :] < np.arange(NE)[:, None]).reshape(-1)
    c[:, C_PLACE:C_PLACE + NR] = np.diff([0] + PLACES)
    c[:, C_NEED:C_NEED + NR] = 3 * 16
    return c


class Steps:

    def __init__(self, eng, sem):
        self.eng, self.sem, self.base, self.n = eng, sem, 0, 0

    def mark(self, ins):
        ins.then_inc(self.sem, 1)
        self.n += 1

    def wait(self):
        self.eng.wait_ge(self.sem, self.base + self.n)

    def __call__(self, ins):
        self.mark(ins)
        self.wait()

    def enter(self):
        self.start, self.n = self.base + self.n, 0

    def turn(self, i, per):
        self.base, self.n, self.per = self.start + i * per, 0, per

    def leave(self, turns):
        assert self.n == self.per, self.n
        self.base, self.n = self.start + turns * self.per, 0


def perceiver_kernel(nc, x, ctx_keys, consts, vecs, rows, Wq, Wv, Wr, Wout, Wkvd, Wqd, Wku, Wqu, Wvu, Wropeq, Wropek,
                     Wo, Wexp, Wrouter, out):
    with ExitStack() as ctx:
        def sem(name):
            return ctx.enter_context(nc.semaphore(name))

        def sbuf(scope, name, shape, dt=F32):
            return scope.enter_context(nc.sbuf_tensor(name, shape, dt))

        bank = [ctx.enter_context(nc.psum_tensor(f"bank{i}", [P, 512], F32)) for i in range(8)]

        y = sbuf(ctx, "y", [P, NT, D])
        cst = sbuf(ctx, "cst", [P, C_END])
        ident = cst[:, C_IDENT:C_IDENT + P]
        stats = sbuf(ctx, "stats", [P, NT, 6])
        mv = sbuf(ctx, "mv", [P, NT, 2])
        mean, var = mv[:, :, 0], mv[:, :, 1]
        rstd = sbuf(ctx, "rstd", [P, NT])
        rs_v = sbuf(ctx, "rs_v", [P, NT])
        rs_h = sbuf(ctx, "rs_h", [P, NT])
        rs_t = sbuf(ctx, "rs_t", [P, NT])
        rs_r = sbuf(ctx, "rs_r", [P, NT])

        vec = sbuf(ctx, "vec", [P, V_END])
        ident_bf = sbuf(ctx, "ident_bf", [P, P], BF16)
        stats2 = sbuf(ctx, "stats2", [P, NT, 6])
        mv2 = sbuf(ctx, "mv2", [P, NT, 2])
        rstd2 = sbuf(ctx, "rstd2", [P, NT])
        hn = [sbuf(ctx, f"hn{i}", [P, D]) for i in range(4)]
        s_max, s_bias, s_sum, s_inv = ([sbuf(ctx, f"{n}{i}", [P, HEADS]) for i in range(2)]
                                       for n in ("s_max", "s_bias", "s_sum", "s_inv"))
        rms_x, rms_f = sbuf(ctx, "rms_x", [P, NT]), sbuf(ctx, "rms_f", [P, NT])
        gates = [sbuf(ctx, f"gates{i}", [P, NT]) for i in range(2)]
        slots = sbuf(ctx, "slots", [P, NT, 2], U32)
        tile_expert = sbuf(ctx, "tile_expert", [P, 2, TILES], I32)
        rbias_sb = sbuf(ctx, "rbias_sb", [P, NR])
        wrout_sb = sbuf(ctx, "wrout_sb", [P, HC, NR])
        a_max, a_bias, a_sum, a_inv = ([sbuf(ctx, f"{n}{i}", [P, NH]) for i in range(2)]
                                       for n in ("a_max", "a_bias", "a_sum", "a_inv"))

        scope = ExitStack()
        nat = [sbuf(scope, f"nat{i}", [P, 2, JT, D]) for i in range(2)]
        ctxT = [sbuf(scope, f"ctxT{i}", [P, HC, SK]) for i in range(2)]
        prob = sbuf(scope, "prob", [P, SK])
        probT = sbuf(scope, "probT", [P, JT, P])
        qn = sbuf(scope, "qn", [P, D])
        qT = sbuf(scope, "qT", [P, HC, P])
        mx = sbuf(scope, "mx", [P, 4])
        nmax = sbuf(scope, "nmax", [P, 1])
        sums = sbuf(scope, "sums", [P, 4])
        total = sbuf(scope, "total", [P, 1])
        rinv = sbuf(scope, "rinv", [P, 1])
        scope.close()

        def place(kb, name, shape, dt=F32):
            with ExitStack() as below:
                if kb:
                    sbuf(below, f"{name}_below", [P, int(kb * 256)])
                return sbuf(below, name, shape, dt)

        wq_raw = place(0, "wq_raw", [P, HC, NH * F])
        wq_lo = place(0, "wq_lo", [P, HC, NH * F], F32R)
        wq_hi = place(16, "wq_hi", [P, HC, NH * F], F32R)
        wout_raw = place(0, "wout_raw", [P, NH, D])
        wout_lo = place(0, "wout_lo", [P, NH, D], F32R)
        wout_hi = place(16, "wout_hi", [P, NH, D], F32R)
        wr_sb = place(32, "wr_sb", [P, HC, NH * F])
        wv_hi = place(32, "wv_hi", [P, HC, NH * F], F32R)
        wv_raw = place(84, "wv_raw", [P, HC, NH * F])
        wv_lo = place(84, "wv_lo", [P, HC, NH * F], F32R)
        bout_sb = place(48, "bout_sb", [P, D])
        block_bf = place(50, "block_bf", [P, 4, P], BF16)
        rT_sb = place(51, "rT_sb", [P, NH * SEQ])
        kT = place(52, "kT", [P, NH, NG, P])
        oT = kT
        pos_g = place(100, "pos_g", [P, NG, SEQ * NH])
        h_hi = place(104, "h_hi", [P, HC, NG, P], F32R)
        h_lo = place(120, "h_lo", [P, HC, NG, P], F32R)
        hf = [place(136 + 2 * i, f"hf{i}", [P, HC, NG, 2 * GB]) for i in range(2)]
        hg_lo = [place(136 + 2 * i, f"hg_lo{i}", [P, HC, P], F32R) for i in range(2)]
        pos_sb = place(140, "pos_sb", [P, NG, PADDED * NH])
        kv_g = [place(146 + 4 * i, f"kv_g{i}", [P, NH, P]) for i in range(4)]
        ku_g = [place(162 + 4 * i, f"ku_g{i}", [P, NH, P]) for i in range(2)]
        attT = place(146, "attT", [P, NH, P])
        hg_hi = [place(150 + 2 * i, f"hg_hi{i}", [P, HC, P], F32R) for i in range(2)]
        att = [place(154 + 4 * i, f"att{i}", [P, NH, P]) for i in range(2)]
        v_g = [place(170 + 4 * i, f"v_g{i}", [P, NH * F]) for i in range(2)]
        o_hi = [place(104 + 4 * i, f"o_hi{i}", [P, NH, P], F32R) for i in range(2)]
        o_lo = [place(112 + 4 * i, f"o_lo{i}", [P, NH, P], F32R) for i in range(2)]
        wkvd_sb = place(120, "wkvd_sb", [P, HC, LAT])
        wqd_sb = place(122, "wqd_sb", [P, HC, LAT])
        wku_sb = place(124, "wku_sb", [LAT, HEADS * RD])
        wvu_sb = place(125, "wvu_sb", [LAT, D])
        wq_up = place(127, "wq_up", [LAT, 2, HEADS * RD])
        wrk_sb = place(129, "wrk_sb", [P, HC, HEADS * RD])
        xnT = [place(133 + 2 * i, f"xnT{i}", [P, HC, P]) for i in range(2)]
        latT = [place(137 + i, f"latT{i}", [LAT, 2, P]) for i in range(2)]
        kq = [place(139 + 4 * i, f"kq{i}", [P, 2 * HEADS, HD]) for i in range(2)]
        raw = place(147, "raw", [P, 2 * HEADS, RD])
        turned = place(149, "turned", [P, 2 * HEADS, RD])
        causal_bf = place(151, "causal_bf", [P, 4, P], BF16)
        yT = place(152, "yT", [P, HC, P])
        zeros = place(172, "zeros", [P, D])
        xx = place(48, "xx", [P, NT, D])
        wo_sb = place(64, "wo_sb", [P, HC, D])
        spT = place(72, "spT", [P, HEADS, P])
        v_t = [place(80 + 2 * i, f"v_t{i}", [P, D]) for i in range(2)]
        qT_h = [place(84 + 2 * i, f"qT_h{i}", [P, QUADS, P]) for i in range(2)]
        kT_h = [place(88 + 8 * i, f"kT_h{i}", [P, QUADS, 4, P]) for i in range(2)]
        sp_ = [place(104 + 8 * i, f"sp{i}", [P, HEADS, P]) for i in range(2)]
        xn = hn[0:2]
        w_raw = [place(8 * i, f"w_raw{i}", [P, HC, D]) for i in range(3)]
        w_lo = [place(8 * i, f"w_lo{i}", [P, HC, D], F32R) for i in range(3)]
        w_hi = [place(24 + 8 * i, f"w_hi{i}", [P, HC, D], F32R) for i in range(3)]
        xf = [hn[2 + i][:].rearrange("p (c t) -> p c t", c=HC) for i in range(2)]
        xT_hi = place(120, "xT_hi", [P, HC, TOK], F32R)
        xT_lo = place(136, "xT_lo", [P, HC, TOK], F32R)
        hm_hi = place(152, "hm_hi", [P, HC, TOK], F32R)
        hm_lo = place(104, "hm_lo", [P, HC, TOK], F32R)
        act_g = [place(168 + 2 * i, f"act_g{i}", [P, HALF]) for i in range(2)]
        hm = [place(172 + 2 * i, f"hm{i}", [P, HALF]) for i in range(2)]
        r_p, r_eq, r_sel0, r_sel1 = (place(64 + i / 4, n, [P, NT, NE]) for i, n in enumerate(("r_p", "r_eq", "r_sel0", "r_sel1")))
        r_sel = [r_sel0, r_sel1]
        r_key = place(65, "r_key", [P, NT])
        r_picks = place(65.25, "r_picks", [P, NT, NE], BF16)
        r_first = place(65.5, "r_first", [P, 3, NE])
        below_bf = place(66, "below_bf", [P, P], BF16)
        ones_bf = place(66.25, "ones_bf", [P, P], BF16)
        r_begun = place(67, "r_begun", [P, TILES, NE])
        r_fill = place(68, "r_fill", [P, NE, NE])
        r_tile = place(68.25, "r_tile", [P, 2, TILES])
        r_slot = place(68.5, "r_slot", [P, NT, 2])
        w_all = place(0, "w_all", [P, NR, 3, HC, D])
        xg = hn[0:2]
        xgT = [place(168 + 2 * i, f"xgT{i}", [P, HC, P]) for i in range(2)]
        rhm = place(172, "rhm", [P, D])
        rhmT = place(174, "rhmT", [P, HC, P])
        yo = hn[2:4]
        picked = [place(2 * i, f"picked{i}", [P, D]) for i in range(2 * NT)]
        pos_dram = nc.dram_tensor("pos_dram", (BATCH, SEQ * PADDED * NH), F32).ap()
        x_slots = nc.dram_tensor("x_slots", (TILES * P, D), F32).ap()
        y_slots = nc.dram_tensor("y_slots", (TILES * P, D), F32).ap()

        w_loaded = {n: sem(f"{n}_loaded") for n in ("wr", "wq", "wv", "wout", "bout")}
        consts_cast = sem("consts_cast")
        whi_ready, wlo_ready = sem("whi_ready"), sem("wlo_ready")
        SPLIT = {"wq": 0, "wv": HC, "wout": 2 * HC, "gate": 3 * HC, "up": 3 * HC + 1, "down": 3 * HC + 2}
        hn_ready, hT_full, hf_act, hf_dve, hhi_done, hlo_done = (sem(n) for n in ("hn_ready", "hT_full", "hf_act", "hf_dve", "hhi_done", "hlo_done"))
        rT_full, rT_ready, kT_full, kT_act, kT_dve = (sem(n) for n in ("rT_full", "rT_ready", "kT_full", "kT_act", "kT_dve"))
        kv_act, kv_dve, pos_full, pos_out, pos_stored = (sem(n) for n in ("kv_act", "kv_dve", "pos_full", "pos_out", "pos_stored"))
        pos_loaded = [sem(f"pos_loaded{i}") for i in range(2)]
        hg_act, hg_dve, ku_ready, v_full, v_out, con_full, con_out = (sem(n) for n in ("hg_act", "hg_dve", "ku_ready", "v_full", "v_out", "con_full", "con_out"))
        abias_ready, exp_ready, ainv_ready, att_ready = (sem(n) for n in ("abias_ready", "exp_ready", "ainv_ready", "att_ready"))
        attT_full, attT_act, attT_dve, o_full, o_act, o_dve = (sem(n) for n in ("attT_full", "attT_act", "attT_dve", "o_full", "o_act", "o_dve"))
        ohi_ready, olo_ready = sem("ohi_ready"), sem("olo_ready")
        bout_added, y2_full, y2_ready = sem("bout_added"), sem("y2_full"), sem("y2_ready")

        mla_loaded, router_loaded, raw_loaded = sem("mla_loaded"), sem("router_loaded"), sem("raw_loaded")
        causal_ready, cleared, xn_ready, xnT_full, xnT_ready = (sem(n) for n in ("causal_ready", "cleared", "xn_ready", "xnT_full", "xnT_ready"))
        lat_full, lat_ready, k_full, vv_full, q_full = (sem(n) for n in ("lat_full", "lat_ready", "k_full", "vv_full", "q_full"))
        raw_ready, vv_ready, kq_ready, qTh_full, kTh_full = (sem(n) for n in ("raw_ready", "vv_ready", "kq_ready", "qTh_full", "kTh_full"))
        qTh_ready, kTh_ready, self_full, sbias_ready, sexp_ready = (sem(n) for n in ("qTh_ready", "kTh_ready", "self_full", "sbias_ready", "sexp_ready"))
        sinv_ready, sp_ready, spT_full, spT_act, spT_dve = (sem(n) for n in ("sinv_ready", "sp_ready", "spT_full", "spT_act", "spT_dve"))
        yT_full, yT_ready, wo_full, xx_ready, y_summed = (sem(n) for n in ("yT_full", "yT_ready", "wo_full", "xx_ready", "y_summed"))
        xn2_ready, xfT_full, xf_ready, logit_full, logit_ready, gate_ready = (sem(n) for n in ("xn2_ready", "xfT_full", "xf_ready", "logit_full", "logit_ready", "gate_ready"))
        xhi_ready, xlo_ready, wo_loaded = sem("xhi_ready"), sem("xlo_ready"), sem("wo_loaded")
        gu_full, silu_ready, hm_ready, hhi_ready, hlo_ready = (sem(n) for n in ("gu_full", "silu_ready", "hm_ready", "hhi_ready", "hlo_ready"))
        down_added, down_full = sem("down_added"), sem("down_full")
        slots_zeroed, picks_ready, ranks_full, slots_ready, scattered = (
            sem(n) for n in ("slots_zeroed", "picks_ready", "ranks_full", "slots_ready", "scattered"))
        routed_loaded, xg_loaded, y_stored = sem("routed_loaded"), *([sem(f"{n}{i}") for i in range(2)] for n in ("xg_loaded", "y_stored"))
        xgT_full, xgT_ready, rgate_full, rup_full, rsilu_ready, rhm_ready, rhmT_full, rhmT_ready, rdown_full, yo_ready = (
            sem(n) for n in ("xgT_full", "xgT_ready", "rgate_full", "rup_full", "rsilu_ready", "rhm_ready", "rhmT_full",
                             "rhmT_ready", "rdown_full", "yo_ready"))
        picked_loaded, first_added, y_ready = [sem(f"picked_loaded{k}") for k in range(NT)], sem("first_added"), sem("y_ready")

        PIECES = [(0, JM // 2), (JM // 2, JM), (JM, JT)]
        x_loaded, cst_loaded, stored = sem("x_loaded"), sem("cst_loaded"), sem("stored")
        keys_loaded = [[[sem(f"keys_loaded{i}{b}{p}") for p in range(3)] for b in range(2)] for i in range(2)]
        ring_full, evac_act, evac_dve = sem("ring_full"), sem("evac_act"), sem("evac_dve")
        qn_ready, qT_full, qT_ready = sem("qn_ready"), sem("qT_full"), sem("qT_ready")
        scores_full, nmax_ready, prob_ready = sem("scores_full"), sem("nmax_ready"), sem("prob_ready")
        context_full, y1_ready = sem("context_full"), sem("y1_ready")
        dve_step = sem("dve_step")

        def evacs(block, g):
            return BLOCK // 2 * block + g // 2 - 1

        def row(t, k):
            return t[:, ds(k, 1), :].rearrange("p a d -> p (a d)")

        block = ctx.enter_context(nc.Block())

        @block.sync
        def _(sp):
            def load_keys(k, par):
                for b in range(2):
                    keys = ctx_keys[ds(2 * k + b, 1)]
                    main = keys[:, 0:JM * P, :].rearrange("a (p j) d -> p (a j) d", j=JM)
                    for p, (j0, j1) in enumerate(PIECES[:2]):
                        sp.dma_start(nat[par][:, b, j0:j1, :], main[:, j0:j1, :]).then_inc(keys_loaded[par][b][p], 16)
                    tail = keys[:, JM * P:SK, :].rearrange("a p d -> p (a d)")
                    sp.dma_start(nat[par][0:TAIL, b, JM, :], tail).then_inc(keys_loaded[par][b][2], 16)

            sp.dma_start(y[:], x.rearrange("(k p) d -> p k d", p=P)).then_inc(x_loaded, 16)
            sp.dma_start(cst[:], consts).then_inc(cst_loaded, 16)
            sp.dma_start(vec[:], vecs).then_inc(cst_loaded, 16)
            load_keys(0, 0)
            load_keys(1, 1)
            with sp.Fori(0, NT // 2 - 1) as i:
                for par in range(2):
                    sp.wait_ge(context_full, 2 * i + par + 1)
                    load_keys(2 * i + par + 2, par)
            sp.wait_ge(context_full, NT - 1)
            sp.dma_start(wq_raw[:], Wq.rearrange("(c p) n -> p c n", p=P)).then_inc(w_loaded["wq"], 16)
            sp.dma_start(wr_sb[:], Wr.rearrange("(c p) n -> p c n", p=P)).then_inc(w_loaded["wr"], 16)
            sp.dma_start(bout_sb[:], rows[0, 0:D].partition_broadcast(P)).then_inc(w_loaded["bout"], 16)
            sp.wait_ge(y1_ready, NT)
            sp.dma_start(wv_raw[:], Wv.rearrange("(c p) n -> p c n", p=P)).then_inc(w_loaded["wv"], 16)
            sp.wait_ge(kT_full, 2 * NH)
            sp.dma_start(wout_raw[:], Wout.rearrange("(n p) d -> p n d", p=P)).then_inc(w_loaded["wout"], 16)
            half_groups = NG // 2
            for h in range(2):
                at = slice(h * half_groups * GB, (h + 1) * half_groups * GB)
                groups = slice(h * half_groups, (h + 1) * half_groups)
                sp.wait_ge(pos_out, half_groups * (h + 1))
                for i in range(SEQ):
                    sp.dma_start(pos_dram[at, i * PADDED * NH:(i + 1) * PADDED * NH].rearrange("(g b) f -> b g f", b=GB),
                                 pos_sb[GB * i:GB * i + GB, groups, :]).then_inc(pos_stored, 16)
                sp.wait_ge(pos_stored, 16 * SEQ * (h + 1))
                for i in range(SEQ):
                    sp.dma_start(pos_g[GB * i:GB * i + GB, groups, :],
                                 pos_dram[at, (i + 1) * SEQ * NH:(i + 2) * SEQ * NH].rearrange("(g b) f -> b g f", b=GB)
                                 ).then_inc(pos_loaded[h], 16)
            sp.wait_ge(v_full, 2 * NG)
            for dst, src in ((wkvd_sb[:], Wkvd.rearrange("(c p) n -> p c n", p=P)), (wqd_sb[:], Wqd.rearrange("(c p) n -> p c n", p=P)),
                             (wrk_sb[:], Wropek.rearrange("(c p) n -> p c n", p=P)), (wku_sb[:], Wku), (wvu_sb[:], Wvu),
                             (wq_up[:, 0, :], Wqu), (wq_up[:, 1, :], Wropeq)):
                sp.dma_start(dst, src).then_inc(mla_loaded, 16)
            sp.dma_start(wrout_sb[:], Wrouter.rearrange("(c p) n -> p c n", p=P)).then_inc(router_loaded, 16)
            sp.dma_start(rbias_sb[:], rows[0, D:D + NR].partition_broadcast(P)).then_inc(router_loaded, 16)

            def matrix(m, e):
                return Wexp[m, e].rearrange("(c p) n -> p c n", p=P)

            sp.wait_ge(y2_full, NT)
            sp.dma_start(wo_sb[:], Wo.rearrange("(c p) n -> p c n", p=P)).then_inc(wo_loaded, 16)
            for m in range(3):
                sp.dma_start(w_raw[m][:], matrix(m, 0)).then_inc(raw_loaded, 16)
            sp.wait_ge(cleared, 3)
            sp.dma_start(x_slots.rearrange("(t p) d -> p t d", p=P),
                         zeros[:].unsqueeze(1).broadcast_to([P, TILES, D])).then_inc(slots_zeroed, 16)
            for e in range(NR):
                if e == 0:
                    sp.wait_ge(wo_full, NT)
                elif e == 1:
                    sp.wait_ge(scattered, 16 * 2 * NT)
                elif e == 2:
                    sp.wait_ge(down_full, NT)
                for m in range(3):
                    sp.dma_start(w_all[:, PLACES[e], m, :, :], matrix(m, e + 1)).then_inc(routed_loaded, 16)
                sp.wait_ge(routed_loaded, 3 * 16 * (e + 1))
            for k in range(NT):
                sp.wait_ge(y_ready, k + 1)
                sp.dma_start(out[k * P:(k + 1) * P, :], y[:, k, :]).then_inc(stored, 16)
            sp.wait_ge(stored, 16 * NT)

        @block.tensor
        def _(pe):
            def ring_free(blk, g):
                v = evacs(blk, g - RING)
                if not (isinstance(v, int) and v <= 0):
                    pe.wait_ge(evac_act if (g - RING) % 2 == 0 else evac_dve, v)

            def key_transposes(k, par, blk, g0):
                turn = 16 * (k // 2 + 1) if isinstance(k, int) else k
                for b in range(2):
                    for j in range(JT):
                        for p, (j0, _) in enumerate(PIECES):
                            if j == j0:
                                pe.wait_ge(keys_loaded[par][b][p], turn)
                        g = g0 + b * JT + j
                        n = P if j < JM else TAIL
                        ring_free(blk, g)
                        for c in range(HC):
                            last = nc.tensor.transpose(bank[4 + g % RING][:, c * P:c * P + n],
                                                       nat[par][0:n, b, j, c * P:(c + 1) * P], ident[0:n, 0:n])
                        last.then_inc(ring_full, 1)

            def query_transposes(k):
                pe.wait_ge(qn_ready, k + 1)
                for c in range(HC):
                    last = nc.tensor.transpose(bank[7][:, c * P:(c + 1) * P], qn[:, c * P:(c + 1) * P], ident)
                last.then_inc(qT_full, 1)

            def scores(k, blk, g_last):
                pe.wait_ge(qT_ready, k + 1)
                for g in (g_last - 1, g_last):
                    pe.wait_ge(evac_act if g % 2 == 0 else evac_dve, evacs(blk, g))
                if not (isinstance(k, int) and k == 0):
                    pe.wait_ge(prob_ready, 4 * k)
                for n, (s0, w) in enumerate(S_CHUNKS):
                    for c in range(HC):
                        for b in range(2):
                            last = nc.tensor.matmul(bank[n][64 * b:64 * b + 64, 0:w], qT[:, c, 64 * b:64 * b + 64],
                                                    ctxT[b][:, c, s0:s0 + w], start=c == 0, stop=c == HC - 1,
                                                    skip_group_check=True)
                    last.then_inc(scores_full, 1)

            def prob_transposes(k, blk, g0):
                pe.wait_ge(prob_ready, 4 * k + 4)
                for f in range(P_FILLS):
                    g = g0 + f
                    ring_free(blk, g)
                    for j in range(4 * f, min(4 * f + 4, JT)):
                        n = P if j < JM else TAIL
                        last = nc.tensor.transpose(bank[4 + g % RING][0:n, (j % 4) * P:(j % 4 + 1) * P],
                                                   prob[:, j * P:j * P + n], ident)
                    last.then_inc(ring_full, 1)

            def context(k, par, blk, g_last):
                for g in (g_last - 1, g_last):
                    pe.wait_ge(evac_act if g % 2 == 0 else evac_dve, evacs(blk, g))
                for j in range(JT):
                    n = P if j < JM else TAIL
                    for b in range(2):
                        last = nc.tensor.matmul(bank[7][64 * b:64 * b + 64, :], probT[0:n, j, 64 * b:64 * b + 64],
                                                nat[par][0:n, b, j, :], start=j == 0, stop=j == JT - 1,
                                                skip_group_check=True)
                last.then_inc(context_full, 1)

            def step(k, par, turn):
                if not (isinstance(k, int) and k == 0):
                    pe.wait_ge(y1_ready, k)
                query_transposes(k + 1)
                key_transposes(turn, 1 - par, k + 1, 0)
                prob_transposes(k, k + 1, T_FILLS)
                pe.wait_ge(qT_ready, k + 2)
                context(k, par, k + 1, BLOCK - 1)
                scores(k + 1, k + 1, T_FILLS - 1)

            pe.wait_ge(cst_loaded, 32)
            query_transposes(0)
            key_transposes(0, 0, 0, BLOCK - T_FILLS)
            scores(0, 0, BLOCK - 1)
            step(0, 0, 1)
            with pe.Fori(0, NT // 2 - 1) as i:
                step(2 * i + 1, 1, 16 * i + 32)
                step(2 * i + 2, 0, 16 * i + 32)
            prob_transposes(NT - 1, NT, 0)

            def norm_transposes(k):
                pe.wait_ge(hn_ready, k + 1)
                if k >= 4:
                    pe.wait_ge(hf_dve if k % 2 else hf_act, (k - 4) // 2 + 1)
                for c in range(HC):
                    last = nc.tensor.transpose(bank[k % 4][:, c * P:(c + 1) * P], hn[k % 4][:, c * P:(c + 1) * P], ident)
                last.then_inc(hT_full, 1)

            def keys(half, n):
                m = half * NH + n
                if m >= 4:
                    pe.wait_ge(kT_act if m % 2 == 0 else kT_dve, (m - 4) // 2 + 1)
                for c in range(HC):
                    hi, lo = (t[:, c, n * F:(n + 1) * F] for t in (wq_hi, wq_lo))
                    hh, hl = (t[:, c, :, half * BATCH:(half + 1) * BATCH] for t in (h_hi, h_lo))
                    nc.tensor.matmul(bank[4 + m % 4][:], lo, hh, start=c == 0, stop=False)
                    nc.tensor.matmul(bank[4 + m % 4][:], hi, hl, start=False, stop=False)
                    last = nc.tensor.matmul(bank[4 + m % 4][:], hi, hh, start=False, stop=c == HC - 1)
                last.then_inc(kT_full, 1)

            pe.wait_ge(prob_ready, 4 * NT)
            for k in range(4):
                norm_transposes(k)
            context(NT - 1, 1, NT, P_FILLS - 1)
            for k in range(4, 7):
                norm_transposes(k)
            for part in (whi_ready, wlo_ready):
                pe.wait_ge(part, SPLIT["wq"] + HC)
            pe.wait_ge(hhi_done, NT // 2)
            pe.wait_ge(hlo_done, NT // 2)
            for n in range(NH):
                if n == 3:
                    pe.wait_ge(y1_ready, NT)
                if n == 4:
                    norm_transposes(7)
                    pe.wait_ge(w_loaded["wr"], 16)
                    pe.wait_ge(hf_act, 4)
                    for m in range(NH):
                        for c in range(HC):
                            last = nc.tensor.matmul(bank[2][:, m * SEQ:(m + 1) * SEQ], wr_sb[:, c, m * F:(m + 1) * F],
                                                    cst[:, C_PE + c * SEQ:C_PE + (c + 1) * SEQ], start=c == 0, stop=c == HC - 1)
                    last.then_inc(rT_full, 1)
                keys(0, n)
            pe.wait_ge(hhi_done, NT)
            pe.wait_ge(hlo_done, NT)
            for n in range(NH):
                keys(1, n)

            pe.wait_ge(rT_ready, 1)
            for g in range(NG):
                pe.wait_ge(kv_act if g % 2 else kv_dve, g // 2 + 1)
                if g >= 4:
                    pe.wait_ge(pos_out, g - 3)
                for n in range(NH):
                    last = nc.tensor.matmul(bank[g % 4][:, n * SEQ:(n + 1) * SEQ], kv_g[g % 4][:, n, :],
                                            rT_sb[:, n * SEQ:(n + 1) * SEQ], start=True, stop=True)
                last.then_inc(pos_full, 1)

            def group_scores(g, par):
                pe.wait_ge(ku_ready, g + 1)
                if not (isinstance(g, int) and g == 0):
                    pe.wait_ge(con_out, 2 * g)
                for h in range(2):
                    nc.tensor.matmul(bank[h][:], ident_bf[:], block_bf[:].rearrange("p n q -> p (n q)"),
                                     start=True, stop=True)
                    for n in range(4 * h, 4 * h + 4):
                        last = nc.tensor.matmul(bank[h][:, (n % 4) * P:(n % 4 + 1) * P], ku_g[par][:, n, :],
                                                kT[:, n, ds(g, 1), :].rearrange("p a q -> p (a q)"), start=False, stop=True,
                                                skip_group_check=True)
                    last.then_inc(con_full, 1)

            def group_values(g, par):
                pe.wait_ge(hg_act, g + 1)
                pe.wait_ge(hg_dve, g + 1)
                for h in range(2):
                    if not (isinstance(g, int) and g == 0):
                        pe.wait_ge(v_out, 2 * g + h - 1)
                    for c in range(HC):
                        hi, lo = (t[:, c, h * 512:(h + 1) * 512] for t in (wv_hi, wv_lo))
                        nc.tensor.matmul(bank[2 + h][:], hg_lo[par][:, c, :], hi, start=c == 0, stop=False)
                        nc.tensor.matmul(bank[2 + h][:], hg_hi[par][:, c, :], lo, start=False, stop=False)
                        last = nc.tensor.matmul(bank[2 + h][:], hg_hi[par][:, c, :], hi, start=False, stop=c == HC - 1)
                    last.then_inc(v_full, 1)

            def weightsT(g, par):
                pe.wait_ge(att_ready, g + 1)
                for n in range(NH):
                    last = nc.tensor.transpose(bank[4 + n // 4][:, (n % 4) * P:(n % 4 + 1) * P], att[par][:, n, :], ident)
                    if n % 4 == 3:
                        last.then_inc(attT_full, 1)

            def group_output(g, par):
                pe.wait_ge(v_out, 2 * g + 2)
                pe.wait_ge(attT_act, g + 1)
                pe.wait_ge(attT_dve, g + 1)
                if not (isinstance(g, int) and g == 0):
                    pe.wait_ge(o_act, g)
                    pe.wait_ge(o_dve, g)
                for n in range(NH):
                    last = nc.tensor.matmul(bank[6 + n // 4][:, (n % 4) * P:(n % 4 + 1) * P],
                                            v_g[par][:, n * F:(n + 1) * F], attT[:, n, :], start=True, stop=True)
                    if n % 4 == 3:
                        last.then_inc(o_full, 1)

            pe.wait_ge(consts_cast, 2)
            pe.wait_ge(pos_out, NG)
            group_scores(0, 0)
            for part in (whi_ready, wlo_ready):
                pe.wait_ge(part, SPLIT["wv"] + HC)
            group_values(0, 0)
            group_values(1, 1)
            group_scores(1, 1)
            weightsT(0, 0)
            group_scores(2, 0)
            group_output(0, 0)
            group_values(2, 0)
            with pe.Fori(0, NG // 2 - 2) as i:
                for par in (1, 0):
                    g = 2 * i + 2 - par
                    weightsT(g, par)
                    group_scores(g + 2, par)
                    group_output(g, par)
                    group_values(g + 2, par)
            weightsT(NG - 3, 1)
            group_scores(NG - 1, 1)
            group_output(NG - 3, 1)
            group_values(NG - 1, 1)
            for g in (NG - 2, NG - 1):
                weightsT(g, g % 2)
                group_output(g, g % 2)
            for part in (whi_ready, wlo_ready):
                pe.wait_ge(part, SPLIT["wout"] + HC)

            def out_product(k, par):
                pe.wait_ge(ohi_ready, k + 1)
                pe.wait_ge(olo_ready, k + 1)
                for n in range(NH):
                    nc.tensor.matmul(bank[6 + par][:], o_lo[par][:, n, :], wout_hi[:, n, :], start=n == 0, stop=False)
                    nc.tensor.matmul(bank[6 + par][:], o_hi[par][:, n, :], wout_lo[:, n, :], start=False, stop=False)
                    last = nc.tensor.matmul(bank[6 + par][:], o_hi[par][:, n, :], wout_hi[:, n, :], start=False, stop=n == NH - 1)
                last.then_inc(y2_full, 1)

            out_product(0, 0)
            out_product(1, 1)
            with pe.Fori(0, NT // 2 - 1) as i:
                for par in range(2):
                    pe.wait_ge(y2_ready, 2 * i + par + 1)
                    out_product(2 * i + par + 2, par)

            def norm_columns(t, par):
                pe.wait_ge(xn_ready, t + 1)
                if isinstance(t, int) and t in (1, 2):
                    pe.wait_ge(xnT_ready, t)
                elif not isinstance(t, int) or t > 2:
                    pe.wait_ge(yT_ready, t - 2)
                for c in range(HC):
                    last = nc.tensor.transpose(bank[0][:, c * P:(c + 1) * P], xn[par][:, c * P:(c + 1) * P], ident)
                last.then_inc(xnT_full, 1)

            def latents(t, par):
                pe.wait_ge(xnT_ready, t + 1)
                if not (isinstance(t, int) and t == 0):
                    pe.wait_ge(raw_ready, t)
                for i, w in enumerate((wkvd_sb, wqd_sb)):
                    for c in range(HC):
                        last = nc.tensor.matmul(bank[1][:, i * P:(i + 1) * P], w[:, c, :], xnT[par][:, c, :], start=c == 0,
                                                stop=c == HC - 1)
                last.then_inc(lat_full, 1)

            def rotary_keys(par):
                for c in range(HC):
                    nc.tensor.matmul(bank[2][:, 0:256], xnT[par][:, c, :], wrk_sb[:, c, :], start=c == 0, stop=c == HC - 1)

            def from_latents(t, par):
                pe.wait_ge(lat_ready, t + 1)
                nc.tensor.matmul(bank[2][:, 256:512], latT[par][:, 0, :], wku_sb[:], start=True, stop=True).then_inc(k_full, 1)
                nc.tensor.matmul(bank[1][:], latT[par][:, 1, :], wq_up[:].rearrange("l a n -> l (a n)"), start=True,
                                 stop=True).then_inc(q_full, 1)
                if not (isinstance(t, int) and t == 0):
                    pe.wait_ge(kTh_ready, t)
                nc.tensor.matmul(bank[3][:], latT[par][:, 0, :], wvu_sb[:], start=True, stop=True).then_inc(vv_full, 1)

            def heads_columns(par, first, full):
                for c in range(QUADS):
                    last = nc.tensor.transpose(bank[3][:, c * P:(c + 1) * P],
                                               kq[par][:, first + 4 * c:first + 4 * c + 4, :].rearrange("p h d -> p (h d)"),
                                               ident)
                last.then_inc(full, 1)

            def query_columns(t, par):
                pe.wait_ge(kq_ready, t + 1)
                pe.wait_ge(vv_ready, t + 1)
                heads_columns(par, HEADS, qTh_full)

            def key_columns(t, par):
                pe.wait_ge(qTh_ready, t + 1)
                heads_columns(par, 0, kTh_full)

            def self_scores(t, par, quads):
                pe.wait_ge(kTh_ready, t + 1)
                for c in quads:
                    if c >= 2:
                        pe.wait_ge(sexp_ready, 4 * t + c - 1)
                    elif not (isinstance(t, int) and t == 0):
                        pe.wait_ge(sexp_ready, 4 * t + c - 1)
                    nc.tensor.matmul(bank[4 + c % 2][:], ident_bf[:], causal_bf[:].rearrange("p n q -> p (n q)"), start=True,
                                     stop=False)
                    nc.tensor.matmul(bank[4 + c % 2][:], qT_h[par][:, c, :], kT_h[par][:, c, :, :].rearrange("p n q -> p (n q)"),
                                     start=False, stop=True).then_inc(self_full, 1)

            def weight_columns(k, par, quads):
                for c in quads:
                    pe.wait_ge(sp_ready, 4 * k + c + 1)
                    if c >= 2:
                        pe.wait_ge(spT_dve if c % 2 else spT_act, 2 * k + 1)
                    elif c == 0 and not (isinstance(k, int) and k == 0):
                        pe.wait_ge(xx_ready, k)
                    for n in range(4):
                        last = nc.tensor.transpose(bank[6 + c % 2][:, n * P:(n + 1) * P], sp_[par][:, 4 * c + n, :], ident)
                    last.then_inc(spT_full, 1)

            def self_output(k, par):
                pe.wait_ge(spT_act, 2 * k + 2)
                pe.wait_ge(spT_dve, 2 * k + 2)
                for h in range(HEADS):
                    last = nc.tensor.matmul(bank[0][HD * (h % 4):HD * (h % 4 + 1), h // 4 * P:(h // 4 + 1) * P],
                                            v_t[par][:, HD * h:HD * (h + 1)], spT[:, h, :], start=True, stop=True,
                                            skip_group_check=True)
                last.then_inc(yT_full, 1)

            def output_product(k):
                pe.wait_ge(yT_ready, k + 1)
                for c in range(HC):
                    last = nc.tensor.matmul(bank[6][:], yT[:, c, :], wo_sb[:, c, :], start=c == 0, stop=c == HC - 1)
                last.then_inc(wo_full, 1)

            def expert_columns(k):
                pe.wait_ge(xn2_ready, k + 1)
                if k < 2:
                    pe.wait_ge(raw_ready, NT)
                else:
                    pe.wait_ge(xf_ready, k - 1)
                for c in range(HC):
                    last = nc.tensor.transpose(bank[1 + k % 2][:, c * P:(c + 1) * P], xx[:, k, c * P:(c + 1) * P], ident)
                last.then_inc(xfT_full, 1)

            def router(k):
                pe.wait_ge(xf_ready, k + 1)
                for c in range(HC):
                    last = nc.tensor.matmul(bank[3][:, NE * k:NE * k + NR], xf[k % 2][:, c, :], wrout_sb[:, c, :],
                                            start=c == 0, stop=c == HC - 1)
                last.then_inc(logit_full, 1)

            def self_step(k, par, scores=True, project=True):
                if project:
                    norm_columns(k + 2, par)
                if scores:
                    query_columns(k + 1, 1 - par)
                if not scores:
                    for t in range(2):
                        router(t)
                        expert_columns(t + 2)
                weight_columns(k, par, (0, 1))
                if project:
                    latents(k + 2, par)
                if scores:
                    key_columns(k + 1, 1 - par)
                weight_columns(k, par, (2, 3))
                if project:
                    rotary_keys(par)
                if scores:
                    self_scores(k + 1, 1 - par, (0, 1))
                self_output(k, par)
                if project:
                    from_latents(k + 2, par)
                if scores:
                    self_scores(k + 1, 1 - par, (2, 3))
                if scores and not project:
                    expert_columns(0)
                    expert_columns(1)
                if not scores:
                    router(2)
                    router(3)
                output_product(k)

            pe.wait_ge(mla_loaded, 16 * 7)
            pe.wait_ge(causal_ready, 1)
            for t in range(2):
                norm_columns(t, t)
                latents(t, t)
                rotary_keys(t)
                if t == 0:
                    from_latents(t, t)
            query_columns(0, 0)
            key_columns(0, 0)
            pe.wait_ge(y2_ready, NT)
            self_scores(0, 0, (0, 1))
            from_latents(1, 1)
            self_scores(0, 0, (2, 3))
            pe.wait_ge(wo_loaded, 16)
            pe.wait_ge(router_loaded, 32)
            self_step(0, 0)
            with pe.Fori(0, NT // 2 - 2) as i:
                self_step(2 * i + 1, 1)
                self_step(2 * i + 2, 0)
            self_step(NT - 3, 1)
            self_step(NT - 2, 0, project=False)
            self_step(NT - 1, 1, scores=False, project=False)

            gate, up, down = range(3)

            def shared_hidden(j):
                half, ic = divmod(j, HC)
                if j >= 2:
                    pe.wait_ge(hm_ready, j - 1)
                for m, b in ((gate, 4 + j % 2), (up, 6 + j % 2)):
                    for c in range(HC):
                        lo, hi = (w[m][:, c, ic * P:(ic + 1) * P] for w in (w_lo, w_hi))
                        xl, xh = (t[:, c, half * HALF:(half + 1) * HALF] for t in (xT_lo, xT_hi))
                        nc.tensor.matmul(bank[b][:], lo, xh, start=c == 0, stop=False)
                        nc.tensor.matmul(bank[b][:], hi, xl, start=False, stop=False)
                        last = nc.tensor.matmul(bank[b][:], hi, xh, start=False, stop=c == HC - 1)
                last.then_inc(gu_full, 1)

            for part in (whi_ready, wlo_ready):
                pe.wait_ge(part, SPLIT["down"] + 1)
            pe.wait_ge(xx_ready, NT)
            pe.wait_ge(sexp_ready, QUADS * NT)
            pe.wait_ge(spT_dve, 2 * NT)
            for j in range(NJ):
                if j % HC == 0:
                    pe.wait_ge(xhi_ready, NT // 2 * (j // HC + 1))
                    pe.wait_ge(xlo_ready, NT // 2 * (j // HC + 1))
                shared_hidden(j)
                if j == 0:
                    expert_columns(4)
                    expert_columns(5)
                elif j == 1:
                    for k in (4, 5):
                        router(k)
                        expert_columns(k + 2)
                elif j == 2:
                    router(6)
                    router(7)
                elif j == 4:
                    pe.wait_ge(consts_cast, 4)
                    pe.wait_ge(picks_ready, 1)
                    picks = r_picks[:].rearrange("p k e -> p (k e)")
                    nc.tensor.matmul(bank[3][:, 0:NT * NE], below_bf[:], picks, start=True, stop=True)
                    for k in range(1, NT):
                        nc.tensor.matmul(bank[3][:, k * NE:NT * NE], ones_bf[:], picks[:, 0:(NT - k) * NE], start=False,
                                         stop=True, skip_group_check=True)
                    for k in range(NT):
                        last = nc.tensor.matmul(bank[3][:, NT * NE:(NT + 1) * NE], ones_bf[:], r_picks[:, k, :], start=k == 0,
                                                stop=k == NT - 1, skip_group_check=True)
                    last.then_inc(ranks_full, 1)
            pe.wait_ge(yT_ready, NT)
            pe.wait_ge(xf_ready, NT)
            for k in range(NT):
                pe.wait_ge(hhi_ready, HC * (k // 4 + 1))
                pe.wait_ge(hlo_ready, HC * (k // 4 + 1))
                if k >= 3:
                    pe.wait_ge(down_added, k - 2)
                for c in range(HC):
                    hl, hh = (t[:, c, k * P:(k + 1) * P] for t in (hm_lo, hm_hi))
                    nc.tensor.matmul(bank[k % 3][:], hl, w_hi[down][:, c, :], start=c == 0, stop=False)
                    nc.tensor.matmul(bank[k % 3][:], hh, w_lo[down][:, c, :], start=False, stop=False)
                    last = nc.tensor.matmul(bank[k % 3][:], hh, w_hi[down][:, c, :], start=False, stop=c == HC - 1)
                last.then_inc(down_full, 1)

            def expert_of(t):
                return pe.value_load(tile_expert[0:1, 0, ds(t, 1)], min_val=0, max_val=NR - 1)

            def rows_columns(t, par, turn):
                pe.wait_ge(xg_loaded[par], 16 * turn)
                if not (isinstance(t, int) and t == 0):
                    pe.wait_ge(xgT_ready, t)
                for c in range(HC):
                    last = nc.tensor.transpose(bank[0][:, c * P:(c + 1) * P], xg[par][:, c * P:(c + 1) * P], ident)
                last.then_inc(xgT_full, 1)

            def routed_hidden(t, par):
                e = expert_of(t)
                loads = pe.value_load(tile_expert[0:1, 1, ds(t, 1)], min_val=3 * 16, max_val=3 * 16 * NR)
                if not (isinstance(t, int) and t == 0):
                    hidden_columns(t - 1)
                pe.wait_ge(routed_loaded, loads)
                pe.wait_ge(xgT_ready, t + 1)
                for m, b, full in ((gate, 1, rgate_full), (up, 2, rup_full)):
                    if not (isinstance(t, int) and t == 0):
                        pe.wait_ge(rsilu_ready if m == gate else rhm_ready, t)
                    for c in range(HC):
                        last = nc.tensor.matmul(bank[b][:], xgT[par][:, c, :],
                                                w_all[:, ds(e, 1), m, c, :].rearrange("p a d -> p (a d)"), start=c == 0,
                                                stop=c == HC - 1)
                    last.then_inc(full, 1)

            def hidden_columns(t):
                pe.wait_ge(rhm_ready, t + 1)
                if not (isinstance(t, int) and t == 0):
                    pe.wait_ge(rhmT_ready, t)
                for c in range(HC):
                    last = nc.tensor.transpose(bank[3][:, c * P:(c + 1) * P], rhm[:, c * P:(c + 1) * P], ident)
                last.then_inc(rhmT_full, 1)

            def routed_output(t, par):
                e = expert_of(t)
                pe.wait_ge(rhmT_ready, t + 1)
                if not isinstance(t, int) or t >= 2:
                    pe.wait_ge(yo_ready, t - 1)
                for c in range(HC):
                    last = nc.tensor.matmul(bank[4 + par][:], rhmT[:, c, :],
                                            w_all[:, ds(e, 1), down, c, :].rearrange("p a d -> p (a d)"), start=c == 0,
                                            stop=c == HC - 1)
                last.then_inc(rdown_full, 1)

            pe.wait_ge(down_added, NT)
            pe.wait_ge(hm_ready, NJ)
            pe.wait_ge(slots_ready, 2)
            rows_columns(0, 0, 1)
            routed_hidden(0, 0)
            rows_columns(1, 1, 1)
            for t in (1, 2):
                routed_hidden(t, t % 2)
                rows_columns(t + 1, (t + 1) % 2, (t + 1) // 2 + 1)
                routed_output(t - 1, (t - 1) % 2)
            with pe.Fori(0, TILES // 2 - 2) as i:
                for par in (1, 0):
                    t = 2 * i + 4 - par
                    routed_hidden(t, par)
                    rows_columns(t + 1, 1 - par, i + 3)
                    routed_output(t - 1, 1 - par)
            routed_hidden(TILES - 1, 1)
            routed_output(TILES - 2, 0)
            hidden_columns(TILES - 1)
            routed_output(TILES - 1, 1)

        @block.gpsimd
        def _(pool):
            def weight_low(lo, raw, hi, first):
                n = raw.shape[1] // HC
                for c in range(HC):
                    pool.wait_ge(whi_ready, first + c + 1)
                    at = slice(n * c, n * (c + 1))
                    nc.gpsimd.tensor_tensor(lo[:, at, :], raw[:, at, :], hi.bitcast(F32)[:, at, :],
                                            ALU.subtract).then_inc(wlo_ready, 1)

            def normalise(g, par):
                pool.wait_ge(ainv_ready, g + 1)
                nc.gpsimd.tensor_tensor(att[par][:], att[par][:], a_inv[par][:].unsqueeze(2).broadcast_to([P, NH, P]),
                                        ALU.mult).then_inc(att_ready, 1)

            def group_queries(g, par):
                nc.gpsimd.tensor_tensor(ku_g[par][:], kT[:, :, ds(g, 1), :].rearrange("p n a q -> p (n a) q"),
                                        vec[:, V_U:V_U + NH].unsqueeze(2).broadcast_to([P, NH, P]), ALU.add).then_inc(ku_ready, 1)

            weight_low(wq_lo, wq_raw, wq_hi, SPLIT["wq"])
            for k in range(NT):
                pool.wait_ge(hhi_done, k + 1)
                at = slice(2 * GB * k, 2 * GB * (k + 1))
                nc.gpsimd.tensor_tensor(h_lo[:, :, :, at], hf[k % 2][:], h_hi.bitcast(F32)[:, :, :, at],
                                        ALU.subtract).then_inc(hlo_done, 1)
            weight_low(wv_lo, wv_raw, wv_hi, SPLIT["wv"])
            pool.wait_ge(kT_act, NH)
            pool.wait_ge(kT_dve, NH)
            group_queries(0, 0)
            group_queries(1, 1)
            pool.wait_ge(w_loaded["bout"], 16)
            pool.wait_ge(hn_ready, NT)
            nc.gpsimd.tensor_tensor(y[:], y[:], bout_sb[:].unsqueeze(1).broadcast_to([P, NT, D]),
                                    ALU.add).then_inc(bout_added, 1)
            weight_low(wout_lo, wout_raw, wout_hi, SPLIT["wout"])
            normalise(0, 0)
            pool.wait_ge(con_full, 2)
            group_queries(2, 0)
            with pool.Fori(0, NG // 2 - 2) as i:
                for par in (1, 0):
                    g = 2 * i + 2 - par
                    normalise(g, par)
                    pool.wait_ge(con_full, 2 * g + 2)
                    group_queries(g + 2, par)
            normalise(NG - 3, 1)
            pool.wait_ge(con_full, 2 * (NG - 3) + 2)
            group_queries(NG - 1, 1)
            normalise(NG - 2, 0)
            normalise(NG - 1, 1)

            pool.wait_ge(o_full, 2 * NG)
            for t in kT_h:
                nc.gpsimd.memset(t[:], 0.0).then_inc(cleared, 1)
            nc.gpsimd.memset(zeros[:], 0.0).then_inc(cleared, 1)

            def self_normalise(k, par):
                for c in range(QUADS):
                    pool.wait_ge(sinv_ready, 4 * k + c + 1)
                    nc.gpsimd.tensor_tensor(sp_[par][:, 4 * c:4 * c + 4, :], sp_[par][:, 4 * c:4 * c + 4, :],
                                            s_inv[par][:, 4 * c:4 * c + 4].unsqueeze(2).broadcast_to([P, 4, P]),
                                            ALU.mult).then_inc(sp_ready, 1)

            def add_up(k):
                pool.wait_ge(xx_ready, k + 1)
                nc.gpsimd.tensor_tensor(row(y, k), row(y, k), row(xx, k), ALU.add).then_inc(y_summed, 1)

            gate, up, down = range(3)

            def low_part(m):
                pool.wait_ge(whi_ready, SPLIT["gate"] + m + 1)
                nc.gpsimd.tensor_tensor(w_lo[m][:], w_raw[m][:], w_hi[m].bitcast(F32)[:], ALU.subtract).then_inc(wlo_ready, 1)

            def columns_low(k):
                pool.wait_ge(xhi_ready, k + 1)
                at = slice(k * P, (k + 1) * P)
                nc.gpsimd.tensor_tensor(xT_lo[:, :, at], xf[k % 2][:], xT_hi.bitcast(F32)[:, :, at],
                                        ALU.subtract).then_inc(xlo_ready, 1)

            self_normalise(0, 0)
            with pool.Fori(0, NT // 2 - 1) as i:
                for par in range(2):
                    self_normalise(2 * i + 1 + par, 1 - par)
                    add_up(2 * i + par)
            low_part(gate)
            self_normalise(NT - 1, 1)
            add_up(NT - 2)
            low_part(up)
            for k in range(2):
                columns_low(k)
            low_part(down)
            for k in range(2, 4):
                columns_low(k)
            add_up(NT - 1)

            def hidden_low(j):
                half, ic = divmod(j, HC)
                at = slice(half * HALF, (half + 1) * HALF)
                pool.wait_ge(hhi_ready, j + 1)
                nc.gpsimd.tensor_tensor(hm_lo[:, ic, at], hm[j % 2][:], hm_hi.bitcast(F32)[:, ic, at],
                                        ALU.subtract).then_inc(hlo_ready, 1)

            def scatter(tiles):
                for k in tiles:
                    for i in range(2):
                        nc.gpsimd.indirect_dma_start(x_slots, bass.IndirectOffsetOnAxis(slots[:, k, i:i + 1], 0), xx[:, k, :],
                                                     None).then_inc(scattered, 16)

            hidden_low(0)
            columns_low(4)
            columns_low(5)
            hidden_low(1)
            columns_low(6)
            columns_low(7)
            for j in range(2, NJ - 3):
                hidden_low(j)
            pool.wait_ge(slots_zeroed, 16)
            pool.wait_ge(slots_ready, 1)
            for j in range(NJ - 3, NJ):
                scatter(range(2 * (j - NJ + 3), 2 * (j - NJ + 3) + 2))
                hidden_low(j)
            scatter(range(6, NT))
            for i in range(2):
                pool.wait_ge(y_stored[i], 16 * (TILES // 2))
            for k in range(NT):
                for i in range(2):
                    nc.gpsimd.indirect_dma_start(picked[2 * k + i][:], None, y_slots,
                                                 bass.IndirectOffsetOnAxis(slots[:, k, i:i + 1], 0)).then_inc(picked_loaded[k], 16)

        def ring_out(copy, blk, g, g_keys, sem_done):
            if g >= g_keys and g < g_keys + T_FILLS:
                b, j = divmod(g - g_keys, JT)
                n = P if j < JM else TAIL
                src = bank[4 + g % RING][:].rearrange("p (c s) -> p c s", c=HC)[:, :, 0:n]
                copy(ctxT[b][:, :, j * P:j * P + n], src).then_inc(sem_done, 1)

        def prob_out(copy, g, f, sem_done):
            j0, j1 = 4 * f, min(4 * f + 4, JT)
            n = P if j1 <= JM else TAIL
            src = bank[4 + g % RING][0:n, 0:(j1 - j0) * P]
            copy(probT[0:n, j0:j1, :].rearrange("p j q -> p (j q)"), src).then_inc(sem_done, 1)

        @block.scalar
        def _(act):
            def keys_out(blk, g, g_keys):
                act.wait_ge(ring_full, BLOCK * blk + g - 3)
                ring_out(nc.scalar.copy, blk, g, g_keys, evac_act)

            def exps(n):
                s0, w = S_CHUNKS[n]
                nc.scalar.activation(prob[:, s0:s0 + w], bank[n][:, 0:w], ACT.Exp, bias=nmax[:, 0:1],
                                     accum_out=sums[:, n:n + 1]).then_inc(prob_ready, 1)

            def probs_out(blk, g0):
                for f in range(P_FILLS):
                    if (g0 + f) % 2 == 0:
                        act.wait_ge(ring_full, BLOCK * blk + g0 + f - 3)
                        prob_out(nc.scalar.copy, g0 + f, f, evac_act)

            def step(k):
                mine = list(range(0, T_FILLS, 2))
                keys_out(k + 1, mine[0], 0)
                act.wait_ge(nmax_ready, k + 1)
                for n in range(4):
                    exps(n)
                    keys_out(k + 1, mine[n + 1], 0)
                for g in mine[5:]:
                    keys_out(k + 1, g, 0)
                probs_out(k + 1, T_FILLS)

            for g in range(BLOCK - T_FILLS, BLOCK, 2):
                keys_out(0, g, BLOCK - T_FILLS)
            step(0)
            with act.Fori(0, NT // 2 - 1) as i:
                step(2 * i + 1)
                step(2 * i + 2)

            def weight_high(hi, raw, loaded):
                act.wait_ge(loaded, 16)
                n = raw.shape[1] // HC
                for c in range(HC):
                    nc.scalar.copy(hi[:, n * c:n * (c + 1), :], raw[:, n * c:n * (c + 1), :]).then_inc(whi_ready, 1)

            def norm_out(k):
                act.wait_ge(hT_full, k + 1)
                if k >= 2:
                    act.wait_ge(hlo_done, k - 1)
                for c in range(HC):
                    last = nc.scalar.activation(hf[k % 2][:, c].rearrange("p g (i b) -> p g i b", b=GB),
                                                bank[k % 4][:, c * P:(c + 1) * P].rearrange("p (i g b) -> p g i b", g=NG, b=GB),
                                                ACT.Identity, bias=vec[:, V_BETA + c:V_BETA + c + 1],
                                                scale=vec[:, V_GAMMA + c:V_GAMMA + c + 1])
                last.then_inc(hf_act, 1)

            def norm_high(k):
                act.wait_ge(hf_dve if k % 2 else hf_act, k // 2 + 1)
                nc.scalar.copy(h_hi[:, :, :, 2 * GB * k:2 * GB * (k + 1)], hf[k % 2][:]).then_inc(hhi_done, 1)

            def keys_half_out(m):
                half, n = divmod(m, NH)
                act.wait_ge(kT_full, m + 1)
                nc.scalar.copy(kT[:, n, :, half * BATCH:(half + 1) * BATCH],
                               bank[4 + m % 4][:].rearrange("p (g t) -> p g t", g=NG)).then_inc(kT_act, 1)

            weight_high(wq_hi, wq_raw, w_loaded["wq"])
            act.wait_ge(nmax_ready, NT)
            for n in range(4):
                exps(n)
            probs_out(NT, 0)
            act.wait_ge(cst_loaded, 32)
            for k in range(0, NT - 2, 2):
                norm_out(k)
                norm_high(k)
                norm_high(k + 1)
            norm_out(NT - 2)
            norm_high(NT - 2)
            keys_half_out(0)
            keys_half_out(2)
            norm_high(NT - 1)
            keys_half_out(4)
            keys_half_out(6)
            act.wait_ge(rT_full, 1)
            weight_high(wv_hi, wv_raw, w_loaded["wv"])
            for m in range(NH, 2 * NH, 2):
                keys_half_out(m)

            def group_high(g, par):
                nc.scalar.copy(hg_hi[par][:], h_hi[:, :, ds(g, 1), :].rearrange("p c a t -> p (c a) t")).then_inc(hg_act, 1)

            def values_out(g, par):
                for h in range(2):
                    act.wait_ge(v_full, 2 * g + h + 1)
                    nc.scalar.copy(v_g[par][:, h * 512:(h + 1) * 512], bank[2 + h][:]).then_inc(v_out, 1)

            def group_exps(g, par):
                act.wait_ge(abias_ready, g + 1)
                for n in range(NH):
                    last = nc.scalar.activation(att[par][:, n, :], att[par][:, n, :], ACT.Exp, bias=a_bias[par][:, n:n + 1],
                                                scale=ATT_SCALE, accum_out=a_sum[par][:, n:n + 1])
                last.then_inc(exp_ready, 1)

            def weightsT_out(g):
                act.wait_ge(attT_full, 2 * g + 1)
                nc.scalar.copy(attT[:, 0:4, :].rearrange("p n q -> p (n q)"), bank[4][:]).then_inc(attT_act, 1)

            def group_out(g):
                act.wait_ge(o_full, 2 * g + 1)
                nc.scalar.copy(oT[:, 0:4, ds(g, 1), :].rearrange("p n a q -> p (n a) q"),
                               bank[6][:].rearrange("p (n q) -> p n q", n=4)).then_inc(o_act, 1)

            act.wait_ge(kT_act, NH)
            act.wait_ge(kT_dve, NH)
            for g in range(1, NG, 2):
                if g >= 4:
                    act.wait_ge(pos_full, g - 3)
                for n in range(NH):
                    last = nc.scalar.activation(kv_g[g % 4][:, n, :], kT[:, n, g, :], ACT.Identity,
                                                bias=vec[:, V_V + n:V_V + n + 1])
                last.then_inc(kv_act, 1)
            weight_high(wout_hi, wout_raw, w_loaded["wout"])
            act.wait_ge(pos_full, NG)
            act.wait_ge(hlo_done, NT)
            group_high(0, 0)
            group_high(1, 1)
            for g in range(2):
                values_out(g, g)
            group_high(2, 0)
            for g in range(2):
                group_exps(g, g)

            def group_step(g, par):
                weightsT_out(g)
                group_out(g)
                group_exps(g + 2, par)
                values_out(g + 2, par)

            group_step(0, 0)
            with act.Fori(0, NG // 2 - 2) as i:
                for par in (1, 0):
                    g = 2 * i + 2 - par
                    group_high(g + 2, par)
                    group_step(g, par)
            group_high(NG - 1, 1)
            group_step(NG - 3, 1)
            for g in (NG - 2, NG - 1):
                weightsT_out(g)
                group_out(g)

            def out_high(k, par):
                for i in range(2):
                    last = nc.scalar.copy(
                        o_hi[par][:, :, i * BATCH:(i + 1) * BATCH].rearrange("p n (g b) -> p n g b", b=GB),
                        oT[:, :, :, ds(2 * GB * k + i * GB, GB)])
                last.then_inc(ohi_ready, 1)

            act.wait_ge(o_dve, NG)
            act.wait_ge(o_act, NG)
            out_high(0, 0)
            out_high(1, 1)
            with act.Fori(0, NT // 2 - 1) as i:
                for par in range(2):
                    act.wait_ge(y2_full, 2 * i + par + 1)
                    out_high(2 * i + par + 2, par)

            def heads_out(k, par):
                act.wait_ge(k_full, k + 1)
                kr = bank[2][:].rearrange("p (a h d) -> p a h d", a=2, d=RD)
                if not (isinstance(k, int) and k == 0):
                    act.wait_ge(kq_ready, k)
                nc.scalar.copy(raw[:, 0:HEADS, :], kr[:, 0])
                nc.scalar.copy(kq[par][:, 0:HEADS, 0:RD], kr[:, 1])
                act.wait_ge(q_full, k + 1)
                qr = bank[1][:].rearrange("p (a h d) -> p a h d", a=2, d=RD)
                nc.scalar.copy(kq[par][:, HEADS:, 0:RD], qr[:, 0])
                nc.scalar.copy(raw[:, HEADS:, :], qr[:, 1]).then_inc(raw_ready, 1)
                act.wait_ge(vv_full, k + 1)
                nc.scalar.copy(v_t[par][:], bank[3][:]).then_inc(vv_ready, 1)

            def keys_spread(k, par):
                act.wait_ge(kTh_full, k + 1)
                for h in range(4):
                    rows_h = slice(HD * h, HD * (h + 1))
                    last = nc.scalar.copy(kT_h[par][rows_h, :, h, :], bank[3][rows_h, :].rearrange("p (c q) -> p c q", c=QUADS))
                last.then_inc(kTh_ready, 1)

            def self_exps(k, par, quads):
                for c in quads:
                    act.wait_ge(sbias_ready, 4 * k + c + 1)
                    for n in range(4):
                        h = 4 * c + n
                        last = nc.scalar.activation(sp_[par][:, h, :], bank[4 + c % 2][:, n * P:(n + 1) * P], ACT.Exp,
                                                    bias=s_bias[par][:, h:h + 1], scale=SELF_SCALE,
                                                    accum_out=s_sum[par][:, h:h + 1])
                    last.then_inc(sexp_ready, 1)

            def weights_out(k, c):
                act.wait_ge(spT_full, 4 * k + c + 1)
                nc.scalar.copy(spT[:, 4 * c:4 * c + 4, :].rearrange("p n q -> p (n q)"), bank[6][:]).then_inc(spT_act, 1)

            def self_step(k, par, scores=True, project=True):
                weights_out(k, 0)
                if scores:
                    keys_spread(k + 1, 1 - par)
                weights_out(k, 2)
                if scores:
                    self_exps(k + 1, 1 - par, (0, 1))
                if project:
                    heads_out(k + 2, par)
                if scores:
                    self_exps(k + 1, 1 - par, (2, 3))

            gate, up, down = range(3)

            def high_part(m):
                act.wait_ge(raw_loaded, 3 * 16)
                nc.scalar.copy(w_hi[m][:], w_raw[m][:]).then_inc(whi_ready, 1)

            def columns_high(k):
                act.wait_ge(xf_ready, k + 1)
                nc.scalar.copy(xT_hi[:, :, k * P:(k + 1) * P], xf[k % 2][:]).then_inc(xhi_ready, 1)

            act.wait_ge(cleared, 2)
            heads_out(0, 0)
            keys_spread(0, 0)
            self_exps(0, 0, (0, 1))
            heads_out(1, 1)
            self_exps(0, 0, (2, 3))
            self_step(0, 0)
            with act.Fori(0, NT // 2 - 2) as i:
                self_step(2 * i + 1, 1)
                self_step(2 * i + 2, 0)
            high_part(gate)
            self_step(NT - 3, 1)
            high_part(up)
            self_step(NT - 2, 0, project=False)
            high_part(down)
            columns_high(0)
            columns_high(1)
            self_step(NT - 1, 1, scores=False, project=False)
            columns_high(2)
            columns_high(3)

            for j in range(NJ):
                half, ic = divmod(j, HC)
                act.wait_ge(gu_full, j + 1)
                nc.scalar.activation(act_g[j % 2][:], bank[4 + j % 2][:], ACT.Silu).then_inc(silu_ready, 1)
                act.wait_ge(hm_ready, j + 1)
                nc.scalar.copy(hm_hi[:, ic, half * HALF:(half + 1) * HALF], hm[j % 2][:]).then_inc(hhi_ready, 1)
                if j < 2:
                    columns_high(4 + 2 * j)
                    columns_high(5 + 2 * j)
                elif j == 2:
                    act.wait_ge(logit_ready, 1)
                    nc.scalar.activation(r_p[:, :, 0:NR], r_p[:, :, 0:NR], ACT.Exp, scale=-1.0).then_inc(gate_ready, 1)

            def load_rows(t, par):
                nc.scalar.dma_start(xg[par][:], x_slots[ds(t * P, P), :]).then_inc(xg_loaded[par], 16)

            def routed_silu(t):
                act.wait_ge(rgate_full, t + 1)
                nc.scalar.activation(rhm[:], bank[1][:], ACT.Silu).then_inc(rsilu_ready, 1)

            def hidden_columns_out(t):
                act.wait_ge(rhmT_full, t + 1)
                nc.scalar.copy(rhmT[:].rearrange("p c q -> p (c q)"), bank[3][:]).then_inc(rhmT_ready, 1)

            def output_rows(t, par, turn):
                act.wait_ge(rdown_full, t + 1)
                if not (isinstance(turn, int) and turn == 0):
                    act.wait_ge(y_stored[par], 16 * turn)
                nc.scalar.copy(yo[par][:], bank[4 + par][:]).then_inc(yo_ready, 1)
                act.wait_ge(yo_ready, t + 1)
                nc.scalar.dma_start(y_slots[ds(t * P, P), :], yo[par][:]).then_inc(y_stored[par], 16)

            act.wait_ge(scattered, 16 * 2 * NT)
            load_rows(0, 0)
            load_rows(1, 1)
            act.wait_ge(xgT_full, 1)
            load_rows(2, 0)
            routed_silu(0)
            hidden_columns_out(0)
            act.wait_ge(xgT_full, 2)
            load_rows(3, 1)
            routed_silu(1)
            output_rows(0, 0, 0)
            hidden_columns_out(1)

            def routed_step(t, par, turn, load=True):
                if load:
                    act.wait_ge(xgT_full, t + 1)
                    load_rows(t + 2, par)
                routed_silu(t)
                output_rows(t - 1, 1 - par, turn)
                hidden_columns_out(t)

            routed_step(2, 0, 0)
            routed_step(3, 1, 1)
            with act.Fori(0, TILES // 2 - 3) as i:
                routed_step(2 * i + 4, 0, i + 1)
                routed_step(2 * i + 5, 1, i + 2)
            routed_step(TILES - 2, 0, TILES // 2 - 2, load=False)
            routed_step(TILES - 1, 1, TILES // 2 - 1, load=False)
            output_rows(TILES - 1, 1, TILES // 2 - 1)

        @block.vector
        def _(dve):
            chain = Steps(dve, dve_step)

            def moments(m, st, t0, t1):
                for k in range(t0, t1):
                    chain.mark(dve.bn_aggr(m[:, k, :], st[:, k, :]))
                chain.wait()

            def row_stats(t):
                for k in range(NT):
                    chain.mark(dve.bn_stats(stats[:, k, :], t[:, k, :]))
                chain.wait()
                moments(mv, stats, 0, NT)

            def rsqrt(dst, v, at=slice(0, NT)):
                half, t = rs_h[:, at], rs_t[:, at]
                chain(dve.tensor_scalar(half, v, -0.5, None, ALU.mult))
                chain(dve.tensor_scalar(t.bitcast(I32), v.bitcast(I32), 1, None, ALU.arith_shift_right))
                chain(dve.tensor_scalar(dst.bitcast(I32), t.bitcast(I32), -1.0, float(0x5F3759DF), ALU.mult, ALU.add))
                for _ in range(3):
                    chain(dve.tensor_tensor(t, dst, dst, ALU.mult))
                    chain(dve.tensor_tensor(t, t, half, ALU.mult))
                    chain(dve.scalar_tensor_tensor(dst, t, 1.5, dst, ALU.add, ALU.mult))

            def queries(k):
                dve.tensor_scalar(qn[:], row(y, k), mean[:, ds(k, 1)], rstd[:, ds(k, 1)], ALU.subtract,
                                  ALU.mult).then_inc(qn_ready, 1)

            def queries_out(k):
                dve.wait_ge(qT_full, k + 1)
                dve.tensor_copy(qT[:].rearrange("p c q -> p (c q)"), bank[7][:]).then_inc(qT_ready, 1)

            def maxima(k):
                for n, (s0, w) in enumerate(S_CHUNKS):
                    dve.wait_ge(scores_full, 4 * k + n + 1)
                    chain.mark(dve.tensor_reduce(mx[:, n:n + 1], bank[n][:, 0:w], AX, ALU.max))
                chain.wait()
                dve.tensor_reduce(nmax[:], mx[:], AX, ALU.max, negate=True).then_inc(nmax_ready, 1)

            def keys_out(blk, g, g_keys):
                dve.wait_ge(ring_full, BLOCK * blk + g - 3)
                ring_out(dve.tensor_copy, blk, g, g_keys, evac_dve)

            def probs_out(k, blk, g0):
                dve.wait_ge(prob_ready, 4 * k + 4)
                chain(dve.tensor_reduce(total[:], sums[:], AX, ALU.add))
                chain(dve.reciprocal(rinv[:], total[:]))
                for f in range(P_FILLS):
                    if (g0 + f) % 2 == 1:
                        dve.wait_ge(ring_full, BLOCK * blk + g0 + f - 3)
                        prob_out(dve.tensor_copy, g0 + f, f, evac_dve)

            def finish(k):
                dve.wait_ge(context_full, k + 1)
                dve.scalar_tensor_tensor(row(y, k), bank[7][:], rinv[:, 0:1], row(y, k), ALU.mult,
                                         ALU.add).then_inc(y1_ready, 1)
                dve.wait_ge(y1_ready, k + 1)
                chain.mark(dve.bn_stats(row(stats2, k), row(y, k)))

            def step(k):
                queries(k + 1)
                maxima(k)
                queries_out(k + 1)
                for g in range(1, T_FILLS, 2):
                    keys_out(k + 1, g, 0)
                probs_out(k, k + 1, T_FILLS)
                finish(k)

            dve.wait_ge(x_loaded, 16)
            row_stats(y)
            chain(dve.tensor_scalar(rs_v[:], var, LN_EPS, None, ALU.add))
            rsqrt(rstd[:], rs_v[:])
            queries(0)
            queries_out(0)
            for g in range(BLOCK - T_FILLS + 1, BLOCK, 2):
                keys_out(0, g, BLOCK - T_FILLS)
            step(0)
            chain.enter()
            with dve.Fori(0, NT // 2 - 1) as i:
                chain.turn(i, 14)
                step(2 * i + 1)
                step(2 * i + 2)
            chain.leave(NT // 2 - 1)

            def double_norm(t0, t1):
                at = slice(t0, t1)
                chain.wait()
                moments(mv2, stats2, t0, t1)
                chain(dve.tensor_scalar(rs_v[:, at], mv2[:, at, 1], 1 + LN_EPS, LN_EPS ** 2, ALU.mult, ALU.add))
                rsqrt(rstd2[:, at], rs_v[:, at], at)

            def norm(k):
                if k >= 4:
                    dve.wait_ge(hT_full, k - 3)
                dve.tensor_scalar(hn[k % 4][:], y[:, k, :], mv2[:, k, 0:1], rstd2[:, k:k + 1], ALU.subtract,
                                  ALU.mult).then_inc(hn_ready, 1)

            def norm_out(k):
                dve.wait_ge(hT_full, k + 1)
                if k >= 2:
                    dve.wait_ge(hlo_done, k - 1)
                for c in range(HC):
                    last = dve.tensor_scalar(hf[k % 2][:, c].rearrange("p g (i b) -> p g i b", b=GB),
                                             bank[k % 4][:, c * P:(c + 1) * P].rearrange("p (i g b) -> p g i b", g=NG, b=GB),
                                             vec[:, V_GAMMA + c:V_GAMMA + c + 1], vec[:, V_BETA + c:V_BETA + c + 1],
                                             ALU.mult, ALU.add)
                last.then_inc(hf_dve, 1)

            def keys_half_out(m):
                half, n = divmod(m, NH)
                dve.wait_ge(kT_full, m + 1)
                dve.tensor_copy(kT[:, n, :, half * BATCH:(half + 1) * BATCH],
                                bank[4 + m % 4][:].rearrange("p (g t) -> p g t", g=NG)).then_inc(kT_dve, 1)

            dve.wait_ge(cst_loaded, 32)
            double_norm(0, NT - 1)
            for k in range(4):
                norm(k)
            dve.tensor_copy(ident_bf[:], ident).then_inc(consts_cast, 1)
            dve.tensor_copy(block_bf[:], cst[:, C_BLOCK:C_BLOCK + P].unsqueeze(1).broadcast_to([P, 4, P])).then_inc(consts_cast, 1)
            maxima(NT - 1)
            probs_out(NT - 1, NT, 0)
            norm_out(1)
            norm(4)
            norm(5)
            norm_out(3)
            norm(6)
            finish(NT - 1)
            norm_out(5)
            double_norm(NT - 1, NT)
            norm(NT - 1)
            keys_half_out(1)
            norm_out(7)
            keys_half_out(3)
            dve.wait_ge(rT_full, 1)
            dve.tensor_copy(rT_sb[:], bank[2][:, 0:NH * SEQ]).then_inc(rT_ready, 1)
            dve.memset(pos_sb[:, :, 0:NH], 0.0)
            for m in range(5, 2 * NH, 2):
                keys_half_out(m)

            def pos_queries(g):
                if g >= 4:
                    dve.wait_ge(pos_full, g - 3)
                dve.tensor_tensor(kv_g[g % 4][:], kT[:, :, g, :], vec[:, V_V:V_V + NH].unsqueeze(2).broadcast_to([P, NH, P]),
                                  ALU.add).then_inc(kv_dve, 1)

            def positions_out(g):
                dve.wait_ge(pos_full, g + 1)
                dve.tensor_tensor(pos_sb[:, g, NH:PADDED * NH].rearrange("p (j n) -> p n j", n=NH),
                                  bank[g % 4][:, 0:NH * SEQ].rearrange("p (n j) -> p n j", n=NH),
                                  cst[:, C_TRIL + NH * g:C_TRIL + NH * (g + 1)].unsqueeze(2).broadcast_to([P, NH, SEQ]),
                                  ALU.mult).then_inc(pos_out, 1)

            dve.wait_ge(kT_act, NH)
            dve.wait_ge(kT_dve, NH)
            pos_queries(0)
            pos_queries(2)
            for g in range(0, NG, 2):
                positions_out(g)
                if g + 4 < NG:
                    pos_queries(g + 4)
                positions_out(g + 1)

            def group_low(g, par):
                dve.tensor_copy(hg_lo[par][:], h_lo[:, :, ds(g, 1), :].rearrange("p c a t -> p (c a) t")).then_inc(hg_dve, 1)

            def group_max(g, par):
                for h in range(2):
                    dve.wait_ge(con_full, 2 * g + h + 1)
                    pos = pos_g[:, ds(g, 1), :].rearrange("p a (j n) -> p n (a j)", n=NH)[:, 4 * h:4 * h + 4, :].unsqueeze(3)
                    dve.tensor_tensor(att[par][:, 4 * h:4 * h + 4, :].rearrange("p n (j b) -> p n j b", b=GB),
                                      bank[h][:].rearrange("p (n j b) -> p n j b", n=4, b=GB),
                                      pos.broadcast_to([P, 4, SEQ, GB]), ALU.add).then_inc(con_out, 1)
                dve.wait_ge(con_out, 2 * g + 2)
                chain(dve.tensor_reduce(a_max[par][:], att[par][:], AX, ALU.max, negate=True))
                dve.tensor_scalar(a_bias[par][:], a_max[par][:], ATT_SCALE, None, ALU.mult).then_inc(abias_ready, 1)

            def group_inv(g, par):
                dve.wait_ge(exp_ready, g + 1)
                dve.reciprocal(a_inv[par][:], a_sum[par][:]).then_inc(ainv_ready, 1)

            def weightsT_out(g):
                dve.wait_ge(attT_full, 2 * g + 2)
                dve.tensor_copy(attT[:, 4:8, :].rearrange("p n q -> p (n q)"), bank[5][:]).then_inc(attT_dve, 1)

            def group_out(g):
                dve.wait_ge(o_full, 2 * g + 2)
                dve.tensor_copy(oT[:, 4:8, ds(g, 1), :].rearrange("p n a q -> p (n a) q"),
                                bank[7][:].rearrange("p (n q) -> p n q", n=4)).then_inc(o_dve, 1)

            def group_step(g, par):
                weightsT_out(g)
                group_max(g + 2, par)
                group_inv(g + 1, 1 - par)
                group_out(g)

            group_low(0, 0)
            group_low(1, 1)
            dve.wait_ge(pos_loaded[0], 16 * SEQ)
            group_max(0, 0)
            dve.wait_ge(v_full, 2)
            group_low(2, 0)
            group_max(1, 1)
            group_inv(0, 0)
            dve.wait_ge(pos_loaded[1], 16 * SEQ)
            group_step(0, 0)
            chain.enter()
            with dve.Fori(0, NG // 2 - 2) as i:
                chain.turn(i, 2)
                for par in (1, 0):
                    g = 2 * i + 2 - par
                    dve.wait_ge(v_full, 2 * g + 2)
                    group_low(g + 2, par)
                    group_step(g, par)
            chain.leave(NG // 2 - 2)
            dve.wait_ge(v_full, 2 * (NG - 3) + 2)
            group_low(NG - 1, 1)
            group_step(NG - 3, 1)
            weightsT_out(NG - 2)
            group_inv(NG - 1, 1)
            group_out(NG - 2)
            weightsT_out(NG - 1)
            group_out(NG - 1)

            def out_low(k, par):
                dve.wait_ge(ohi_ready, k + 1)
                for i in range(2):
                    at = slice(i * BATCH, (i + 1) * BATCH)
                    last = dve.tensor_tensor(o_lo[par][:, :, at].rearrange("p n (g b) -> p n g b", b=GB),
                                             oT[:, :, :, ds(2 * GB * k + i * GB, GB)],
                                             o_hi[par].bitcast(F32)[:, :, at].rearrange("p n (g b) -> p n g b", b=GB),
                                             ALU.subtract)
                last.then_inc(olo_ready, 1)

            def out_added(k, par):
                dve.wait_ge(y2_full, k + 1)
                dve.tensor_tensor(row(y, k), bank[6 + par][:], row(y, k), ALU.add).then_inc(y2_ready, 1)
                dve.wait_ge(y2_ready, k + 1)
                chain.mark(dve.bn_stats(row(stats, k), row(y, k)))

            dve.wait_ge(o_act, NG)
            dve.wait_ge(o_dve, NG)
            out_low(0, 0)
            out_low(1, 1)
            dve.tensor_copy(causal_bf[:], cst[:, C_CAUSAL:C_CAUSAL + P].unsqueeze(1).broadcast_to([P, 4, P])).then_inc(causal_ready, 1)
            dve.wait_ge(bout_added, 1)
            chain.enter()
            with dve.Fori(0, NT // 2 - 1) as i:
                chain.turn(i, 2)
                for par in range(2):
                    out_added(2 * i + par, par)
                    out_low(2 * i + par + 2, par)
            chain.leave(NT // 2 - 1)

            def rms_inverse(dst, at=slice(0, NT)):
                chain(dve.tensor_scalar(rs_v[:, at], rs_v[:, at], 1e-30, None, ALU.max))
                rsqrt(rs_r[:, at], rs_v[:, at], at)
                chain(dve.tensor_tensor(rs_r[:, at], rs_r[:, at], rs_v[:, at], ALU.mult))
                chain(dve.tensor_scalar(rs_r[:, at], rs_r[:, at], RMS_EPS, None, ALU.add))
                chain(dve.reciprocal(dst[:, at], rs_r[:, at]))

            def self_factors(t0, t1):
                at = slice(t0, t1)
                chain.wait()
                moments(mv, stats, t0, t1)
                chain(dve.tensor_scalar(rs_v[:, at], var[:, at], LN_EPS, None, ALU.add))
                rsqrt(rstd[:, at], rs_v[:, at], at)
                chain(dve.tensor_tensor(rs_v[:, at], rstd[:, at], rstd[:, at], ALU.mult))
                chain(dve.tensor_tensor(rs_v[:, at], rs_v[:, at], var[:, at], ALU.mult))
                rms_inverse(rms_x, at)
                chain(dve.tensor_tensor(rms_x[:, at], rms_x[:, at], rstd[:, at], ALU.mult))

            def self_norm(k, par):
                if not isinstance(k, int) or k >= 2:
                    dve.wait_ge(xnT_full, k - 1)
                dve.tensor_scalar(xn[par][:], row(y, k), mean[:, ds(k, 1)], rms_x[:, ds(k, 1)], ALU.subtract,
                                  ALU.mult).then_inc(xn_ready, 1)
                chain.mark(dve.tensor_scalar(row(xx, k), row(y, k), mean[:, ds(k, 1)], rstd[:, ds(k, 1)], ALU.subtract,
                                             ALU.mult))

            def norm_columns_out(k, par):
                dve.wait_ge(xnT_full, k + 1)
                for c in range(HC):
                    last = dve.tensor_scalar(xnT[par][:, c, :], bank[0][:, c * P:(c + 1) * P], vec[:, V_W1 + c:V_W1 + c + 1],
                                             None, ALU.mult)
                last.then_inc(xnT_ready, 1)

            def latents_out(k, par):
                dve.wait_ge(lat_full, k + 1)
                dve.tensor_copy(latT[par][:].rearrange("l a t -> l (a t)"), bank[1][:, 0:2 * P]).then_inc(lat_ready, 1)

            def rotate(k, par):
                dve.wait_ge(raw_ready, k + 1)
                cos = cst[:, C_COS:C_COS + RD].unsqueeze(1).broadcast_to([P, 2 * HEADS, RD])
                sin = cst[:, C_SIN:C_SIN + RD].unsqueeze(1).broadcast_to([P, 2 * HEADS, RD])
                half = RD // 2
                chain.mark(dve.tensor_tensor(kq[par][:, :, RD:HD], raw[:], cos, ALU.mult))
                chain.mark(dve.tensor_tensor(turned[:, :, 0:half], raw[:, :, half:RD], sin[:, :, 0:half], ALU.mult))
                chain(dve.tensor_tensor(turned[:, :, half:RD], raw[:, :, 0:half], sin[:, :, half:RD], ALU.mult))
                dve.tensor_tensor(kq[par][:, :, RD:HD], kq[par][:, :, RD:HD], turned[:], ALU.add).then_inc(kq_ready, 1)

            def queries_columns_out(k, par):
                dve.wait_ge(qTh_full, k + 1)
                dve.tensor_copy(qT_h[par][:].rearrange("p c q -> p (c q)"), bank[3][:]).then_inc(qTh_ready, 1)

            def self_max(k, par, quads):
                for c in quads:
                    dve.wait_ge(self_full, 4 * k + c + 1)
                    at = slice(4 * c, 4 * c + 4)
                    chain(dve.tensor_reduce(s_max[par][:, at], bank[4 + c % 2][:].rearrange("p (n q) -> p n q", n=4), AX,
                                            ALU.max, negate=True))
                    dve.tensor_scalar(s_bias[par][:, at], s_max[par][:, at], SELF_SCALE, None, ALU.mult).then_inc(sbias_ready, 1)

            def self_inv(k, par, quads):
                for c in quads:
                    dve.wait_ge(sexp_ready, 4 * k + c + 1)
                    dve.reciprocal(s_inv[par][:, 4 * c:4 * c + 4], s_sum[par][:, 4 * c:4 * c + 4]).then_inc(sinv_ready, 1)

            def weights_columns_out(k, c):
                dve.wait_ge(spT_full, 4 * k + c + 1)
                dve.tensor_copy(spT[:, 4 * c:4 * c + 4, :].rearrange("p n q -> p (n q)"), bank[7][:]).then_inc(spT_dve, 1)

            def self_output_out(k):
                dve.wait_ge(yT_full, k + 1)
                dve.tensor_copy(yT[:].rearrange("p c q -> p (c q)"), bank[0][:]).then_inc(yT_ready, 1)

            def output_added(k):
                dve.wait_ge(wo_full, k + 1)
                dve.tensor_tensor(row(xx, k), bank[6][:], row(xx, k), ALU.add).then_inc(xx_ready, 1)

            def self_step(k, par, norm=True, scores=True, project=True):
                if project:
                    norm_columns_out(k + 2, par)
                if scores:
                    queries_columns_out(k + 1, 1 - par)
                weights_columns_out(k, 1)
                if project:
                    latents_out(k + 2, par)
                weights_columns_out(k, 3)
                if scores:
                    self_max(k + 1, 1 - par, (0, 1))
                self_output_out(k)
                if norm:
                    self_norm(k + 3, 1 - par)
                if scores:
                    self_inv(k + 1, 1 - par, (0, 1))
                    self_max(k + 1, 1 - par, (2, 3))
                if project:
                    rotate(k + 2, par)
                if scores:
                    self_inv(k + 1, 1 - par, (2, 3))
                output_added(k)

            def expert_norm(t0, t1):
                at = slice(t0, t1)
                dve.wait_ge(xx_ready, t1)
                for k in range(t0, t1):
                    chain.mark(dve.bn_stats(stats[:, k, :], xx[:, k, :]))
                chain.wait()
                moments(mv, stats, t0, t1)
                chain(dve.tensor_tensor(rs_v[:, at], mean[:, at], mean[:, at], ALU.mult))
                chain(dve.tensor_tensor(rs_v[:, at], rs_v[:, at], var[:, at], ALU.add))
                rms_inverse(rms_f, at)
                dve.wait_ge(y_summed, t1)
                for k in range(t0, t1):
                    dve.tensor_scalar(xx[:, k, :], xx[:, k, :], rms_f[:, k:k + 1], None, ALU.mult).then_inc(xn2_ready, 1)

            def expert_columns_out(k):
                dve.wait_ge(xfT_full, k + 1)
                if k >= 2:
                    dve.wait_ge(logit_full, k - 1)
                    dve.wait_ge(xlo_ready, k - 1)
                for c in range(HC):
                    last = dve.tensor_scalar(xf[k % 2][:, c, :], bank[1 + k % 2][:, c * P:(c + 1) * P],
                                             vec[:, V_W2 + c:V_W2 + c + 1], None, ALU.mult)
                last.then_inc(xf_ready, 1)

            self_factors(0, NT - 2)
            self_norm(0, 0)
            self_norm(1, 1)
            out_added(NT - 2, 0)
            out_added(NT - 1, 1)
            norm_columns_out(0, 0)
            latents_out(0, 0)
            norm_columns_out(1, 1)
            rotate(0, 0)
            latents_out(1, 1)
            queries_columns_out(0, 0)
            self_norm(2, 0)
            self_max(0, 0, (0, 1))
            self_inv(0, 0, (0, 1))
            self_max(0, 0, (2, 3))
            rotate(1, 1)
            self_inv(0, 0, (2, 3))
            self_factors(NT - 2, NT)
            self_step(0, 0)
            chain.enter()
            with dve.Fori(0, NT // 2 - 2) as i:
                chain.turn(i, 16)
                self_step(2 * i + 1, 1)
                self_step(2 * i + 2, 0)
            chain.leave(NT // 2 - 2)
            self_step(NT - 3, 1, norm=False)
            expert_norm(0, NT // 2)
            self_step(NT - 2, 0, norm=False, project=False)
            for k in range(NT // 2):
                expert_columns_out(k)
            self_step(NT - 1, 1, norm=False, scores=False, project=False)

            def logits_out():
                dve.wait_ge(logit_full, NT)
                dve.tensor_tensor(r_p[:, :, 0:NR], bank[3][:, 0:NT * NE].rearrange("p (k e) -> p k e", e=NE)[:, :, 0:NR],
                                  rbias_sb[:].unsqueeze(1).broadcast_to([P, NT, NR]), ALU.add).then_inc(logit_ready, 1)

            def per_expert(t):
                return t.unsqueeze(2).broadcast_to([P, NT, NE])

            def choose():
                dve.wait_ge(gate_ready, 1)
                chain(dve.tensor_scalar(r_p[:, :, 0:NR], r_p[:, :, 0:NR], 1.0, None, ALU.add))
                chain.mark(dve.memset(r_p[:, :, NR:NE], -1.0))
                chain(dve.reciprocal(r_p[:, :, 0:NR], r_p[:, :, 0:NR]))
                rank = cst[:, C_RANK:C_RANK + NE].unsqueeze(1).broadcast_to([P, NT, NE])
                for i in range(2):
                    chain(dve.tensor_reduce(gates[i][:], r_p[:], AX, ALU.max))
                    chain(dve.tensor_tensor(r_eq[:], r_p[:], per_expert(gates[i][:]), ALU.is_equal))
                    chain(dve.tensor_tensor(r_eq[:], r_eq[:], rank, ALU.mult))
                    chain(dve.tensor_reduce(r_key[:], r_eq[:], AX, ALU.max))
                    chain(dve.tensor_tensor(r_sel[i][:], r_eq[:], per_expert(r_key[:]), ALU.is_equal))
                    if i == 0:
                        chain(dve.scalar_tensor_tensor(r_p[:], r_sel[0][:], -4.0, r_p[:], ALU.mult, ALU.add))
                dve.tensor_tensor(r_picks[:], r_sel[0][:], r_sel[1][:], ALU.add).then_inc(picks_ready, 1)

            def allot():
                dve.wait_ge(ranks_full, 1)
                pairs, tiles, first = (r_first[:, i, :] for i in range(3))
                ranks = bank[3][:, 0:NT * NE].rearrange("p (k e) -> p k e", e=NE)
                chain(dve.tensor_copy(pairs, bank[3][:, NT * NE:(NT + 1) * NE]))
                square = [P, NE, NE]
                chain(dve.tensor_tensor(r_fill[:], pairs.unsqueeze(2).broadcast_to(square),
                                        cst[:, C_FILL:C_FILL + NE].unsqueeze(1).broadcast_to(square), ALU.is_gt))
                chain(dve.tensor_reduce(tiles, r_fill[:], AX, ALU.add))
                chain(dve.tensor_tensor(r_fill[:], tiles.unsqueeze(1).broadcast_to(square),
                                        cst[:, C_EARLIER:C_EARLIER + NE * NE].rearrange("p (e f) -> p e f", e=NE), ALU.mult))
                chain(dve.tensor_reduce(first, r_fill[:], AX, ALU.add))
                chain(dve.scalar_tensor_tensor(r_p[:], first.unsqueeze(1).broadcast_to([P, NT, NE]), float(P), ranks, ALU.mult,
                                               ALU.add))
                for i in range(2):
                    chain(dve.tensor_tensor(r_eq[:], r_sel[i][:], r_p[:], ALU.mult))
                    chain(dve.tensor_reduce(r_slot[:, :, i], r_eq[:], AX, ALU.add))
                dve.tensor_copy(slots[:], r_slot[:]).then_inc(slots_ready, 1)
                table = [P, TILES, NE]
                for i, at in enumerate((C_PLACE, C_NEED)):
                    chain(dve.tensor_tensor(r_begun[:], cst[:, C_TILE:C_TILE + TILES].unsqueeze(2).broadcast_to(table),
                                            first.unsqueeze(1).broadcast_to(table), ALU.is_ge))
                    chain(dve.tensor_tensor(r_begun[:], r_begun[:], cst[:, at:at + NE].unsqueeze(1).broadcast_to(table), ALU.mult))
                    chain(dve.tensor_reduce(r_tile[:, i, :], r_begun[:], AX, ALU.add))
                dve.tensor_copy(tile_expert[:], r_tile[:]).then_inc(slots_ready, 1)
                chain(dve.tensor_tensor(r_key[:], gates[0][:], gates[1][:], ALU.add))
                chain(dve.reciprocal(r_key[:], r_key[:]))
                for i in range(2):
                    chain(dve.tensor_tensor(gates[i][:], gates[i][:], r_key[:], ALU.mult))

            expert_norm(NT // 2, NT)
            dve.tensor_copy(below_bf[:], cst[:, C_BELOW:C_BELOW + P]).then_inc(consts_cast, 1)
            dve.memset(ones_bf[:], 1.0).then_inc(consts_cast, 1)
            dve.wait_ge(slots_zeroed, 16)
            for j in range(NJ):
                dve.wait_ge(silu_ready, j + 1)
                if j >= 2:
                    dve.wait_ge(hlo_ready, j - 1)
                dve.tensor_tensor(hm[j % 2][:], act_g[j % 2][:], bank[6 + j % 2][:], ALU.mult).then_inc(hm_ready, 1)
                if j < 2:
                    expert_columns_out(4 + 2 * j)
                    expert_columns_out(5 + 2 * j)
                elif j == 2:
                    logits_out()
                    choose()
                elif j == 4:
                    allot()
            for k in range(NT):
                dve.wait_ge(down_full, k + 1)
                dve.tensor_tensor(y[:, k, :], bank[k % 3][:], y[:, k, :], ALU.add).then_inc(down_added, 1)

            def rows_columns_out(t, par):
                dve.wait_ge(xgT_full, t + 1)
                for c in range(HC):
                    last = dve.tensor_scalar(xgT[par][:, c, :], bank[0][:, c * P:(c + 1) * P], vec[:, V_W2 + c:V_W2 + c + 1],
                                             None, ALU.mult)
                last.then_inc(xgT_ready, 1)

            def routed_mult(t):
                dve.wait_ge(rup_full, t + 1)
                dve.wait_ge(rsilu_ready, t + 1)
                dve.tensor_tensor(rhm[:], rhm[:], bank[2][:], ALU.mult).then_inc(rhm_ready, 1)

            rows_columns_out(0, 0)
            routed_mult(0)
            rows_columns_out(1, 1)
            with dve.Fori(0, TILES // 2 - 1) as i:
                for par in range(2):
                    t = 2 * i + 1 + par
                    rows_columns_out(t + 1, par)
                    routed_mult(t)
            routed_mult(TILES - 1)
            for k in range(NT):
                dve.wait_ge(picked_loaded[k], 2 * 16)
                for i in range(2):
                    if i == 1:
                        dve.wait_ge(first_added, k + 1)
                    dve.scalar_tensor_tensor(y[:, k, :], picked[2 * k + i][:], gates[i][:, k:k + 1], y[:, k, :], ALU.mult,
                                             ALU.add).then_inc(first_added if i == 0 else y_ready, 1)


def kernel(x, ctx_1024, L0_attn_gamma, L0_attn_beta, L0_attn_Wq, L0_attn_Wv, L0_attn_Wr, L0_attn_u_bias, L0_attn_v_bias,
           L0_attn_Wout, L0_attn_bout, L0_ffn_w_ln1, L0_ffn_w_ln2, L0_ffn_W_kvd, L0_ffn_W_qd, L0_ffn_W_ku, L0_ffn_W_qu,
           L0_ffn_W_vu, L0_ffn_W_ropeq, L0_ffn_W_ropek, L0_ffn_W_o, L0_ffn_Wg_s, L0_ffn_Wu_s, L0_ffn_Wd_s, L0_ffn_Wg_r,
           L0_ffn_Wu_r, L0_ffn_Wd_r, L0_ffn_W_router, L0_ffn_routing_bias):
    import concourse.bacc as bacc
    from concourse.bass_utils import run_bass_kernel_spmd

    def columns(v):
        return np.asarray(v).reshape(-1, P).T

    arrays = {
        "x": np.asarray(x).reshape(TOK, D),
        "ctx_keys": np.asarray(ctx_1024),
        "consts": shape_constants(),
        "vecs": np.concatenate([columns(v) for v in (L0_attn_gamma, L0_attn_beta, L0_ffn_w_ln1, L0_ffn_w_ln2,
                                                     L0_attn_u_bias, L0_attn_v_bias)], axis=1),
        "rows": np.concatenate([np.asarray(L0_attn_bout), np.asarray(L0_ffn_routing_bias)])[None, :],
        "Wq": L0_attn_Wq, "Wv": L0_attn_Wv, "Wr": L0_attn_Wr, "Wout": L0_attn_Wout,
        "Wkvd": L0_ffn_W_kvd, "Wqd": L0_ffn_W_qd, "Wku": L0_ffn_W_ku, "Wqu": L0_ffn_W_qu, "Wvu": L0_ffn_W_vu,
        "Wropeq": L0_ffn_W_ropeq, "Wropek": L0_ffn_W_ropek, "Wo": L0_ffn_W_o,
        "Wexp": np.stack([np.concatenate([np.asarray(s)[None], np.asarray(r)]) for s, r in (
            (L0_ffn_Wg_s, L0_ffn_Wg_r), (L0_ffn_Wu_s, L0_ffn_Wu_r), (L0_ffn_Wd_s, L0_ffn_Wd_r))]),
        "Wrouter": L0_ffn_W_router,
    }
    arrays = {f"in_{n}": np.ascontiguousarray(a) for n, a in arrays.items()}
    nc = bacc.Bacc("TRN2", target_bir_lowering=False, num_devices=1)
    args = [nc.dram_tensor(n, a.shape, mybir.dt.from_np(a.dtype), kind="ExternalInput").ap() for n, a in arrays.items()]
    args.append(nc.dram_tensor("out", (TOK, D), F32, kind="ExternalOutput").ap())
    perceiver_kernel(nc, *args)
    r = run_bass_kernel_spmd(nc, [arrays], core_ids=[0])
    return np.asarray(r.results[0]["out"]).reshape(16, 64, D)
```

```python
from contextlib import ExitStack

import numpy as np

import concourse.bass as bass
from concourse import mybir
from concourse.alu_op_type import AluOpType as ALU

F32 = mybir.dt.float32
F32R = mybir.dt.float32r
BF16 = mybir.dt.bfloat16
I32 = mybir.dt.int32
U32 = mybir.dt.uint32
ACT = mybir.ActivationFunctionType
AX = mybir.AxisListType.X
ds = bass.ds

P = 128
D = 512
HC = D // P
TOK = 16 * 64
NT = TOK // P
SQ = 64
SK = 1601
JM = SK // P
TAIL = SK - JM * P
JT = JM + 1
S_CHUNKS = [(0, 401), (401, 400), (801, 400), (1201, 400)]
RING = 3
T_FILLS = 2 * JT
P_FILLS = -(-JT // 4)
BLOCK = T_FILLS + P_FILLS
assert BLOCK % RING == 0 and BLOCK % 2 == 0
NG, GB, NH, F, SEQ = 8, 8, 8, 128, 16
BATCH = NG * GB
PADDED = SEQ + 1
ATT_SCALE = D ** -0.5
LN_EPS = 1e-5
V_GAMMA, V_BETA, V_W1, V_W2, V_U, V_V, V_END = 0, 4, 8, 12, 16, 24, 32
NEG = -1e30

HEADS, HD, RD, LAT = 16, 32, 16, 128
QUADS = HEADS // 4
SELF_SCALE = HD ** -0.5
RMS_EPS = 1e-5
NE = 8
NR = NE - 1
HALF = TOK // 2
NJ = 2 * HC
PICKS = 2 * TOK
TILES = PICKS // P + NR - 1
RING3 = 3
PLACES = [0, 2, 1, 0, 2, 1, 0]
C_IDENT, C_PE, C_BLOCK, C_CAUSAL, C_COS, C_SIN, C_TRIL, C_RANK, C_BELOW, C_TILE, C_FILL, C_EARLIER, C_PLACE, \
    C_NEED, C_ZERO, C_END = np.cumsum([0, P, HC * 16, P, P, 16, 16, NG * NH, NE, P, TILES, NE, NE * NE, NE, NE, 1]).tolist()


def shape_constants():
    c = np.zeros((P, C_END), np.float32)
    c[:, C_IDENT:C_IDENT + P] = np.eye(P)
    pos = np.arange(16, dtype=np.float32)[:, None]
    div = np.exp(np.arange(0, D, 2, dtype=np.float32) * np.float32(-np.log(10000.0) / D))
    ang = pos * div
    pe = np.stack([np.sin(ang), np.cos(ang)], axis=-1).reshape(16, D)[::-1]
    c[:, C_PE:C_PE + HC * 16] = pe.T.reshape(HC, P, 16).transpose(1, 0, 2).reshape(P, HC * 16)
    p, q = np.arange(P)[:, None], np.arange(P)[None, :]
    c[:, C_BLOCK:C_BLOCK + P] = np.where(p % 8 == q % 8, 0.0, NEG)
    c[:, C_CAUSAL:C_CAUSAL + P] = np.where((p // 64 == q // 64) & (q <= p), 0.0, NEG)
    inv = (1.0 / np.float32(10000.0) ** (np.arange(0, 16, 2, dtype=np.float32) / np.float32(16))).astype(np.float32)
    f = (np.arange(P) % 64).astype(np.float32)[:, None] * inv[None, :]
    c[:, C_COS:C_COS + 16] = np.concatenate([np.cos(f), np.cos(f)], 1)
    c[:, C_SIN:C_SIN + 16] = np.concatenate([-np.sin(f), np.sin(f)], 1)
    batch = np.arange(NG)[None, :, None] * GB + (p // SEQ)[:, :, None]
    c[:, C_TRIL:C_TRIL + NG * NH] = (np.arange(NH)[None, None, :] <= batch).reshape(P, NG * NH)
    c[:, C_RANK:C_RANK + NE] = NE - np.arange(NE)
    c[:, C_BELOW:C_BELOW + P] = p < q
    c[:, C_TILE:C_TILE + TILES] = np.arange(TILES)
    c[:, C_FILL:C_FILL + NE] = P * np.arange(NE)
    c[:, C_FILL] = -1
    c[:, C_EARLIER:C_EARLIER + NE * NE] = (np.arange(NE)[None, :] < np.arange(NE)[:, None]).reshape(-1)
    c[:, C_PLACE:C_PLACE + NR] = np.diff([0] + PLACES)
    c[:, C_NEED:C_NEED + NR] = 1
    return c


class Steps:

    def __init__(self, eng, sem):
        self.eng, self.sem, self.base, self.n = eng, sem, 0, 0

    def mark(self, ins):
        ins.then_inc(self.sem, 1)
        self.n += 1

    def wait(self):
        self.eng.wait_ge(self.sem, self.base + self.n)

    def __call__(self, ins):
        self.mark(ins)
        self.wait()

    def enter(self):
        self.start, self.n = self.base + self.n, 0

    def turn(self, i, per):
        self.base, self.n, self.per = self.start + i * per, 0, per

    def leave(self, turns):
        assert self.n == self.per, self.n
        self.base, self.n = self.start + turns * self.per, 0


def perceiver_kernel(nc, x, ctx_keys, consts, vecs, rows, Wq, Wv, Wr, Wout, Wkvd, Wqd, Wku, Wqu, Wvu, Wropeq, Wropek,
                     Wo, Wexp, Wrouter, out):
    with ExitStack() as ctx:
        def sem(name):
            return ctx.enter_context(nc.semaphore(name))

        def sbuf(scope, name, shape, dt=F32):
            return scope.enter_context(nc.sbuf_tensor(name, shape, dt))

        bank = [ctx.enter_context(nc.psum_tensor(f"bank{i}", [P, 512], F32)) for i in range(8)]

        y = sbuf(ctx, "y", [P, NT, D])
        cst = sbuf(ctx, "cst", [P, C_END])
        ident = cst[:, C_IDENT:C_IDENT + P]
        stats = sbuf(ctx, "stats", [P, NT, 6])
        mv = sbuf(ctx, "mv", [P, NT, 2])
        mean, var = mv[:, :, 0], mv[:, :, 1]
        rstd = sbuf(ctx, "rstd", [P, NT])
        rs_v = sbuf(ctx, "rs_v", [P, NT])
        rs_h = sbuf(ctx, "rs_h", [P, NT])
        rs_t = sbuf(ctx, "rs_t", [P, NT])
        rs_r = sbuf(ctx, "rs_r", [P, NT])

        vec = sbuf(ctx, "vec", [P, V_END])
        ident_bf = sbuf(ctx, "ident_bf", [P, P], BF16)
        pos_bias = sbuf(ctx, "pos_bias", [P, 2])
        stats2 = sbuf(ctx, "stats2", [P, NT, 6])
        mv2 = sbuf(ctx, "mv2", [P, NT, 2])
        rstd2 = sbuf(ctx, "rstd2", [P, NT])
        hn = [sbuf(ctx, f"hn{i}", [P, D]) for i in range(4)]
        s_max, s_bias, s_sum, s_inv = ([sbuf(ctx, f"{n}{i}", [P, HEADS]) for i in range(2)]
                                       for n in ("s_max", "s_bias", "s_sum", "s_inv"))
        rms_x, rms_f = sbuf(ctx, "rms_x", [P, NT]), sbuf(ctx, "rms_f", [P, NT])
        gates = [sbuf(ctx, f"gates{i}", [P, NT]) for i in range(2)]
        slots = sbuf(ctx, "slots", [P, NT, 2], U32)
        tile_expert = sbuf(ctx, "tile_expert", [P, 2, TILES], I32)
        expert_begins = sbuf(ctx, "expert_begins", [P, NE], I32)
        rbias_sb = sbuf(ctx, "rbias_sb", [P, NR])
        wrout_sb = sbuf(ctx, "wrout_sb", [P, HC, NR])
        a_max, a_bias, a_sum, a_inv = ([sbuf(ctx, f"{n}{i}", [P, NH]) for i in range(2)]
                                       for n in ("a_max", "a_bias", "a_sum", "a_inv"))

        scope = ExitStack()
        nat = [sbuf(scope, f"nat{i}", [P, 2, JT, D]) for i in range(2)]
        ctxT = [sbuf(scope, f"ctxT{i}", [P, HC, SK]) for i in range(2)]
        prob = sbuf(scope, "prob", [P, SK])
        probT = sbuf(scope, "probT", [P, JT, P])
        qn = sbuf(scope, "qn", [P, D])
        qT = sbuf(scope, "qT", [P, HC, P])
        mx = sbuf(scope, "mx", [P, 4])
        nmax = sbuf(scope, "nmax", [P, 1])
        sums = sbuf(scope, "sums", [P, 4])
        total = sbuf(scope, "total", [P, 1])
        rinv = sbuf(scope, "rinv", [P, 1])
        scope.close()

        def place(kb, name, shape, dt=F32):
            with ExitStack() as below:
                if kb:
                    sbuf(below, f"{name}_below", [P, int(kb * 256)])
                return sbuf(below, name, shape, dt)

        wq_raw = place(0, "wq_raw", [P, HC, NH * F])
        wq_lo = place(0, "wq_lo", [P, HC, NH * F], F32R)
        wq_hi = place(16, "wq_hi", [P, HC, NH * F], F32R)
        wout_raw = place(0, "wout_raw", [P, NH, D])
        wout_lo = place(0, "wout_lo", [P, NH, D], F32R)
        wout_hi = place(16, "wout_hi", [P, NH, D], F32R)
        wr_sb = place(32, "wr_sb", [P, HC, NH * F])
        wv_hi = place(32, "wv_hi", [P, HC, NH * F], F32R)
        wv_raw = place(84, "wv_raw", [P, HC, NH * F])
        wv_lo = place(84, "wv_lo", [P, HC, NH * F], F32R)
        bout_sb = place(48, "bout_sb", [P, D])
        block_bf = place(50, "block_bf", [P, 4, P], BF16)
        rT_pad = place(51, "rT_pad", [P, NH, 32])
        kT = place(52, "kT", [P, NH, NG, P])
        oT = kT
        pos_g = place(100, "pos_g", [P, NG, SEQ * NH])
        h_hi = place(104, "h_hi", [P, HC, NG, P], F32R)
        h_lo = place(120, "h_lo", [P, HC, NG, P], F32R)
        hf = [place(136 + 2 * i, f"hf{i}", [P, HC, NG, 2 * GB]) for i in range(2)]
        hg_lo = [place(136 + 2 * i, f"hg_lo{i}", [P, HC, P], F32R) for i in range(2)]
        pos_sb = place(140, "pos_sb", [P, NG, PADDED * NH])
        posT = [place(154 + 4 * i, f"posT{i}", [P, NG, P]) for i in range(2)]
        ku_g = [place(162 + 4 * i, f"ku_g{i}", [P, NH, P]) for i in range(2)]
        attT = place(146, "attT", [P, NH, P])
        hg_hi = [place(150 + 2 * i, f"hg_hi{i}", [P, HC, P], F32R) for i in range(2)]
        att = [place(154 + 4 * i, f"att{i}", [P, NH, P]) for i in range(2)]
        v_g = [place(170 + 4 * i, f"v_g{i}", [P, NH * F]) for i in range(2)]
        o_hi = [place(104 + 4 * i, f"o_hi{i}", [P, NH, P], F32R) for i in range(2)]
        o_lo = [place(112 + 4 * i, f"o_lo{i}", [P, NH, P], F32R) for i in range(2)]
        wkvd_sb = place(120, "wkvd_sb", [P, HC, LAT])
        wqd_sb = place(122, "wqd_sb", [P, HC, LAT])
        wku_sb = place(124, "wku_sb", [LAT, HEADS * RD])
        wvu_sb = place(125, "wvu_sb", [LAT, D])
        wq_up = place(127, "wq_up", [LAT, 2, HEADS * RD])
        wrk_sb = place(129, "wrk_sb", [P, HC, HEADS * RD])
        xnT = [place(133 + 2 * i, f"xnT{i}", [P, HC, P]) for i in range(2)]
        latT = [place(137 + i, f"latT{i}", [LAT, 2, P]) for i in range(2)]
        kq = [place(139 + 4 * i, f"kq{i}", [P, 2 * HEADS, HD]) for i in range(2)]
        raw = place(147, "raw", [P, 2 * HEADS, RD])
        turned = place(149, "turned", [P, 2 * HEADS, RD])
        causal_bf = place(151, "causal_bf", [P, 4, P], BF16)
        y_hi = place(152, "y_hi", [P, HC, P], F32R)
        y_lo = place(154, "y_lo", [P, HC, P], F32R)
        zeros = place(172, "zeros", [P, D])
        xx = place(48, "xx", [P, NT, D])
        wo_raw = place(64, "wo_raw", [P, HC, D])
        wo_lo = place(64, "wo_lo", [P, HC, D], F32R)
        wo_hi = place(156, "wo_hi", [P, HC, D], F32R)
        spT = place(72, "spT", [P, HEADS, P])
        v_t = [place(80 + 2 * i, f"v_t{i}", [P, D]) for i in range(2)]
        qT_h = [place(84 + 2 * i, f"qT_h{i}", [P, QUADS, P]) for i in range(2)]
        kT_h = [place(88 + 8 * i, f"kT_h{i}", [P, QUADS, 4, P]) for i in range(2)]
        sp_ = [place(104 + 8 * i, f"sp{i}", [P, HEADS, P]) for i in range(2)]
        xn = hn[0:2]
        w_raw = [place(kb, f"w_raw{kb}", [P, HC, D]) for kb in (0, 8, 32)]
        w_lo = [place(kb, f"w_lo{kb}", [P, HC, D], F32R) for kb in (0, 8, 32)]
        w_hi = [place(kb, f"w_hi{kb}", [P, HC, D], F32R) for kb in (16, 24, 40)]
        xf = [hn[i][:].rearrange("p (c t) -> p c t", c=HC) for i in (2, 3, 0, 1)]
        xT_hi = place(120, "xT_hi", [P, HC, TOK], F32R)
        xT_lo = place(136, "xT_lo", [P, HC, TOK], F32R)
        hm_hi = place(152, "hm_hi", [P, HC, TOK], F32R)
        hm_lo = place(104, "hm_lo", [P, HC, TOK], F32R)
        act_g = [place(168 + 2 * i, f"act_g{i}", [P, HALF]) for i in range(2)]
        hm = [place(172 + 2 * i, f"hm{i}", [P, HALF]) for i in range(2)]
        r_p, r_eq, r_sel0, r_sel1 = (place(64 + i / 4, n, [P, NT, NE]) for i, n in enumerate(("r_p", "r_eq", "r_sel0", "r_sel1")))
        r_sel = [r_sel0, r_sel1]
        r_key = place(65, "r_key", [P, NT])
        r_picks = place(65.25, "r_picks", [P, NT, NE], BF16)
        r_first = place(65.5, "r_first", [P, 3, NE])
        below_bf = place(66, "below_bf", [P, P], BF16)
        ones_bf = place(66.25, "ones_bf", [P, P], BF16)
        r_begun = place(67, "r_begun", [P, TILES, NE])
        r_fill = place(68, "r_fill", [P, NE, NE])
        r_tile = place(68.25, "r_tile", [P, 2, TILES])
        r_slot = place(68.5, "r_slot", [P, NT, 2])
        ring_hi = place(0, "ring_hi", [P, RING3, 3, HC, D], F32R)
        ring_raw = place(72, "ring_raw", [P, RING3, 3, HC, D])
        ring_lo = place(72, "ring_lo", [P, RING3, 3, HC, D], F32R)
        xg = hn[0:2]
        xg_hi = [place(168 + 2 * i, f"xg_hi{i}", [P, HC, P], F32R) for i in range(2)]
        xg_lo = [place(144 + 2 * i, f"xg_lo{i}", [P, HC, P], F32R) for i in range(2)]
        rhm = place(172, "rhm", [P, D])
        rhm_hi = place(174, "rhm_hi", [P, HC, P], F32R)
        rhm_lo = place(148, "rhm_lo", [P, HC, P], F32R)
        yo = hn[2:4]
        picked = [place(2 * i, f"picked{i}", [P, D]) for i in range(2 * NT)]
        pos_dram = nc.dram_tensor("pos_dram", (BATCH, SEQ * PADDED * NH), F32).ap()
        x_slots = nc.dram_tensor("x_slots", (TILES * P, D), F32).ap()
        y_slots = nc.dram_tensor("y_slots", (TILES * P, D), F32).ap()

        w_loaded = {n: sem(f"{n}_loaded") for n in ("wr", "wq", "wv", "wout", "bout")}
        consts_cast = sem("consts_cast")
        whi_ready, wlo_ready = sem("whi_ready"), sem("wlo_ready")
        SPLIT = {"wq": 0, "wv": HC, "wout": 2 * HC, "wo": 3 * HC, "gate": 3 * HC + 1, "up": 3 * HC + 2, "down": 3 * HC + 3}
        hn_ready, hT_full, hf_act, hf_dve, hhi_done, hlo_done = (sem(n) for n in ("hn_ready", "hT_full", "hf_act", "hf_dve", "hhi_done", "hlo_done"))
        rT_full, rT_ready, kT_full, kT_act, kT_dve = (sem(n) for n in ("rT_full", "rT_ready", "kT_full", "kT_act", "kT_dve"))
        posT_full, bias_ready, posT_ready, pos_full, pos_out, pos_stored = (
            sem(n) for n in ("posT_full", "bias_ready", "posT_ready", "pos_full", "pos_out", "pos_stored"))
        pos_loaded = sem("pos_loaded")
        hg_act, hg_dve, ku_ready, v_full, v_out, con_full, con_out = (sem(n) for n in ("hg_act", "hg_dve", "ku_ready", "v_full", "v_out", "con_full", "con_out"))
        abias_ready, exp_ready, ainv_ready, att_ready = (sem(n) for n in ("abias_ready", "exp_ready", "ainv_ready", "att_ready"))
        attT_full, attT_act, attT_dve, o_full, o_act, o_dve = (sem(n) for n in ("attT_full", "attT_act", "attT_dve", "o_full", "o_act", "o_dve"))
        ohi_ready, olo_ready = sem("ohi_ready"), sem("olo_ready")
        bout_added, y2_full, y2_ready = sem("bout_added"), sem("y2_full"), sem("y2_ready")

        mla_loaded, raw_loaded = sem("mla_loaded"), sem("raw_loaded")
        causal_ready, cleared, xn_ready, xnT_full, xnT_ready = (sem(n) for n in ("causal_ready", "cleared", "xn_ready", "xnT_full", "xnT_ready"))
        lat_full, lat_ready, k_full, vv_full, q_full = (sem(n) for n in ("lat_full", "lat_ready", "k_full", "vv_full", "q_full"))
        raw_ready, vv_ready, kq_ready, qTh_full, kTh_full = (sem(n) for n in ("raw_ready", "vv_ready", "kq_ready", "qTh_full", "kTh_full"))
        qTh_ready, kTh_ready, self_full, sbias_ready, sexp_ready = (sem(n) for n in ("qTh_ready", "kTh_ready", "self_full", "sbias_ready", "sexp_ready"))
        sinv_ready, sp_ready, spT_full, spT_act, spT_dve = (sem(n) for n in ("sinv_ready", "sp_ready", "spT_full", "spT_act", "spT_dve"))
        yT_full, yT_ready, wo_full, xx_ready, y_summed = (sem(n) for n in ("yT_full", "yT_ready", "wo_full", "xx_ready", "y_summed"))
        xn2_ready, xfT_full, xf_ready, logit_full, logit_ready, gate_ready = (sem(n) for n in ("xn2_ready", "xfT_full", "xf_ready", "logit_full", "logit_ready", "gate_ready"))
        xhi_ready, xlo_ready = sem("xhi_ready"), sem("xlo_ready")
        y_high = sem("y_high")
        gu_full, silu_ready, hm_ready, hhi_ready, hlo_ready, hlo_dve = (
            sem(n) for n in ("gu_full", "silu_ready", "hm_ready", "hhi_ready", "hlo_ready", "hlo_dve"))
        down_added, down_full = sem("down_added"), sem("down_full")
        slots_zeroed, picks_ready, ranks_full, slots_ready, scattered = (
            sem(n) for n in ("slots_zeroed", "picks_ready", "ranks_full", "slots_ready", "scattered"))
        split_hi, split_ready = sem("split_hi"), sem("split_ready")
        routed_loaded = [sem(f"routed_loaded{m}") for m in range(3)]
        xg_loaded, y_stored = ([sem(f"{n}{i}") for i in range(2)] for n in ("xg_loaded", "y_stored"))
        xgT_full, xg_split, xgT_ready, rgate_full, rup_full, rsilu_ready, rhm_ready, rhmT_full, rhm_split, rhmT_ready, rdown_full, yo_ready = (
            sem(n) for n in ("xgT_full", "xg_split", "xgT_ready", "rgate_full", "rup_full", "rsilu_ready", "rhm_ready", "rhmT_full",
                             "rhm_split", "rhmT_ready", "rdown_full", "yo_ready"))
        picked_loaded, y_ready = [sem(f"picked_loaded{i}") for i in range(NT // 2 + 1)], sem("y_ready")

        PIECES = [(0, JM // 2), (JM // 2, JM), (JM, JT)]
        x_loaded, cst_loaded, stored = [sem(f"x_loaded{i}") for i in range(2)], sem("cst_loaded"), sem("stored")
        keys_loaded = [[[sem(f"keys_loaded{i}{b}{p}") for p in range(3)] for b in range(2)] for i in range(2)]
        ring_full, evac_act, evac_dve = sem("ring_full"), sem("evac_act"), sem("evac_dve")
        qn_ready, qT_full, qT_ready = sem("qn_ready"), sem("qT_full"), sem("qT_ready")
        scores_full, nmax_ready, prob_ready = sem("scores_full"), sem("nmax_ready"), sem("prob_ready")
        context_full, y1_ready = sem("context_full"), sem("y1_ready")
        dve_step = sem("dve_step")

        def picked_part(k):
            return (k // 2, 2) if k < NT - 2 else (k - NT // 2 + 1, 1)

        def evacs(block, g):
            return BLOCK // 2 * block + g // 2 - 1

        def gate_bank(j):
            return bank[7 if j % 2 else 4]

        def up_bank(j):
            return bank[6 if j % 2 else 5]

        def score_bank(t, c):
            return bank[4 + c] if isinstance(t, int) and t == 0 else bank[4 + c % 2]

        def row(t, k):
            return t[:, ds(k, 1), :].rearrange("p a d -> p (a d)")

        block = ctx.enter_context(nc.Block())

        @block.sync
        def _(sp):
            def load_keys(k, par):
                for b in range(2):
                    keys = ctx_keys[ds(2 * k + b, 1)]
                    main = keys[:, 0:JM * P, :].rearrange("a (p j) d -> p (a j) d", j=JM)
                    for p, (j0, j1) in enumerate(PIECES[:2]):
                        sp.dma_start(nat[par][:, b, j0:j1, :], main[:, j0:j1, :]).then_inc(keys_loaded[par][b][p], 16)
                    tail = keys[:, JM * P:SK, :].rearrange("a p d -> p (a d)")
                    sp.dma_start(nat[par][0:TAIL, b, JM, :], tail).then_inc(keys_loaded[par][b][2], 16)

            sp.dma_start(ident, consts[:, C_IDENT:C_IDENT + P]).then_inc(cst_loaded, 16)
            sp.dma_start(y[:, 0, :], x[0:P, :]).then_inc(x_loaded[0], 16)
            load_keys(0, 0)
            sp.dma_start(y[:, 1:NT, :], x[P:TOK, :].rearrange("(k p) d -> p k d", p=P)).then_inc(x_loaded[1], 16)
            sp.dma_start(vec[:], vecs).then_inc(x_loaded[1], 16)
            sp.dma_start(cst[:, C_PE:C_END], consts[:, C_PE:C_END]).then_inc(x_loaded[1], 16)
            load_keys(1, 1)
            with sp.Fori(0, NT // 2 - 1) as i:
                for par in range(2):
                    sp.wait_ge(context_full, 2 * i + par + 1)
                    load_keys(2 * i + par + 2, par)
            sp.wait_ge(context_full, NT - 1)
            sp.dma_start(wq_raw[:], Wq.rearrange("(c p) n -> p c n", p=P)).then_inc(w_loaded["wq"], 16)
            sp.dma_start(wr_sb[:], Wr.rearrange("(c p) n -> p c n", p=P)).then_inc(w_loaded["wr"], 16)
            sp.dma_start(bout_sb[:], rows[0, 0:D].partition_broadcast(P)).then_inc(w_loaded["bout"], 16)
            sp.wait_ge(y1_ready, NT)
            sp.dma_start(wv_raw[:], Wv.rearrange("(c p) n -> p c n", p=P)).then_inc(w_loaded["wv"], 16)
            sp.wait_ge(pos_out, NG)
            sp.dma_start(pos_dram.rearrange("(g b) (i f) -> (b i) g f", b=GB, i=SEQ), pos_sb[:]).then_inc(pos_stored, 16)
            sp.wait_ge(pos_stored, 16)
            for b in range(GB):
                sp.dma_start(pos_g[b:P:GB, :, :],
                             pos_dram.rearrange("(g b) f -> b g f", b=GB)[b, :, SEQ * NH:PADDED * SEQ * NH].rearrange(
                                 "g (i f) -> i g f", i=SEQ)).then_inc(pos_loaded, 16)
            sp.wait_ge(kT_full, 2 * NH)
            sp.dma_start(wout_raw[:], Wout.rearrange("(n p) d -> p n d", p=P)).then_inc(w_loaded["wout"], 16)
            sp.wait_ge(v_full, 2 * NG)
            for dst, src in ((wkvd_sb[:], Wkvd.rearrange("(c p) n -> p c n", p=P)), (wqd_sb[:], Wqd.rearrange("(c p) n -> p c n", p=P)),
                             (wrk_sb[:], Wropek.rearrange("(c p) n -> p c n", p=P)), (wku_sb[:], Wku), (wvu_sb[:], Wvu),
                             (wq_up[:, 0, :], Wqu), (wq_up[:, 1, :], Wropeq)):
                sp.dma_start(dst, src).then_inc(mla_loaded, 16)
            sp.dma_start(wrout_sb[:], Wrouter.rearrange("(c p) n -> p c n", p=P)).then_inc(mla_loaded, 16)
            sp.dma_start(rbias_sb[:], rows[0, D:D + NR].partition_broadcast(P)).then_inc(mla_loaded, 16)

            def matrix(m, e):
                return Wexp[m, e].rearrange("(c p) n -> p c n", p=P)

            sp.wait_ge(y2_full, NT)
            sp.dma_start(wo_raw[:], Wo.rearrange("(c p) n -> p c n", p=P)).then_inc(raw_loaded, 16)
            for m in range(3):
                sp.dma_start(w_raw[m][:], matrix(m, 0)).then_inc(raw_loaded, 16)
            sp.wait_ge(cleared, 3)
            sp.dma_start(x_slots.rearrange("(t p) d -> p t d", p=P),
                         zeros[:].unsqueeze(1).broadcast_to([P, TILES, D])).then_inc(slots_zeroed, 16)
            for e in range(NR):
                if e == 0:
                    sp.wait_ge(wo_full, NT)
                elif e == 1:
                    sp.wait_ge(gu_full, NJ)
                    sp.wait_ge(scattered, 16 * 2 * NT)
                elif e == 2:
                    sp.wait_ge(down_full, NT)
                else:
                    sp.wait_ge(rdown_full, sp.value_load(expert_begins[0:1, e - RING3 + 1:e - RING3 + 2], min_val=1, max_val=TILES))
                for m in range(3):
                    sp.dma_start(ring_raw[:, PLACES[e], m, :, :], matrix(m, e + 1)).then_inc(routed_loaded[m], 16)
                for m in range(3):
                    sp.wait_ge(routed_loaded[m], 16 * (e + 1))
            for k in range(NT):
                sp.wait_ge(y_ready, k + 1)
                sp.dma_start(out[k * P:(k + 1) * P, :], y[:, k, :]).then_inc(stored, 16)
            sp.wait_ge(stored, 16 * NT)

        @block.tensor
        def _(pe):
            def ring_free(blk, g):
                v = evacs(blk, g - RING)
                if not (isinstance(v, int) and v <= 0):
                    pe.wait_ge(evac_act if (g - RING) % 2 == 0 else evac_dve, v)

            def key_transposes(k, par, blk, g0):
                turn = 16 * (k // 2 + 1) if isinstance(k, int) else k
                for b in range(2):
                    for j in range(JT):
                        for p, (j0, _) in enumerate(PIECES):
                            if j == j0:
                                pe.wait_ge(keys_loaded[par][b][p], turn)
                        g = g0 + b * JT + j
                        n = P if j < JM else TAIL
                        ring_free(blk, g)
                        for c in range(HC):
                            last = nc.tensor.transpose(bank[4 + g % RING][:, c * P:c * P + n],
                                                       nat[par][0:n, b, j, c * P:(c + 1) * P], ident[0:n, 0:n])
                        last.then_inc(ring_full, 1)

            def query_transposes(k):
                pe.wait_ge(qn_ready, k + 1)
                for c in range(HC):
                    last = nc.tensor.transpose(bank[7][:, c * P:(c + 1) * P], qn[:, c * P:(c + 1) * P], ident)
                last.then_inc(qT_full, 1)

            def scores(k, blk, g_last):
                pe.wait_ge(qT_ready, k + 1)
                for g in (g_last - 1, g_last):
                    pe.wait_ge(evac_act if g % 2 == 0 else evac_dve, evacs(blk, g))
                if not (isinstance(k, int) and k == 0):
                    pe.wait_ge(prob_ready, 4 * k)
                for n, (s0, w) in enumerate(S_CHUNKS):
                    for c in range(HC):
                        for b in range(2):
                            last = nc.tensor.matmul(bank[n][64 * b:64 * b + 64, 0:w], qT[:, c, 64 * b:64 * b + 64],
                                                    ctxT[b][:, c, s0:s0 + w], start=c == 0, stop=c == HC - 1,
                                                    skip_group_check=True)
                    last.then_inc(scores_full, 1)

            def prob_transposes(k, blk, g0):
                pe.wait_ge(prob_ready, 4 * k + 4)
                for f in range(P_FILLS):
                    g = g0 + f
                    ring_free(blk, g)
                    for j in range(4 * f, min(4 * f + 4, JT)):
                        n = P if j < JM else TAIL
                        last = nc.tensor.transpose(bank[4 + g % RING][0:n, (j % 4) * P:(j % 4 + 1) * P],
                                                   prob[:, j * P:j * P + n], ident)
                    last.then_inc(ring_full, 1)

            def context(k, par, blk, g_last):
                for g in (g_last - 1, g_last):
                    pe.wait_ge(evac_act if g % 2 == 0 else evac_dve, evacs(blk, g))
                for j in range(JT):
                    n = P if j < JM else TAIL
                    for b in range(2):
                        last = nc.tensor.matmul(bank[7][64 * b:64 * b + 64, :], probT[0:n, j, 64 * b:64 * b + 64],
                                                nat[par][0:n, b, j, :], start=j == 0, stop=j == JT - 1,
                                                skip_group_check=True)
                last.then_inc(context_full, 1)

            def step(k, par, turn):
                if not (isinstance(k, int) and k == 0):
                    pe.wait_ge(y1_ready, k)
                query_transposes(k + 1)
                key_transposes(turn, 1 - par, k + 1, 0)
                prob_transposes(k, k + 1, T_FILLS)
                pe.wait_ge(qT_ready, k + 2)
                context(k, par, k + 1, BLOCK - 1)
                scores(k + 1, k + 1, T_FILLS - 1)

            pe.wait_ge(cst_loaded, 16)
            key_transposes(0, 0, 0, BLOCK - T_FILLS)
            query_transposes(0)
            scores(0, 0, BLOCK - 1)
            step(0, 0, 1)
            with pe.Fori(0, NT // 2 - 1) as i:
                step(2 * i + 1, 1, 16 * i + 32)
                step(2 * i + 2, 0, 16 * i + 32)
            prob_transposes(NT - 1, NT, 0)

            def norm_transposes(k):
                pe.wait_ge(hn_ready, k + 1)
                if k >= 4:
                    pe.wait_ge(hf_dve if k % 2 else hf_act, (k - 4) // 2 + 1)
                for c in range(HC):
                    last = nc.tensor.transpose(bank[k % 4][:, c * P:(c + 1) * P], hn[k % 4][:, c * P:(c + 1) * P], ident)
                last.then_inc(hT_full, 1)

            def keys(half, n):
                m = half * NH + n
                if m >= 4:
                    pe.wait_ge(kT_act if m % 2 == 0 else kT_dve, (m - 4) // 2 + 1)
                for c in range(HC):
                    hi, lo = (t[:, c, n * F:(n + 1) * F] for t in (wq_hi, wq_lo))
                    hh, hl = (t[:, c, :, half * BATCH:(half + 1) * BATCH] for t in (h_hi, h_lo))
                    nc.tensor.matmul(bank[4 + m % 4][:], lo, hh, start=c == 0, stop=False)
                    nc.tensor.matmul(bank[4 + m % 4][:], hi, hl, start=False, stop=False)
                    last = nc.tensor.matmul(bank[4 + m % 4][:], hi, hh, start=False, stop=c == HC - 1)
                last.then_inc(kT_full, 1)

            pe.wait_ge(prob_ready, 4 * NT)
            for k in range(4):
                norm_transposes(k)
            context(NT - 1, 1, NT, P_FILLS - 1)
            for k in range(4, 7):
                norm_transposes(k)
            for part in (whi_ready, wlo_ready):
                pe.wait_ge(part, SPLIT["wq"] + HC)
            pe.wait_ge(hhi_done, NT // 2)
            pe.wait_ge(hlo_done, NT // 2)
            for n in range(NH):
                if n == 3:
                    pe.wait_ge(y1_ready, NT)
                if n == 4:
                    norm_transposes(7)
                    pe.wait_ge(w_loaded["wr"], 16)
                    pe.wait_ge(hf_act, 4)
                    for m in range(NH):
                        for c in range(HC):
                            last = nc.tensor.matmul(bank[2][:, m * SEQ:(m + 1) * SEQ], wr_sb[:, c, m * F:(m + 1) * F],
                                                    cst[:, C_PE + c * SEQ:C_PE + (c + 1) * SEQ], start=c == 0, stop=c == HC - 1)
                    last.then_inc(rT_full, 1)
                keys(0, n)
            pe.wait_ge(hhi_done, NT)
            pe.wait_ge(hlo_done, NT)

            def pos_bias_scores():
                pe.wait_ge(rT_ready, 1)
                pe.wait_ge(x_loaded[1], 3 * 16)
                for n in range(NH):
                    h, q = divmod(n, 4)
                    last = nc.tensor.matmul(bank[0][32 * q:32 * q + 32, h:h + 1], rT_pad[:, n, :], vec[:, V_V + n:V_V + n + 1],
                                            start=True, stop=True, skip_group_check=True)
                last.then_inc(posT_full, 1)

            def pos_scores(half):
                pe.wait_ge(kT_act, NH // 2 * (half + 1))
                pe.wait_ge(kT_dve, NH // 2 * (half + 1))
                for h in range(2):
                    for q in range(4):
                        last = nc.tensor.matmul(bank[2 - 2 * half + h][32 * q:32 * q + 32, :], rT_pad[:, 4 * h + q, :],
                                                kT[:, 4 * h + q, :, half * BATCH:(half + 1) * BATCH], start=True, stop=True,
                                                skip_group_check=True)
                    last.then_inc(posT_full, 1)

            for n in range(NH):
                if n == NH // 2:
                    pos_bias_scores()
                    pos_scores(0)
                keys(1, n)
            pos_scores(1)
            pe.wait_ge(posT_ready, 4)
            for g in range(NG):
                if g >= 4:
                    pe.wait_ge(pos_out, g - 3)
                for h in range(2):
                    last = nc.tensor.transpose(bank[4 + g % 4][:, h * P:(h + 1) * P],
                                               posT[h][:, g, :], ident)
                last.then_inc(pos_full, 1)

            def group_scores(g, par):
                pe.wait_ge(ku_ready, g + 1)
                if not (isinstance(g, int) and g == 0):
                    pe.wait_ge(con_out, 2 * g)
                for h in range(2):
                    nc.tensor.matmul(bank[h][:], ident_bf[:], block_bf[:].rearrange("p n q -> p (n q)"),
                                     start=True, stop=True)
                    for n in range(4 * h, 4 * h + 4):
                        last = nc.tensor.matmul(bank[h][:, (n % 4) * P:(n % 4 + 1) * P], ku_g[par][:, n, :],
                                                kT[:, n, ds(g, 1), :].rearrange("p a q -> p (a q)"), start=False, stop=True,
                                                skip_group_check=True)
                    last.then_inc(con_full, 1)

            def group_values(g, par):
                pe.wait_ge(hg_act, g + 1)
                pe.wait_ge(hg_dve, g + 1)
                for h in range(2):
                    if not (isinstance(g, int) and g == 0):
                        pe.wait_ge(v_out, 2 * g + h - 1)
                    for c in range(HC):
                        hi, lo = (t[:, c, h * 512:(h + 1) * 512] for t in (wv_hi, wv_lo))
                        nc.tensor.matmul(bank[2 + h][:], hg_lo[par][:, c, :], hi, start=c == 0, stop=False)
                        nc.tensor.matmul(bank[2 + h][:], hg_hi[par][:, c, :], lo, start=False, stop=False)
                        last = nc.tensor.matmul(bank[2 + h][:], hg_hi[par][:, c, :], hi, start=False, stop=c == HC - 1)
                    last.then_inc(v_full, 1)

            def weightsT(g, par):
                pe.wait_ge(att_ready, g + 1)
                for n in range(NH):
                    last = nc.tensor.transpose(bank[4 + n // 4][:, (n % 4) * P:(n % 4 + 1) * P], att[par][:, n, :], ident)
                    if n % 4 == 3:
                        last.then_inc(attT_full, 1)

            def group_output(g, par):
                pe.wait_ge(v_out, 2 * g + 2)
                pe.wait_ge(attT_act, g + 1)
                pe.wait_ge(attT_dve, g + 1)
                if not (isinstance(g, int) and g == 0):
                    pe.wait_ge(o_act, g)
                    pe.wait_ge(o_dve, g)
                for n in range(NH):
                    last = nc.tensor.matmul(bank[6 + n // 4][:, (n % 4) * P:(n % 4 + 1) * P],
                                            v_g[par][:, n * F:(n + 1) * F], attT[:, n, :], start=True, stop=True)
                    if n % 4 == 3:
                        last.then_inc(o_full, 1)

            pe.wait_ge(consts_cast, 2)
            group_scores(0, 0)
            for part in (whi_ready, wlo_ready):
                pe.wait_ge(part, SPLIT["wv"] + HC)
            group_values(0, 0)
            group_values(1, 1)
            group_scores(1, 1)
            weightsT(0, 0)
            group_scores(2, 0)
            group_output(0, 0)
            group_values(2, 0)
            with pe.Fori(0, NG // 2 - 2) as i:
                for par in (1, 0):
                    g = 2 * i + 2 - par
                    weightsT(g, par)
                    group_scores(g + 2, par)
                    group_output(g, par)
                    group_values(g + 2, par)
            weightsT(NG - 3, 1)
            group_scores(NG - 1, 1)
            group_output(NG - 3, 1)
            group_values(NG - 1, 1)
            for g in (NG - 2, NG - 1):
                weightsT(g, g % 2)
                group_output(g, g % 2)
            for part in (whi_ready, wlo_ready):
                pe.wait_ge(part, SPLIT["wout"] + HC)

            def out_product(k, par):
                pe.wait_ge(ohi_ready, k + 1)
                for n in range(NH):
                    nc.tensor.matmul(bank[6 + par][:], o_hi[par][:, n, :], wout_hi[:, n, :], start=n == 0, stop=False)
                    nc.tensor.matmul(bank[6 + par][:], o_hi[par][:, n, :], wout_lo[:, n, :], start=False, stop=False)
                pe.wait_ge(olo_ready, k + 1)
                for n in range(NH):
                    last = nc.tensor.matmul(bank[6 + par][:], o_lo[par][:, n, :], wout_hi[:, n, :], start=False, stop=n == NH - 1)
                last.then_inc(y2_full, 1)

            out_product(0, 0)
            out_product(1, 1)
            with pe.Fori(0, NT // 2 - 2) as i:
                for par in range(2):
                    pe.wait_ge(y2_ready, 2 * i + par + 1)
                    out_product(2 * i + par + 2, par)

            def norm_columns(t, par):
                pe.wait_ge(xn_ready, t + 1)
                if isinstance(t, int) and t in (1, 2):
                    pe.wait_ge(xnT_ready, t)
                elif not isinstance(t, int) or t > 2:
                    pe.wait_ge(yT_ready, t - 2)
                for c in range(HC):
                    last = nc.tensor.transpose(bank[0][:, c * P:(c + 1) * P], xn[par][:, c * P:(c + 1) * P], ident)
                last.then_inc(xnT_full, 1)

            def latents(t, par):
                pe.wait_ge(xnT_ready, t + 1)
                if not (isinstance(t, int) and t == 0):
                    pe.wait_ge(raw_ready, t)
                for i, w in enumerate((wkvd_sb, wqd_sb)):
                    for c in range(HC):
                        last = nc.tensor.matmul(bank[1][:, i * P:(i + 1) * P], w[:, c, :], xnT[par][:, c, :], start=c == 0,
                                                stop=c == HC - 1)
                last.then_inc(lat_full, 1)

            def rotary_keys(par):
                for c in range(HC):
                    nc.tensor.matmul(bank[2][:, 0:256], xnT[par][:, c, :], wrk_sb[:, c, :], start=c == 0, stop=c == HC - 1)

            def from_latents(t, par):
                pe.wait_ge(lat_ready, t + 1)
                nc.tensor.matmul(bank[2][:, 256:512], latT[par][:, 0, :], wku_sb[:], start=True, stop=True).then_inc(k_full, 1)
                nc.tensor.matmul(bank[1][:], latT[par][:, 1, :], wq_up[:].rearrange("l a n -> l (a n)"), start=True,
                                 stop=True).then_inc(q_full, 1)
                if not (isinstance(t, int) and t == 0):
                    pe.wait_ge(kTh_ready, t)
                nc.tensor.matmul(bank[3][:], latT[par][:, 0, :], wvu_sb[:], start=True, stop=True).then_inc(vv_full, 1)

            def heads_columns(par, first, full):
                for c in range(QUADS):
                    last = nc.tensor.transpose(bank[3][:, c * P:(c + 1) * P],
                                               kq[par][:, first + 4 * c:first + 4 * c + 4, :].rearrange("p h d -> p (h d)"),
                                               ident)
                last.then_inc(full, 1)

            def query_columns(t, par):
                pe.wait_ge(kq_ready, t + 1)
                pe.wait_ge(vv_ready, t + 1)
                heads_columns(par, HEADS, qTh_full)

            def key_columns(t, par):
                pe.wait_ge(qTh_ready, t + 1)
                heads_columns(par, 0, kTh_full)

            def self_scores(t, par, quads):
                pe.wait_ge(kTh_ready, t + 1)
                for c in quads:
                    b = score_bank(t, c)
                    if not (isinstance(t, int) and t == 0):
                        pe.wait_ge(sexp_ready, 4 * t + c - 1)
                    nc.tensor.matmul(b[:], ident_bf[:], causal_bf[:].rearrange("p n q -> p (n q)"), start=True,
                                     stop=False)
                    nc.tensor.matmul(b[:], qT_h[par][:, c, :], kT_h[par][:, c, :, :].rearrange("p n q -> p (n q)"),
                                     start=False, stop=True).then_inc(self_full, 1)

            def weight_columns(k, par, quads):
                for c in quads:
                    pe.wait_ge(sp_ready, 4 * k + c + 1)
                    if c >= 2:
                        pe.wait_ge(spT_dve if c % 2 else spT_act, 2 * k + 1)
                    elif c == 0 and not (isinstance(k, int) and k == 0):
                        pe.wait_ge(xx_ready, k)
                    elif isinstance(k, int) and k == 0:
                        pe.wait_ge(sexp_ready, c + 3)
                    for n in range(4):
                        last = nc.tensor.transpose(bank[6 + c % 2][:, n * P:(n + 1) * P], sp_[par][:, 4 * c + n, :], ident)
                    last.then_inc(spT_full, 1)

            def self_output(k, par):
                pe.wait_ge(spT_act, 2 * k + 2)
                pe.wait_ge(spT_dve, 2 * k + 2)
                for h in range(HEADS):
                    last = nc.tensor.matmul(bank[0][HD * (h % 4):HD * (h % 4 + 1), h // 4 * P:(h // 4 + 1) * P],
                                            v_t[par][:, HD * h:HD * (h + 1)], spT[:, h, :], start=True, stop=True,
                                            skip_group_check=True)
                last.then_inc(yT_full, 1)

            def output_product(k):
                if isinstance(k, int) and k == 0:
                    pe.wait_ge(wlo_ready, SPLIT["wo"] + 1)
                pe.wait_ge(yT_ready, k + 1)
                for c in range(HC):
                    nc.tensor.matmul(bank[6][:], y_hi[:, c, :], wo_hi[:, c, :], start=c == 0, stop=False)
                    nc.tensor.matmul(bank[6][:], y_hi[:, c, :], wo_lo[:, c, :], start=False, stop=False)
                    last = nc.tensor.matmul(bank[6][:], y_lo[:, c, :], wo_hi[:, c, :], start=False, stop=c == HC - 1)
                last.then_inc(wo_full, 1)

            def expert_columns(k):
                pe.wait_ge(xn2_ready, k + 1)
                if k < 2:
                    pe.wait_ge(raw_ready, NT)
                else:
                    pe.wait_ge(xf_ready, k - 1)
                for c in range(HC):
                    last = nc.tensor.transpose(bank[1 + k % 2][:, c * P:(c + 1) * P], xx[:, k, c * P:(c + 1) * P], ident)
                last.then_inc(xfT_full, 1)

            def router(k):
                pe.wait_ge(xf_ready, k + 1)
                for c in range(HC):
                    last = nc.tensor.matmul(bank[3][:, NE * k:NE * k + NR], xf[k % 4][:, c, :], wrout_sb[:, c, :],
                                            start=c == 0, stop=c == HC - 1)
                last.then_inc(logit_full, 1)

            gate, up, down = range(3)

            def shared_hidden(j, m):
                half, ic = divmod(j, HC)
                b = gate_bank(j) if m == gate else up_bank(j)
                if j == 0:
                    for part in (whi_ready, wlo_ready):
                        pe.wait_ge(part, SPLIT["gate"] + m + 1)
                    pe.wait_ge(sexp_ready, QUADS * NT)
                elif j == 1 and m == gate:
                    pe.wait_ge(spT_dve, 2 * NT)
                elif j == 1:
                    pe.wait_ge(xx_ready, NT)
                elif m == gate:
                    pe.wait_ge(hm_ready, j - 1)
                if j % HC == 0 and m == gate:
                    pe.wait_ge(xhi_ready, NT // 2 * (half + 1))
                    pe.wait_ge(xlo_ready, NT // 2 * (half + 1))
                for c in range(HC):
                    lo, hi = (w[m][:, c, ic * P:(ic + 1) * P] for w in (w_lo, w_hi))
                    xl, xh = (t[:, c, half * HALF:(half + 1) * HALF] for t in (xT_lo, xT_hi))
                    nc.tensor.matmul(b[:], lo, xh, start=c == 0, stop=False)
                    nc.tensor.matmul(b[:], hi, xl, start=False, stop=False)
                    last = nc.tensor.matmul(b[:], hi, xh, start=False, stop=c == HC - 1)
                if m == up:
                    last.then_inc(gu_full, 1)

            def self_step(k, par, scores=True, project=True):
                if project:
                    norm_columns(k + 2, par)
                if scores:
                    query_columns(k + 1, 1 - par)
                if not scores:
                    for t in range(2):
                        router(t)
                        expert_columns(t + 2)
                weight_columns(k, par, (0, 1))
                if project:
                    latents(k + 2, par)
                if scores:
                    key_columns(k + 1, 1 - par)
                weight_columns(k, par, (2, 3))
                if project:
                    rotary_keys(par)
                if scores:
                    self_scores(k + 1, 1 - par, (0, 1))
                self_output(k, par)
                if project:
                    from_latents(k + 2, par)
                if scores:
                    self_scores(k + 1, 1 - par, (2, 3))
                if scores and not project:
                    expert_columns(0)
                    expert_columns(1)
                if not scores:
                    router(2)
                    router(3)
                output_product(k)
                if not scores:
                    shared_hidden(0, gate)
                    shared_hidden(0, up)

            pe.wait_ge(y2_ready, NT - 3)
            out_product(NT - 2, 0)
            pe.wait_ge(y2_ready, NT - 2)
            out_product(NT - 1, 1)
            pe.wait_ge(mla_loaded, 16 * 9)
            pe.wait_ge(causal_ready, 1)
            norm_columns(0, 0)
            latents(0, 0)
            norm_columns(1, 1)
            rotary_keys(0)
            from_latents(0, 0)
            latents(1, 1)
            rotary_keys(1)
            query_columns(0, 0)
            key_columns(0, 0)
            from_latents(1, 1)
            pe.wait_ge(y2_ready, NT)
            self_scores(0, 0, range(QUADS))
            self_step(0, 0)
            with pe.Fori(0, NT // 2 - 2) as i:
                self_step(2 * i + 1, 1)
                self_step(2 * i + 2, 0)
            self_step(NT - 3, 1)
            self_step(NT - 2, 0, project=False)
            self_step(NT - 1, 1, scores=False, project=False)

            for j in range(NJ):
                if j >= 1:
                    shared_hidden(j, gate)
                    shared_hidden(j, up)
                if j == 1:
                    expert_columns(4)
                    expert_columns(5)
                elif j == 2:
                    for k in (4, 5):
                        router(k)
                        expert_columns(k + 2)
                elif j == 3:
                    router(6)
                    router(7)
                elif j == 5:
                    pe.wait_ge(consts_cast, 4)
                    pe.wait_ge(picks_ready, 1)
                    picks = r_picks[:].rearrange("p k e -> p (k e)")
                    nc.tensor.matmul(bank[3][:, 0:NT * NE], below_bf[:], picks, start=True, stop=True)
                    for k in range(1, NT):
                        nc.tensor.matmul(bank[3][:, k * NE:NT * NE], ones_bf[:], picks[:, 0:(NT - k) * NE], start=False,
                                         stop=True, skip_group_check=True)
                    for k in range(NT):
                        last = nc.tensor.matmul(bank[3][:, NT * NE:(NT + 1) * NE], ones_bf[:], r_picks[:, k, :], start=k == 0,
                                                stop=k == NT - 1, skip_group_check=True)
                    last.then_inc(ranks_full, 1)
            def places_of(t, n):
                _, places = nc.values_load_multi_w_load_instructions(tile_expert[0:1, 0, ds(t, n)], engines=(mybir.EngineType.PE,),
                                                                     min_val=0, max_val=RING3 - 1)
                return places

            def routed_product(b, m, at, x_hi, x_lo, full):
                for c in range(HC):
                    hi, lo = (t[:, ds(at, 1), m, c, :].rearrange("p a d -> p (a d)") for t in (ring_hi, ring_lo))
                    nc.tensor.matmul(b[:], x_lo[:, c, :], hi, start=c == 0, stop=False)
                    nc.tensor.matmul(b[:], x_hi[:, c, :], lo, start=False, stop=False)
                    last = nc.tensor.matmul(b[:], x_hi[:, c, :], hi, start=False, stop=c == HC - 1)
                last.then_inc(full, 1)

            def rows_columns(t, par, turn):
                pe.wait_ge(xg_loaded[par], 16 * turn)
                if not (isinstance(t, int) and t < 2):
                    pe.wait_ge(xgT_ready, t - 1)
                for c in range(HC):
                    last = nc.tensor.transpose(bank[6 + par][:, c * P:(c + 1) * P], xg[par][:, c * P:(c + 1) * P], ident)
                last.then_inc(xgT_full, 1)

            def routed_hidden(t, par, at, turn=None):
                if not (isinstance(t, int) and t < 2):
                    hidden_columns(t - 1)
                pe.wait_ge(xgT_ready, t + 1)
                for m, b, full in ((gate, 1, rgate_full), (up, 2, rup_full)):
                    if not (isinstance(t, int) and t == 0):
                        pe.wait_ge(rsilu_ready if m == gate else rhm_ready, t)
                    routed_product(bank[b], m, at, xg_hi[par], xg_lo[par], full)
                    if isinstance(t, int) and t == 1 and m == gate:
                        hidden_columns(0)
                    if m == gate and turn is not None:
                        rows_columns(t + 1, 1 - par, turn)

            def hidden_columns(t):
                pe.wait_ge(rhm_ready, t + 1)
                if not (isinstance(t, int) and t == 0):
                    pe.wait_ge(rhmT_ready, t)
                for c in range(HC):
                    last = nc.tensor.transpose(bank[3][:, c * P:(c + 1) * P], rhm[:, c * P:(c + 1) * P], ident)
                last.then_inc(rhmT_full, 1)

            def routed_output(t, par, at):
                pe.wait_ge(rhmT_ready, t + 1)
                if not isinstance(t, int) or t >= 2:
                    pe.wait_ge(yo_ready, t - 1)
                routed_product(bank[4 + par], down, at, rhm_hi, rhm_lo, rdown_full)

            for part in (whi_ready, wlo_ready):
                pe.wait_ge(part, SPLIT["down"] + 1)
            pe.wait_ge(yT_ready, NT)
            pe.wait_ge(xf_ready, NT)
            for k in range(NT):
                if k < NT // 2:
                    pe.wait_ge(hhi_ready, HC)
                    pe.wait_ge(hlo_ready, HC)
                else:
                    pe.wait_ge(hhi_ready, NJ)
                    pe.wait_ge(hlo_ready, NJ - 2)
                    pe.wait_ge(hlo_dve, 2)
                if k >= 3:
                    pe.wait_ge(down_added, k - 2)
                for c in range(HC):
                    hl, hh = (t[:, c, k * P:(k + 1) * P] for t in (hm_lo, hm_hi))
                    nc.tensor.matmul(bank[k % 3][:], hl, w_hi[down][:, c, :], start=c == 0, stop=False)
                    nc.tensor.matmul(bank[k % 3][:], hh, w_lo[down][:, c, :], start=False, stop=False)
                    last = nc.tensor.matmul(bank[k % 3][:], hh, w_hi[down][:, c, :], start=False, stop=c == HC - 1)
                last.then_inc(down_full, 1)
                if k == NT - 3:
                    pe.wait_ge(slots_ready, 2)
                    at = places_of(0, 3)
                if k >= NT - 2:
                    pe.wait_ge(hm_ready, NJ)
                    rows_columns(k - NT + 2, k % 2, 1)

            pe.wait_ge(down_added, NT)
            routed_hidden(0, 0, at[0])
            for t in (1, 2):
                routed_hidden(t, t % 2, at[t], (t + 1) // 2 + 1)
                routed_output(t - 1, (t - 1) % 2, at[t - 1])
            with pe.Fori(0, TILES // 2 - 2) as i:
                at = places_of(2 * i + 2, 3)
                for n, par in enumerate((1, 0)):
                    t = 2 * i + 4 - par
                    routed_hidden(t, par, at[n + 1], i + 3)
                    routed_output(t - 1, 1 - par, at[n])
            at = places_of(TILES - 2, 2)
            routed_hidden(TILES - 1, 1, at[1])
            routed_output(TILES - 2, 0, at[0])
            hidden_columns(TILES - 1)
            routed_output(TILES - 1, 1, at[1])

        @block.gpsimd
        def _(pool):
            def weight_low(lo, raw, hi, first, pieces=range(HC)):
                n = raw.shape[1] // HC
                for c in pieces:
                    pool.wait_ge(whi_ready, first + c + 1)
                    at = slice(n * c, n * (c + 1))
                    nc.gpsimd.tensor_tensor(lo[:, at, :], raw[:, at, :], hi.bitcast(F32)[:, at, :],
                                            ALU.subtract).then_inc(wlo_ready, 1)

            def normalise(g, par):
                pool.wait_ge(ainv_ready, g + 1)
                nc.gpsimd.tensor_tensor(att[par][:], att[par][:], a_inv[par][:].unsqueeze(2).broadcast_to([P, NH, P]),
                                        ALU.mult).then_inc(att_ready, 1)

            def group_queries(g, par):
                nc.gpsimd.tensor_tensor(ku_g[par][:], kT[:, :, ds(g, 1), :].rearrange("p n a q -> p (n a) q"),
                                        vec[:, V_U:V_U + NH].unsqueeze(2).broadcast_to([P, NH, P]), ALU.add).then_inc(ku_ready, 1)

            weight_low(wq_lo, wq_raw, wq_hi, SPLIT["wq"])
            for k in range(NT):
                pool.wait_ge(hhi_done, k + 1)
                at = slice(2 * GB * k, 2 * GB * (k + 1))
                nc.gpsimd.tensor_tensor(h_lo[:, :, :, at], hf[k % 2][:], h_hi.bitcast(F32)[:, :, :, at],
                                        ALU.subtract).then_inc(hlo_done, 1)
            weight_low(wv_lo, wv_raw, wv_hi, SPLIT["wv"])
            pool.wait_ge(kT_act, NH)
            pool.wait_ge(kT_dve, NH)
            group_queries(0, 0)
            group_queries(1, 1)
            pool.wait_ge(w_loaded["bout"], 16)
            pool.wait_ge(hn_ready, NT)
            nc.gpsimd.tensor_tensor(y[:], y[:], bout_sb[:].unsqueeze(1).broadcast_to([P, NT, D]),
                                    ALU.add).then_inc(bout_added, 1)
            normalise(0, 0)
            pool.wait_ge(con_full, 2)
            group_queries(2, 0)
            with pool.Fori(0, NG // 2 - 2) as i:
                for par in (1, 0):
                    g = 2 * i + 2 - par
                    normalise(g, par)
                    pool.wait_ge(con_full, 2 * g + 2)
                    group_queries(g + 2, par)
            weight_low(wout_lo, wout_raw, wout_hi, SPLIT["wout"], range(HC // 2))
            normalise(NG - 3, 1)
            pool.wait_ge(con_full, 2 * (NG - 3) + 2)
            group_queries(NG - 1, 1)
            weight_low(wout_lo, wout_raw, wout_hi, SPLIT["wout"], range(HC // 2, HC))
            normalise(NG - 2, 0)
            normalise(NG - 1, 1)

            pool.wait_ge(o_full, 2 * NG)
            for t in kT_h:
                nc.gpsimd.memset(t[:], 0.0).then_inc(cleared, 1)
            nc.gpsimd.memset(zeros[:], 0.0).then_inc(cleared, 1)

            def self_normalise(k, par):
                for c in range(QUADS):
                    pool.wait_ge(sinv_ready, 4 * k + c + 1)
                    nc.gpsimd.tensor_tensor(sp_[par][:, 4 * c:4 * c + 4, :], sp_[par][:, 4 * c:4 * c + 4, :],
                                            s_inv[par][:, 4 * c:4 * c + 4].unsqueeze(2).broadcast_to([P, 4, P]),
                                            ALU.mult).then_inc(sp_ready, 1)

            def add_up(k):
                pool.wait_ge(xx_ready, k + 1)
                nc.gpsimd.tensor_tensor(row(y, k), row(y, k), row(xx, k), ALU.add).then_inc(y_summed, 1)

            gate, up, down = range(3)

            def low_part(m):
                pool.wait_ge(whi_ready, SPLIT["gate"] + m + 1)
                nc.gpsimd.tensor_tensor(w_lo[m][:], w_raw[m][:], w_hi[m].bitcast(F32)[:], ALU.subtract).then_inc(wlo_ready, 1)

            def columns_low(k):
                pool.wait_ge(xhi_ready, k + 1)
                at = slice(k * P, (k + 1) * P)
                nc.gpsimd.tensor_tensor(xT_lo[:, :, at], xf[k % 4][:], xT_hi.bitcast(F32)[:, :, at],
                                        ALU.subtract).then_inc(xlo_ready, 1)

            self_normalise(0, 0)
            pool.wait_ge(whi_ready, SPLIT["wo"] + 1)
            nc.gpsimd.tensor_tensor(wo_lo[:], wo_raw[:], wo_hi.bitcast(F32)[:], ALU.subtract).then_inc(wlo_ready, 1)
            low_part(gate)
            with pool.Fori(0, NT // 2 - 2) as i:
                for par in range(2):
                    self_normalise(2 * i + 1 + par, 1 - par)
                    add_up(2 * i + par)
            self_normalise(NT - 3, 1)
            add_up(NT - 4)
            low_part(up)
            self_normalise(NT - 2, 0)
            add_up(NT - 3)
            low_part(down)
            self_normalise(NT - 1, 1)
            for k in range(4):
                columns_low(k)
            for k in (NT - 2, NT - 1):
                add_up(k)

            def hidden_low(j):
                half, ic = divmod(j, HC)
                at = slice(half * HALF, (half + 1) * HALF)
                pool.wait_ge(hhi_ready, j + 1)
                nc.gpsimd.tensor_tensor(hm_lo[:, ic, at], hm[j % 2][:], hm_hi.bitcast(F32)[:, ic, at],
                                        ALU.subtract).then_inc(hlo_ready, 1)

            for j in range(NJ - 2):
                hidden_low(j)
                if j in (1, 2):
                    columns_low(2 + 2 * j)
                    columns_low(3 + 2 * j)
            pool.wait_ge(slots_zeroed, 16)
            pool.wait_ge(slots_ready, 1)
            for k in range(NT):
                for i in range(2):
                    nc.gpsimd.indirect_dma_start(x_slots, bass.IndirectOffsetOnAxis(slots[:, k, i:i + 1], 0), xx[:, k, :],
                                                 None).then_inc(scattered, 16)

            pool.wait_ge(scattered, 16 * 2 * NT)
            pool.wait_ge(slots_ready, 4)
            pool.wait_ge(split_ready, 1)
            zero = cst[:, C_ZERO:C_ZERO + 1].unsqueeze(2).broadcast_to([P, HC, D])
            for e in range(1, NR):
                for m in range(3):
                    pool.wait_ge(routed_loaded[m], 16 * (e + 1))
                    at = (slice(None), PLACES[e], m)
                    nc.gpsimd.tensor_tensor(ring_hi[at], ring_raw[at], zero, ALU.add).then_inc(split_hi, 1)
                    pool.wait_ge(split_hi, 3 * e + m + 1)
                    last = nc.gpsimd.tensor_tensor(ring_lo[at], ring_raw[at], ring_hi.bitcast(F32)[at], ALU.subtract)
                last.then_inc(split_ready, 1)
            for i in range(2):
                pool.wait_ge(y_stored[i], 16 * (TILES // 2))
            for k in range(NT):
                for i in range(2):
                    nc.gpsimd.indirect_dma_start(picked[2 * k + i][:], None, y_slots,
                                                 bass.IndirectOffsetOnAxis(slots[:, k, i:i + 1], 0)).then_inc(picked_loaded[picked_part(k)[0]], 16)

        def ring_out(copy, blk, g, g_keys, sem_done):
            if g >= g_keys and g < g_keys + T_FILLS:
                b, j = divmod(g - g_keys, JT)
                n = P if j < JM else TAIL
                src = bank[4 + g % RING][:].rearrange("p (c s) -> p c s", c=HC)[:, :, 0:n]
                copy(ctxT[b][:, :, j * P:j * P + n], src).then_inc(sem_done, 1)

        def prob_out(copy, g, f, sem_done):
            j0, j1 = 4 * f, min(4 * f + 4, JT)
            n = P if j1 <= JM else TAIL
            src = bank[4 + g % RING][0:n, 0:(j1 - j0) * P]
            copy(probT[0:n, j0:j1, :].rearrange("p j q -> p (j q)"), src).then_inc(sem_done, 1)

        @block.scalar
        def _(act):
            def keys_out(blk, g, g_keys):
                act.wait_ge(ring_full, BLOCK * blk + g - 3)
                ring_out(nc.scalar.copy, blk, g, g_keys, evac_act)

            def exps(n):
                s0, w = S_CHUNKS[n]
                nc.scalar.activation(prob[:, s0:s0 + w], bank[n][:, 0:w], ACT.Exp, bias=nmax[:, 0:1],
                                     accum_out=sums[:, n:n + 1]).then_inc(prob_ready, 1)

            def probs_out(blk, g0):
                for f in range(P_FILLS):
                    if (g0 + f) % 2 == 0:
                        act.wait_ge(ring_full, BLOCK * blk + g0 + f - 3)
                        prob_out(nc.scalar.copy, g0 + f, f, evac_act)

            def step(k):
                mine = list(range(0, T_FILLS, 2))
                keys_out(k + 1, mine[0], 0)
                act.wait_ge(nmax_ready, k + 1)
                for n in range(4):
                    exps(n)
                    keys_out(k + 1, mine[n + 1], 0)
                for g in mine[5:]:
                    keys_out(k + 1, g, 0)
                probs_out(k + 1, T_FILLS)

            for g in range(BLOCK - T_FILLS, BLOCK, 2):
                keys_out(0, g, BLOCK - T_FILLS)
            step(0)
            with act.Fori(0, NT // 2 - 1) as i:
                step(2 * i + 1)
                step(2 * i + 2)

            def weight_high(hi, raw, loaded):
                act.wait_ge(loaded, 16)
                n = raw.shape[1] // HC
                for c in range(HC):
                    nc.scalar.copy(hi[:, n * c:n * (c + 1), :], raw[:, n * c:n * (c + 1), :]).then_inc(whi_ready, 1)

            def norm_out(k):
                act.wait_ge(hT_full, k + 1)
                if k >= 2:
                    act.wait_ge(hlo_done, k - 1)
                for c in range(HC):
                    last = nc.scalar.activation(hf[k % 2][:, c].rearrange("p g (i b) -> p g i b", b=GB),
                                                bank[k % 4][:, c * P:(c + 1) * P].rearrange("p (i g b) -> p g i b", g=NG, b=GB),
                                                ACT.Identity, bias=vec[:, V_BETA + c:V_BETA + c + 1],
                                                scale=vec[:, V_GAMMA + c:V_GAMMA + c + 1])
                last.then_inc(hf_act, 1)

            def norm_high(k):
                act.wait_ge(hf_dve if k % 2 else hf_act, k // 2 + 1)
                nc.scalar.copy(h_hi[:, :, :, 2 * GB * k:2 * GB * (k + 1)], hf[k % 2][:]).then_inc(hhi_done, 1)

            def keys_half_out(m):
                half, n = divmod(m, NH)
                act.wait_ge(kT_full, m + 1)
                nc.scalar.copy(kT[:, n, :, half * BATCH:(half + 1) * BATCH],
                               bank[4 + m % 4][:].rearrange("p (g t) -> p g t", g=NG)).then_inc(kT_act, 1)

            weight_high(wq_hi, wq_raw, w_loaded["wq"])
            act.wait_ge(nmax_ready, NT)
            for n in range(4):
                exps(n)
            probs_out(NT, 0)
            act.wait_ge(x_loaded[1], 3 * 16)
            for k in range(0, NT - 2, 2):
                norm_out(k)
                norm_high(k)
                norm_high(k + 1)
            norm_out(NT - 2)
            norm_high(NT - 2)
            keys_half_out(0)
            keys_half_out(2)
            norm_high(NT - 1)
            keys_half_out(4)
            keys_half_out(6)
            act.wait_ge(rT_full, 1)
            weight_high(wv_hi, wv_raw, w_loaded["wv"])
            def pos_scores_out(half):
                act.wait_ge(bias_ready, 1)
                act.wait_ge(posT_full, 2 * half + 2)
                nc.scalar.activation(posT[0].rearrange("p g (b i) -> p g i b", i=SEQ)[:, :, half * GB:(half + 1) * GB, :],
                                     bank[2 - 2 * half][:].rearrange("p (g i b) -> p g i b", g=NG, b=GB), ACT.Identity,
                                     bias=pos_bias[:, 0:1]).then_inc(posT_ready, 1)

            for m in range(NH, 2 * NH, 2):
                if m == NH + NH // 2:
                    pos_scores_out(0)
                keys_half_out(m)
            pos_scores_out(1)

            def group_high(g, par):
                nc.scalar.copy(hg_hi[par][:], h_hi[:, :, ds(g, 1), :].rearrange("p c a t -> p (c a) t")).then_inc(hg_act, 1)

            def values_out(g, par):
                for h in range(2):
                    act.wait_ge(v_full, 2 * g + h + 1)
                    nc.scalar.copy(v_g[par][:, h * 512:(h + 1) * 512], bank[2 + h][:]).then_inc(v_out, 1)

            def group_exps(g, par):
                act.wait_ge(abias_ready, g + 1)
                for n in range(NH):
                    last = nc.scalar.activation(att[par][:, n, :], att[par][:, n, :], ACT.Exp, bias=a_bias[par][:, n:n + 1],
                                                scale=ATT_SCALE, accum_out=a_sum[par][:, n:n + 1])
                last.then_inc(exp_ready, 1)

            def weightsT_out(g):
                act.wait_ge(attT_full, 2 * g + 1)
                nc.scalar.copy(attT[:, 0:4, :].rearrange("p n q -> p (n q)"), bank[4][:]).then_inc(attT_act, 1)

            def group_out(g):
                act.wait_ge(o_full, 2 * g + 1)
                nc.scalar.copy(oT[:, 0:4, ds(g, 1), :].rearrange("p n a q -> p (n a) q"),
                               bank[6][:].rearrange("p (n q) -> p n q", n=4)).then_inc(o_act, 1)

            act.wait_ge(hlo_done, NT)
            group_high(0, 0)
            group_high(1, 1)
            for g in range(2):
                values_out(g, g)
            group_high(2, 0)
            for g in range(2):
                group_exps(g, g)

            def group_step(g, par):
                weightsT_out(g)
                group_out(g)
                group_exps(g + 2, par)
                values_out(g + 2, par)

            group_step(0, 0)
            weight_high(wout_hi, wout_raw, w_loaded["wout"])
            with act.Fori(0, NG // 2 - 2) as i:
                for par in (1, 0):
                    g = 2 * i + 2 - par
                    group_high(g + 2, par)
                    group_step(g, par)
            group_high(NG - 1, 1)
            group_step(NG - 3, 1)
            for g in (NG - 2, NG - 1):
                weightsT_out(g)
                group_out(g)

            def out_high(k, par):
                for i in range(2):
                    last = nc.scalar.copy(
                        o_hi[par][:, :, i * BATCH:(i + 1) * BATCH].rearrange("p n (g b) -> p n g b", b=GB),
                        oT[:, :, :, ds(2 * GB * k + i * GB, GB)])
                last.then_inc(ohi_ready, 1)

            act.wait_ge(o_dve, NG)
            act.wait_ge(o_act, NG)
            out_high(0, 0)
            out_high(1, 1)
            with act.Fori(0, NT // 2 - 1) as i:
                for par in range(2):
                    act.wait_ge(y2_full, 2 * i + par + 1)
                    out_high(2 * i + par + 2, par)

            def heads_out(k, par):
                act.wait_ge(k_full, k + 1)
                kr = bank[2][:].rearrange("p (a h d) -> p a h d", a=2, d=RD)
                if not (isinstance(k, int) and k == 0):
                    act.wait_ge(kq_ready, k)
                nc.scalar.copy(raw[:, 0:HEADS, :], kr[:, 0])
                nc.scalar.copy(kq[par][:, 0:HEADS, 0:RD], kr[:, 1])
                act.wait_ge(q_full, k + 1)
                qr = bank[1][:].rearrange("p (a h d) -> p a h d", a=2, d=RD)
                nc.scalar.copy(kq[par][:, HEADS:, 0:RD], qr[:, 0])
                nc.scalar.copy(raw[:, HEADS:, :], qr[:, 1]).then_inc(raw_ready, 1)
                act.wait_ge(vv_full, k + 1)
                nc.scalar.copy(v_t[par][:], bank[3][:]).then_inc(vv_ready, 1)

            def keys_spread(k, par):
                act.wait_ge(kTh_full, k + 1)
                for h in range(4):
                    rows_h = slice(HD * h, HD * (h + 1))
                    last = nc.scalar.copy(kT_h[par][rows_h, :, h, :], bank[3][rows_h, :].rearrange("p (c q) -> p c q", c=QUADS))
                last.then_inc(kTh_ready, 1)

            def self_exps(k, par, quads):
                for c in quads:
                    act.wait_ge(sbias_ready, 4 * k + c + 1)
                    for n in range(4):
                        h = 4 * c + n
                        last = nc.scalar.activation(sp_[par][:, h, :], score_bank(k, c)[:, n * P:(n + 1) * P], ACT.Exp,
                                                    bias=s_bias[par][:, h:h + 1], scale=SELF_SCALE,
                                                    accum_out=s_sum[par][:, h:h + 1])
                    last.then_inc(sexp_ready, 1)

            def weights_out(k, c):
                act.wait_ge(spT_full, 4 * k + c + 1)
                nc.scalar.copy(spT[:, 4 * c:4 * c + 4, :].rearrange("p n q -> p (n q)"), bank[6][:]).then_inc(spT_act, 1)

            def self_step(k, par, scores=True, project=True):
                weights_out(k, 0)
                if scores:
                    keys_spread(k + 1, 1 - par)
                else:
                    columns_high(2)
                    columns_high(3)
                weights_out(k, 2)
                if scores:
                    self_exps(k + 1, 1 - par, (0, 1))
                if project:
                    heads_out(k + 2, par)
                if scores:
                    self_exps(k + 1, 1 - par, (2, 3))

            gate, up, down = range(3)

            def high_part(m):
                nc.scalar.copy(w_hi[m][:], w_raw[m][:]).then_inc(whi_ready, 1)

            def columns_high(k):
                act.wait_ge(xf_ready, k + 1)
                nc.scalar.copy(xT_hi[:, :, k * P:(k + 1) * P], xf[k % 4][:]).then_inc(xhi_ready, 1)

            act.wait_ge(cleared, 2)
            heads_out(0, 0)
            keys_spread(0, 0)
            heads_out(1, 1)
            self_exps(0, 0, range(QUADS))
            act.wait_ge(raw_loaded, 4 * 16)
            nc.scalar.copy(wo_hi[:], wo_raw[:]).then_inc(whi_ready, 1)
            high_part(gate)
            self_step(0, 0)
            with act.Fori(0, NT // 2 - 2) as i:
                self_step(2 * i + 1, 1)
                self_step(2 * i + 2, 0)
            high_part(up)
            self_step(NT - 3, 1)
            high_part(down)
            self_step(NT - 2, 0, project=False)
            columns_high(0)
            columns_high(1)
            self_step(NT - 1, 1, scores=False, project=False)

            for j in range(NJ):
                half, ic = divmod(j, HC)
                act.wait_ge(gu_full, j + 1)
                nc.scalar.activation(act_g[j % 2][:], gate_bank(j)[:], ACT.Silu).then_inc(silu_ready, 1)
                act.wait_ge(hm_ready, j + 1)
                nc.scalar.copy(hm_hi[:, ic, half * HALF:(half + 1) * HALF], hm[j % 2][:]).then_inc(hhi_ready, 1)
                if j in (1, 2):
                    columns_high(2 + 2 * j)
                    columns_high(3 + 2 * j)
                elif j == 3:
                    act.wait_ge(logit_ready, 1)
                    nc.scalar.activation(r_p[:, :, 0:NR], r_p[:, :, 0:NR], ACT.Exp, scale=-1.0).then_inc(gate_ready, 1)

            for m in range(3):
                act.wait_ge(routed_loaded[m], 16)
                nc.scalar.copy(ring_hi[:, PLACES[0], m, :, :], ring_raw[:, PLACES[0], m, :, :]).then_inc(split_hi, 1)

            def load_rows(t, par):
                nc.scalar.dma_start(xg[par][:], x_slots[ds(t * P, P), :]).then_inc(xg_loaded[par], 16)

            def routed_silu(t):
                act.wait_ge(rgate_full, t + 1)
                nc.scalar.activation(rhm[:], bank[1][:], ACT.Silu).then_inc(rsilu_ready, 1)

            def hidden_columns_out(t):
                act.wait_ge(rhmT_full, t + 1)
                nc.scalar.copy(rhm_hi[:].rearrange("p c q -> p (c q)"), bank[3][:]).then_inc(rhm_split, 1)

            def output_rows(t, par, turn):
                act.wait_ge(rdown_full, t + 1)
                if not (isinstance(turn, int) and turn == 0):
                    act.wait_ge(y_stored[par], 16 * turn)
                nc.scalar.copy(yo[par][:], bank[4 + par][:]).then_inc(yo_ready, 1)
                act.wait_ge(yo_ready, t + 1)
                nc.scalar.dma_start(y_slots[ds(t * P, P), :], yo[par][:]).then_inc(y_stored[par], 16)

            act.wait_ge(scattered, 16 * 2 * NT)
            load_rows(0, 0)
            load_rows(1, 1)
            act.wait_ge(xgT_full, 1)
            load_rows(2, 0)
            routed_silu(0)
            hidden_columns_out(0)
            act.wait_ge(xgT_full, 2)
            load_rows(3, 1)
            routed_silu(1)
            output_rows(0, 0, 0)
            hidden_columns_out(1)

            def routed_step(t, par, turn, load=True):
                if load:
                    act.wait_ge(xgT_full, t + 1)
                    load_rows(t + 2, par)
                routed_silu(t)
                output_rows(t - 1, 1 - par, turn)
                hidden_columns_out(t)

            routed_step(2, 0, 0)
            routed_step(3, 1, 1)
            with act.Fori(0, TILES // 2 - 3) as i:
                routed_step(2 * i + 4, 0, i + 1)
                routed_step(2 * i + 5, 1, i + 2)
            routed_step(TILES - 2, 0, TILES // 2 - 2, load=False)
            routed_step(TILES - 1, 1, TILES // 2 - 1, load=False)
            output_rows(TILES - 1, 1, TILES // 2 - 1)

        @block.vector
        def _(dve):
            chain = Steps(dve, dve_step)

            def moments(m, st, t0, t1):
                for k in range(t0, t1):
                    chain.mark(dve.bn_aggr(m[:, k, :], st[:, k, :]))
                chain.wait()

            def rsqrt_guess(dst, v, at):
                half, t = rs_h[:, at], rs_t[:, at]
                chain(dve.tensor_scalar(half, v, -0.5, None, ALU.mult))
                chain(dve.tensor_scalar(t.bitcast(I32), v.bitcast(I32), 1, None, ALU.arith_shift_right))
                chain(dve.tensor_scalar(dst.bitcast(I32), t.bitcast(I32), -1.0, float(0x5F3759DF), ALU.mult, ALU.add))

            def newton(dst, steps, at):
                half, t = rs_h[:, at], rs_t[:, at]
                for _ in range(steps):
                    chain(dve.tensor_tensor(t, dst, dst, ALU.mult))
                    chain(dve.tensor_tensor(t, t, half, ALU.mult))
                    chain(dve.scalar_tensor_tensor(dst, t, 1.5, dst, ALU.add, ALU.mult))

            def rsqrt(dst, v, at=slice(0, NT)):
                rsqrt_guess(dst, v, at)
                newton(dst, 3, at)

            def queries(k):
                dve.tensor_scalar(qn[:], row(y, k), mean[:, ds(k, 1)], rstd[:, ds(k, 1)], ALU.subtract,
                                  ALU.mult).then_inc(qn_ready, 1)

            def queries_out(k):
                dve.wait_ge(qT_full, k + 1)
                dve.tensor_copy(qT[:].rearrange("p c q -> p (c q)"), bank[7][:]).then_inc(qT_ready, 1)

            def maxima(k):
                for n, (s0, w) in enumerate(S_CHUNKS):
                    dve.wait_ge(scores_full, 4 * k + n + 1)
                    chain.mark(dve.tensor_reduce(mx[:, n:n + 1], bank[n][:, 0:w], AX, ALU.max))
                chain.wait()
                dve.tensor_reduce(nmax[:], mx[:], AX, ALU.max, negate=True).then_inc(nmax_ready, 1)

            def keys_out(blk, g, g_keys):
                dve.wait_ge(ring_full, BLOCK * blk + g - 3)
                ring_out(dve.tensor_copy, blk, g, g_keys, evac_dve)

            def probs_out(k, blk, g0):
                dve.wait_ge(prob_ready, 4 * k + 4)
                chain(dve.tensor_reduce(total[:], sums[:], AX, ALU.add))
                chain(dve.reciprocal(rinv[:], total[:]))
                for f in range(P_FILLS):
                    if (g0 + f) % 2 == 1:
                        dve.wait_ge(ring_full, BLOCK * blk + g0 + f - 3)
                        prob_out(dve.tensor_copy, g0 + f, f, evac_dve)

            def finish(k):
                dve.wait_ge(context_full, k + 1)
                dve.scalar_tensor_tensor(row(y, k), bank[7][:], rinv[:, 0:1], row(y, k), ALU.mult,
                                         ALU.add).then_inc(y1_ready, 1)
                dve.wait_ge(y1_ready, k + 1)
                chain.mark(dve.bn_stats(row(stats2, k), row(y, k)))

            def step(k):
                queries(k + 1)
                maxima(k)
                queries_out(k + 1)
                for g in range(1, T_FILLS, 2):
                    keys_out(k + 1, g, 0)
                probs_out(k, k + 1, T_FILLS)
                finish(k)

            def first_norm(t0, t1):
                at = slice(t0, t1)
                for k in range(t0, t1):
                    chain.mark(dve.bn_stats(stats[:, k, :], y[:, k, :]))
                chain.wait()
                moments(mv, stats, t0, t1)
                chain(dve.tensor_scalar(rs_v[:, at], var[:, at], LN_EPS, None, ALU.add))
                rsqrt(rstd[:, at], rs_v[:, at], at)

            dve.wait_ge(x_loaded[0], 16)
            first_norm(0, 1)
            queries(0)
            for g in range(BLOCK - T_FILLS + 1, BLOCK, 2):
                keys_out(0, g, BLOCK - T_FILLS)
            queries_out(0)
            dve.wait_ge(x_loaded[1], 3 * 16)
            first_norm(1, NT)
            step(0)
            chain.enter()
            with dve.Fori(0, NT // 2 - 1) as i:
                chain.turn(i, 14)
                step(2 * i + 1)
                step(2 * i + 2)
            chain.leave(NT // 2 - 1)

            def double_norm(t0, t1):
                at = slice(t0, t1)
                chain.wait()
                moments(mv2, stats2, t0, t1)
                chain(dve.tensor_scalar(rs_v[:, at], mv2[:, at, 1], 1 + LN_EPS, LN_EPS ** 2, ALU.mult, ALU.add))
                rsqrt(rstd2[:, at], rs_v[:, at], at)

            def norm(k):
                if k >= 4:
                    dve.wait_ge(hT_full, k - 3)
                dve.tensor_scalar(hn[k % 4][:], y[:, k, :], mv2[:, k, 0:1], rstd2[:, k:k + 1], ALU.subtract,
                                  ALU.mult).then_inc(hn_ready, 1)

            def norm_out(k):
                dve.wait_ge(hT_full, k + 1)
                if k >= 2:
                    dve.wait_ge(hlo_done, k - 1)
                for c in range(HC):
                    last = dve.tensor_scalar(hf[k % 2][:, c].rearrange("p g (i b) -> p g i b", b=GB),
                                             bank[k % 4][:, c * P:(c + 1) * P].rearrange("p (i g b) -> p g i b", g=NG, b=GB),
                                             vec[:, V_GAMMA + c:V_GAMMA + c + 1], vec[:, V_BETA + c:V_BETA + c + 1],
                                             ALU.mult, ALU.add)
                last.then_inc(hf_dve, 1)

            def keys_half_out(m):
                half, n = divmod(m, NH)
                dve.wait_ge(kT_full, m + 1)
                dve.tensor_copy(kT[:, n, :, half * BATCH:(half + 1) * BATCH],
                                bank[4 + m % 4][:].rearrange("p (g t) -> p g t", g=NG)).then_inc(kT_dve, 1)

            dve.wait_ge(x_loaded[1], 3 * 16)
            double_norm(0, NT - 1)
            for k in range(4):
                norm(k)
            dve.tensor_copy(ident_bf[:], ident).then_inc(consts_cast, 1)
            dve.tensor_copy(block_bf[:], cst[:, C_BLOCK:C_BLOCK + P].unsqueeze(1).broadcast_to([P, 4, P])).then_inc(consts_cast, 1)
            maxima(NT - 1)
            probs_out(NT - 1, NT, 0)
            norm_out(1)
            norm(4)
            norm(5)
            norm_out(3)
            norm(6)
            finish(NT - 1)
            norm_out(5)
            double_norm(NT - 1, NT)
            norm(NT - 1)
            keys_half_out(1)
            norm_out(7)
            keys_half_out(3)
            dve.wait_ge(rT_full, 1)
            chain(dve.memset(rT_pad[:], 0.0))
            dve.tensor_copy(rT_pad[:, :, 0:SEQ], bank[2][:, 0:NH * SEQ].rearrange("p (n j) -> p n j", n=NH)).then_inc(rT_ready, 1)
            dve.memset(pos_sb[:, :, 0:NH], 0.0)

            def pos_scores_out(half):
                dve.wait_ge(posT_full, 2 * half + 3)
                dve.tensor_scalar(posT[1].rearrange("p g (b i) -> p g i b", i=SEQ)[:, :, half * GB:(half + 1) * GB, :],
                                  bank[3 - 2 * half][:].rearrange("p (g i b) -> p g i b", g=NG, b=GB), pos_bias[:, 1:2], None,
                                  ALU.add).then_inc(posT_ready, 1)

            for m in range(5, 2 * NH, 2):
                if m == NH + NH // 2 + 1:
                    dve.wait_ge(posT_full, 1)
                    dve.tensor_copy(pos_bias[:], bank[0][:, 0:2]).then_inc(bias_ready, 1)
                    dve.wait_ge(bias_ready, 1)
                    pos_scores_out(0)
                keys_half_out(m)
            pos_scores_out(1)
            for g in range(NG):
                dve.wait_ge(pos_full, g + 1)
                dve.tensor_tensor(pos_sb[:, g, NH:PADDED * NH].rearrange("p (j n) -> p n j", n=NH),
                                  bank[4 + g % 4][:, 0:2 * P].rearrange("p (n j) -> p n j", n=NH)[:, :, 0:SEQ],
                                  cst[:, C_TRIL + NH * g:C_TRIL + NH * (g + 1)].unsqueeze(2).broadcast_to([P, NH, SEQ]),
                                  ALU.mult).then_inc(pos_out, 1)

            def group_low(g, par):
                dve.tensor_copy(hg_lo[par][:], h_lo[:, :, ds(g, 1), :].rearrange("p c a t -> p (c a) t")).then_inc(hg_dve, 1)

            def group_max(g, par):
                for h in range(2):
                    dve.wait_ge(con_full, 2 * g + h + 1)
                    pos = pos_g[:, ds(g, 1), :].rearrange("p a (j n) -> p n (a j)", n=NH)[:, 4 * h:4 * h + 4, :].unsqueeze(3)
                    dve.tensor_tensor(att[par][:, 4 * h:4 * h + 4, :].rearrange("p n (j b) -> p n j b", b=GB),
                                      bank[h][:].rearrange("p (n j b) -> p n j b", n=4, b=GB),
                                      pos.broadcast_to([P, 4, SEQ, GB]), ALU.add).then_inc(con_out, 1)
                dve.wait_ge(con_out, 2 * g + 2)
                chain(dve.tensor_reduce(a_max[par][:], att[par][:], AX, ALU.max, negate=True))
                dve.tensor_scalar(a_bias[par][:], a_max[par][:], ATT_SCALE, None, ALU.mult).then_inc(abias_ready, 1)

            def group_inv(g, par):
                dve.wait_ge(exp_ready, g + 1)
                dve.reciprocal(a_inv[par][:], a_sum[par][:]).then_inc(ainv_ready, 1)

            def weightsT_out(g):
                dve.wait_ge(attT_full, 2 * g + 2)
                dve.tensor_copy(attT[:, 4:8, :].rearrange("p n q -> p (n q)"), bank[5][:]).then_inc(attT_dve, 1)

            def group_out(g):
                dve.wait_ge(o_full, 2 * g + 2)
                dve.tensor_copy(oT[:, 4:8, ds(g, 1), :].rearrange("p n a q -> p (n a) q"),
                                bank[7][:].rearrange("p (n q) -> p n q", n=4)).then_inc(o_dve, 1)

            def group_step(g, par):
                weightsT_out(g)
                group_max(g + 2, par)
                group_inv(g + 1, 1 - par)
                group_out(g)

            group_low(0, 0)
            group_low(1, 1)
            dve.wait_ge(pos_loaded, 16 * GB)
            group_max(0, 0)
            dve.wait_ge(v_full, 2)
            group_low(2, 0)
            group_max(1, 1)
            group_inv(0, 0)
            group_step(0, 0)
            chain.enter()
            with dve.Fori(0, NG // 2 - 2) as i:
                chain.turn(i, 2)
                for par in (1, 0):
                    g = 2 * i + 2 - par
                    dve.wait_ge(v_full, 2 * g + 2)
                    group_low(g + 2, par)
                    group_step(g, par)
            chain.leave(NG // 2 - 2)
            dve.wait_ge(v_full, 2 * (NG - 3) + 2)
            group_low(NG - 1, 1)
            group_step(NG - 3, 1)
            weightsT_out(NG - 2)
            group_inv(NG - 1, 1)
            group_out(NG - 2)
            weightsT_out(NG - 1)
            group_out(NG - 1)

            def out_low(k, par):
                dve.wait_ge(ohi_ready, k + 1)
                for i in range(2):
                    at = slice(i * BATCH, (i + 1) * BATCH)
                    last = dve.tensor_tensor(o_lo[par][:, :, at].rearrange("p n (g b) -> p n g b", b=GB),
                                             oT[:, :, :, ds(2 * GB * k + i * GB, GB)],
                                             o_hi[par].bitcast(F32)[:, :, at].rearrange("p n (g b) -> p n g b", b=GB),
                                             ALU.subtract)
                last.then_inc(olo_ready, 1)

            def out_added(k, par):
                dve.wait_ge(y2_full, k + 1)
                dve.tensor_tensor(row(y, k), bank[6 + par][:], row(y, k), ALU.add).then_inc(y2_ready, 1)
                dve.wait_ge(y2_ready, k + 1)
                chain.mark(dve.bn_stats(row(stats, k), row(y, k)))

            dve.wait_ge(o_act, NG)
            dve.wait_ge(o_dve, NG)
            out_low(0, 0)
            out_low(1, 1)
            dve.tensor_copy(causal_bf[:], cst[:, C_CAUSAL:C_CAUSAL + P].unsqueeze(1).broadcast_to([P, 4, P])).then_inc(causal_ready, 1)
            dve.wait_ge(bout_added, 1)
            chain.enter()
            with dve.Fori(0, NT // 2 - 2) as i:
                chain.turn(i, 2)
                for par in range(2):
                    out_added(2 * i + par, par)
                    out_low(2 * i + par + 2, par)
            chain.leave(NT // 2 - 2)

            def rms_begin(at):
                chain(dve.tensor_scalar(rs_v[:, at], rs_v[:, at], 1e-30, None, ALU.max))
                rsqrt_guess(rs_r[:, at], rs_v[:, at], at)

            def rms_end(dst, at):
                chain(dve.tensor_tensor(rs_r[:, at], rs_r[:, at], rs_v[:, at], ALU.mult))
                chain(dve.tensor_scalar(rs_r[:, at], rs_r[:, at], RMS_EPS, None, ALU.add))
                chain(dve.reciprocal(dst[:, at], rs_r[:, at]))

            def layer_factors(t0, t1):
                at = slice(t0, t1)
                chain.wait()
                moments(mv, stats, t0, t1)
                chain(dve.tensor_scalar(rs_v[:, at], var[:, at], LN_EPS, None, ALU.add))
                rsqrt(rstd[:, at], rs_v[:, at], at)

            def rms_factors(t0, t1):
                at = slice(t0, t1)
                chain(dve.tensor_tensor(rs_v[:, at], rstd[:, at], rstd[:, at], ALU.mult))
                chain(dve.tensor_tensor(rs_v[:, at], rs_v[:, at], var[:, at], ALU.mult))
                rms_begin(at)
                newton(rs_r[:, at], 3, at)
                rms_end(rms_x, at)
                chain(dve.tensor_tensor(rms_x[:, at], rms_x[:, at], rstd[:, at], ALU.mult))

            def self_norm(k, par):
                if not isinstance(k, int) or k >= 2:
                    dve.wait_ge(xnT_full, k - 1)
                dve.tensor_scalar(xn[par][:], row(y, k), mean[:, ds(k, 1)], rms_x[:, ds(k, 1)], ALU.subtract,
                                  ALU.mult).then_inc(xn_ready, 1)
                chain.mark(dve.tensor_scalar(row(xx, k), row(y, k), mean[:, ds(k, 1)], rstd[:, ds(k, 1)], ALU.subtract,
                                             ALU.mult))

            def norm_columns_out(k, par):
                dve.wait_ge(xnT_full, k + 1)
                for c in range(HC):
                    last = dve.tensor_scalar(xnT[par][:, c, :], bank[0][:, c * P:(c + 1) * P], vec[:, V_W1 + c:V_W1 + c + 1],
                                             None, ALU.mult)
                last.then_inc(xnT_ready, 1)

            def latents_out(k, par):
                dve.wait_ge(lat_full, k + 1)
                dve.tensor_copy(latT[par][:].rearrange("l a t -> l (a t)"), bank[1][:, 0:2 * P]).then_inc(lat_ready, 1)

            def rotate(k, par):
                dve.wait_ge(raw_ready, k + 1)
                cos = cst[:, C_COS:C_COS + RD].unsqueeze(1).broadcast_to([P, 2 * HEADS, RD])
                sin = cst[:, C_SIN:C_SIN + RD].unsqueeze(1).broadcast_to([P, 2 * HEADS, RD])
                half = RD // 2
                chain.mark(dve.tensor_tensor(kq[par][:, :, RD:HD], raw[:], cos, ALU.mult))
                chain.mark(dve.tensor_tensor(turned[:, :, 0:half], raw[:, :, half:RD], sin[:, :, 0:half], ALU.mult))
                chain(dve.tensor_tensor(turned[:, :, half:RD], raw[:, :, 0:half], sin[:, :, half:RD], ALU.mult))
                dve.tensor_tensor(kq[par][:, :, RD:HD], kq[par][:, :, RD:HD], turned[:], ALU.add).then_inc(kq_ready, 1)

            def queries_columns_out(k, par):
                dve.wait_ge(qTh_full, k + 1)
                dve.tensor_copy(qT_h[par][:].rearrange("p c q -> p (c q)"), bank[3][:]).then_inc(qTh_ready, 1)

            def self_max(k, par, quads):
                for c in quads:
                    dve.wait_ge(self_full, 4 * k + c + 1)
                    at = slice(4 * c, 4 * c + 4)
                    chain(dve.tensor_reduce(s_max[par][:, at], score_bank(k, c)[:].rearrange("p (n q) -> p n q", n=4), AX,
                                            ALU.max, negate=True))
                    dve.tensor_scalar(s_bias[par][:, at], s_max[par][:, at], SELF_SCALE, None, ALU.mult).then_inc(sbias_ready, 1)

            def self_inv(k, par, quads):
                for c in quads:
                    dve.wait_ge(sexp_ready, 4 * k + c + 1)
                    dve.reciprocal(s_inv[par][:, 4 * c:4 * c + 4], s_sum[par][:, 4 * c:4 * c + 4]).then_inc(sinv_ready, 1)

            def weights_columns_out(k, c):
                dve.wait_ge(spT_full, 4 * k + c + 1)
                dve.tensor_copy(spT[:, 4 * c:4 * c + 4, :].rearrange("p n q -> p (n q)"), bank[7][:]).then_inc(spT_dve, 1)

            def self_output_out(k):
                dve.wait_ge(yT_full, k + 1)
                dve.tensor_copy(y_hi[:].rearrange("p c q -> p (c q)"), bank[0][:]).then_inc(y_high, 1)
                dve.wait_ge(y_high, k + 1)
                dve.tensor_tensor(y_lo[:].rearrange("p c q -> p (c q)"), bank[0][:],
                                  y_hi.bitcast(F32)[:].rearrange("p c q -> p (c q)"), ALU.subtract).then_inc(yT_ready, 1)

            def output_added(k):
                dve.wait_ge(wo_full, k + 1)
                dve.tensor_tensor(row(xx, k), bank[6][:], row(xx, k), ALU.add).then_inc(xx_ready, 1)

            def expert_stats(t0, t1):
                dve.wait_ge(xx_ready, t1)
                for k in range(t0, t1):
                    chain.mark(dve.bn_stats(stats[:, k, :], xx[:, k, :]))

            def expert_moments(t0, t1):
                chain.wait()
                moments(mv, stats, t0, t1)

            def expert_begin(t0, t1):
                at = slice(t0, t1)
                chain(dve.tensor_tensor(rs_v[:, at], mean[:, at], mean[:, at], ALU.mult))
                chain(dve.tensor_tensor(rs_v[:, at], rs_v[:, at], var[:, at], ALU.add))
                rms_begin(at)

            def expert_newton(t0, t1, steps):
                newton(rs_r[:, t0:t1], steps, slice(t0, t1))

            def expert_scale(t0, t1):
                at = slice(t0, t1)
                rms_end(rms_f, at)
                dve.wait_ge(y_summed, t1)
                for k in range(t0, t1):
                    dve.tensor_scalar(xx[:, k, :], xx[:, k, :], rms_f[:, k:k + 1], None, ALU.mult).then_inc(xn2_ready, 1)

            def expert_columns_out(k):
                dve.wait_ge(xfT_full, k + 1)
                if k >= 4:
                    dve.wait_ge(logit_full, k - 3)
                    dve.wait_ge(xlo_ready, k - 3)
                for c in range(HC):
                    last = dve.tensor_scalar(xf[k % 4][:, c, :], bank[1 + k % 2][:, c * P:(c + 1) * P],
                                             vec[:, V_W2 + c:V_W2 + c + 1], None, ALU.mult)
                last.then_inc(xf_ready, 1)

            def self_step(k, par, norm=True, scores=True, project=True, between=(None, None, None)):
                if project:
                    norm_columns_out(k + 2, par)
                if scores:
                    queries_columns_out(k + 1, 1 - par)
                weights_columns_out(k, 1)
                if project:
                    latents_out(k + 2, par)
                weights_columns_out(k, 3)
                if between[0]:
                    between[0]()
                if scores:
                    self_max(k + 1, 1 - par, (0, 1))
                self_output_out(k)
                if between[1]:
                    between[1]()
                if norm:
                    self_norm(k + 3, 1 - par)
                if scores:
                    self_inv(k + 1, 1 - par, (0, 1))
                    self_max(k + 1, 1 - par, (2, 3))
                if project:
                    rotate(k + 2, par)
                if between[2]:
                    between[2]()
                if scores:
                    self_inv(k + 1, 1 - par, (2, 3))
                output_added(k)

            layer_factors(0, NT // 2)
            out_added(NT - 4, 0)
            out_low(NT - 2, 0)
            out_added(NT - 3, 1)
            out_low(NT - 1, 1)
            rms_factors(0, NT // 2)
            self_norm(0, 0)
            out_added(NT - 2, 0)
            norm_columns_out(0, 0)
            self_norm(1, 1)
            out_added(NT - 1, 1)
            latents_out(0, 0)
            norm_columns_out(1, 1)
            layer_factors(NT // 2, NT)
            rotate(0, 0)
            latents_out(1, 1)
            self_norm(2, 0)
            queries_columns_out(0, 0)
            rms_factors(NT // 2, NT)
            self_max(0, 0, range(QUADS))
            rotate(1, 1)
            self_inv(0, 0, range(QUADS))
            self_step(0, 0)
            chain.enter()
            with dve.Fori(0, NT // 2 - 2) as i:
                chain.turn(i, 16)
                self_step(2 * i + 1, 1)
                self_step(2 * i + 2, 0)
            chain.leave(NT // 2 - 2)
            half = (0, NT // 2)
            self_step(NT - 3, 1, norm=False, between=(lambda: [expert_stats(*half), expert_moments(*half)], lambda: expert_begin(*half),
                                                      lambda: expert_newton(*half, 1)))
            self_step(NT - 2, 0, norm=False, project=False, between=(lambda: expert_newton(*half, 2),
                                                                     lambda: expert_scale(*half),
                                                                     lambda: [expert_columns_out(k) for k in range(2)]))
            for k in range(2, 4):
                expert_columns_out(k)
            self_step(NT - 1, 1, norm=False, scores=False, project=False, between=(None, lambda: expert_stats(NT // 2, NT - 1), None))

            def logits_out():
                dve.wait_ge(logit_full, NT)
                dve.tensor_tensor(r_p[:, :, 0:NR], bank[3][:, 0:NT * NE].rearrange("p (k e) -> p k e", e=NE)[:, :, 0:NR],
                                  rbias_sb[:].unsqueeze(1).broadcast_to([P, NT, NR]), ALU.add).then_inc(logit_ready, 1)

            def per_expert(t):
                return t.unsqueeze(2).broadcast_to([P, NT, NE])

            def choose():
                dve.wait_ge(gate_ready, 1)
                chain(dve.tensor_scalar(r_p[:, :, 0:NR], r_p[:, :, 0:NR], 1.0, None, ALU.add))
                chain.mark(dve.memset(r_p[:, :, NR:NE], -1.0))
                chain(dve.reciprocal(r_p[:, :, 0:NR], r_p[:, :, 0:NR]))
                rank = cst[:, C_RANK:C_RANK + NE].unsqueeze(1).broadcast_to([P, NT, NE])
                for i in range(2):
                    chain(dve.tensor_reduce(gates[i][:], r_p[:], AX, ALU.max))
                    chain(dve.tensor_tensor(r_eq[:], r_p[:], per_expert(gates[i][:]), ALU.is_equal))
                    chain(dve.tensor_tensor(r_eq[:], r_eq[:], rank, ALU.mult))
                    chain(dve.tensor_reduce(r_key[:], r_eq[:], AX, ALU.max))
                    chain(dve.tensor_tensor(r_sel[i][:], r_eq[:], per_expert(r_key[:]), ALU.is_equal))
                    if i == 0:
                        chain(dve.scalar_tensor_tensor(r_p[:], r_sel[0][:], -4.0, r_p[:], ALU.mult, ALU.add))
                dve.tensor_tensor(r_picks[:], r_sel[0][:], r_sel[1][:], ALU.add).then_inc(picks_ready, 1)

            def allot():
                dve.wait_ge(ranks_full, 1)
                pairs, tiles, first = (r_first[:, i, :] for i in range(3))
                ranks = bank[3][:, 0:NT * NE].rearrange("p (k e) -> p k e", e=NE)
                chain(dve.tensor_copy(pairs, bank[3][:, NT * NE:(NT + 1) * NE]))
                square = [P, NE, NE]
                chain(dve.tensor_tensor(r_fill[:], pairs.unsqueeze(2).broadcast_to(square),
                                        cst[:, C_FILL:C_FILL + NE].unsqueeze(1).broadcast_to(square), ALU.is_gt))
                chain(dve.tensor_reduce(tiles, r_fill[:], AX, ALU.add))
                chain(dve.tensor_tensor(r_fill[:], tiles.unsqueeze(1).broadcast_to(square),
                                        cst[:, C_EARLIER:C_EARLIER + NE * NE].rearrange("p (e f) -> p e f", e=NE), ALU.mult))
                chain(dve.tensor_reduce(first, r_fill[:], AX, ALU.add))
                chain(dve.scalar_tensor_tensor(r_p[:], first.unsqueeze(1).broadcast_to([P, NT, NE]), float(P), ranks, ALU.mult,
                                               ALU.add))
                for i in range(2):
                    chain(dve.tensor_tensor(r_eq[:], r_sel[i][:], r_p[:], ALU.mult))
                    chain(dve.tensor_reduce(r_slot[:, :, i], r_eq[:], AX, ALU.add))
                dve.tensor_copy(slots[:], r_slot[:]).then_inc(slots_ready, 1)
                table = [P, TILES, NE]
                for i, at in enumerate((C_PLACE, C_NEED)):
                    chain(dve.tensor_tensor(r_begun[:], cst[:, C_TILE:C_TILE + TILES].unsqueeze(2).broadcast_to(table),
                                            first.unsqueeze(1).broadcast_to(table), ALU.is_ge))
                    chain(dve.tensor_tensor(r_begun[:], r_begun[:], cst[:, at:at + NE].unsqueeze(1).broadcast_to(table), ALU.mult))
                    chain(dve.tensor_reduce(r_tile[:, i, :], r_begun[:], AX, ALU.add))
                dve.tensor_copy(tile_expert[:], r_tile[:]).then_inc(slots_ready, 1)
                dve.tensor_copy(expert_begins[:], first).then_inc(slots_ready, 1)
                chain(dve.tensor_tensor(r_key[:], gates[0][:], gates[1][:], ALU.add))
                chain(dve.reciprocal(r_key[:], r_key[:]))
                chain.mark(dve.tensor_tensor(gates[0][:], gates[0][:], r_key[:], ALU.mult))
                dve.tensor_tensor(gates[1][:], gates[1][:], r_key[:], ALU.mult).then_inc(slots_ready, 1)
                dve.wait_ge(slots_ready, 4)
                chain.wait()

            expert_stats(NT - 1, NT)
            expert_moments(NT // 2, NT)
            expert_begin(NT // 2, NT)
            expert_newton(NT // 2, NT, 3)
            expert_scale(NT // 2, NT)
            dve.tensor_copy(below_bf[:], cst[:, C_BELOW:C_BELOW + P]).then_inc(consts_cast, 1)
            dve.memset(ones_bf[:], 1.0).then_inc(consts_cast, 1)
            dve.wait_ge(slots_zeroed, 16)
            for j in range(NJ):
                dve.wait_ge(silu_ready, j + 1)
                if j >= 2:
                    dve.wait_ge(hlo_ready, j - 1)
                dve.tensor_tensor(hm[j % 2][:], act_g[j % 2][:], up_bank(j)[:], ALU.mult).then_inc(hm_ready, 1)
                if j in (1, 2):
                    expert_columns_out(2 + 2 * j)
                    expert_columns_out(3 + 2 * j)
                elif j == 3:
                    logits_out()
                    choose()
                elif j == 5:
                    allot()
                if j >= NJ - 2:
                    half, ic = divmod(j, HC)
                    at = slice(half * HALF, (half + 1) * HALF)
                    dve.wait_ge(hhi_ready, j + 1)
                    dve.tensor_tensor(hm_lo[:, ic, at], hm[j % 2][:], hm_hi.bitcast(F32)[:, ic, at],
                                      ALU.subtract).then_inc(hlo_dve, 1)
            def down_out(k):
                dve.wait_ge(down_full, k + 1)
                dve.tensor_tensor(y[:, k, :], bank[k % 3][:], y[:, k, :], ALU.add).then_inc(down_added, 1)

            for k in range(NT - 1):
                down_out(k)
                if 1 <= k <= 3:
                    dve.wait_ge(split_hi, k)
                    at = (slice(None), PLACES[0], k - 1)
                    last = dve.tensor_tensor(ring_lo[at], ring_raw[at], ring_hi.bitcast(F32)[at], ALU.subtract)
                    if k == 3:
                        last.then_inc(split_ready, 1)

            def rows_columns_out(t, par):
                nth = dve.value_load(tile_expert[0:1, 1, ds(t, 1)], min_val=1, max_val=NR)
                dve.wait_ge(xgT_full, t + 1)
                columns = [bank[6 + par][:, c * P:(c + 1) * P] for c in range(HC)]
                weights = [vec[:, V_W2 + c:V_W2 + c + 1] for c in range(HC)]
                for c in range(HC):
                    last = dve.tensor_scalar(xg_hi[par][:, c, :], columns[c], weights[c], None, ALU.mult)
                last.then_inc(xg_split, 1)
                dve.wait_ge(xg_split, t + 1)
                dve.wait_ge(split_ready, nth)
                for c in range(HC):
                    last = dve.scalar_tensor_tensor(xg_lo[par][:, c, :], columns[c], weights[c], xg_hi[par].bitcast(F32)[:, c, :],
                                                    ALU.mult, ALU.subtract)
                last.then_inc(xgT_ready, 1)

            def routed_mult(t):
                dve.wait_ge(rup_full, t + 1)
                dve.wait_ge(rsilu_ready, t + 1)
                dve.tensor_tensor(rhm[:], rhm[:], bank[2][:], ALU.mult).then_inc(rhm_ready, 1)

            def hidden_split(t):
                dve.wait_ge(rhm_split, t + 1)
                dve.tensor_tensor(rhm_lo[:].rearrange("p c q -> p (c q)"), bank[3][:],
                                  rhm_hi.bitcast(F32)[:].rearrange("p c q -> p (c q)"), ALU.subtract).then_inc(rhmT_ready, 1)

            rows_columns_out(0, 0)
            down_out(NT - 1)
            rows_columns_out(1, 1)
            routed_mult(0)
            hidden_split(0)
            with dve.Fori(0, TILES // 2 - 1) as i:
                for par in range(2):
                    t = 2 * i + 1 + par
                    rows_columns_out(t + 1, par)
                    routed_mult(t)
                    hidden_split(t)
            routed_mult(TILES - 1)
            hidden_split(TILES - 1)
            for k in range(NT):
                part, tiles = picked_part(k)
                dve.wait_ge(picked_loaded[part], tiles * 2 * 16)
                chain(dve.scalar_tensor_tensor(y[:, k, :], picked[2 * k][:], gates[0][:, k:k + 1], y[:, k, :], ALU.mult, ALU.add))
                dve.scalar_tensor_tensor(y[:, k, :], picked[2 * k + 1][:], gates[1][:, k:k + 1], y[:, k, :], ALU.mult,
                                         ALU.add).then_inc(y_ready, 1)


def kernel(x, ctx_1024, L0_attn_gamma, L0_attn_beta, L0_attn_Wq, L0_attn_Wv, L0_attn_Wr, L0_attn_u_bias, L0_attn_v_bias,
           L0_attn_Wout, L0_attn_bout, L0_ffn_w_ln1, L0_ffn_w_ln2, L0_ffn_W_kvd, L0_ffn_W_qd, L0_ffn_W_ku, L0_ffn_W_qu,
           L0_ffn_W_vu, L0_ffn_W_ropeq, L0_ffn_W_ropek, L0_ffn_W_o, L0_ffn_Wg_s, L0_ffn_Wu_s, L0_ffn_Wd_s, L0_ffn_Wg_r,
           L0_ffn_Wu_r, L0_ffn_Wd_r, L0_ffn_W_router, L0_ffn_routing_bias):
    import concourse.bacc as bacc
    from concourse.bass_utils import run_bass_kernel_spmd

    def columns(v):
        return np.asarray(v).reshape(-1, P).T

    arrays = {
        "x": np.asarray(x).reshape(TOK, D),
        "ctx_keys": np.asarray(ctx_1024),
        "consts": shape_constants(),
        "vecs": np.concatenate([columns(v) for v in (L0_attn_gamma, L0_attn_beta, L0_ffn_w_ln1, L0_ffn_w_ln2,
                                                     L0_attn_u_bias, L0_attn_v_bias)], axis=1),
        "rows": np.concatenate([np.asarray(L0_attn_bout), np.asarray(L0_ffn_routing_bias)])[None, :],
        "Wq": L0_attn_Wq, "Wv": L0_attn_Wv, "Wr": L0_attn_Wr, "Wout": L0_attn_Wout,
        "Wkvd": L0_ffn_W_kvd, "Wqd": L0_ffn_W_qd, "Wku": L0_ffn_W_ku, "Wqu": L0_ffn_W_qu, "Wvu": L0_ffn_W_vu,
        "Wropeq": L0_ffn_W_ropeq, "Wropek": L0_ffn_W_ropek, "Wo": L0_ffn_W_o,
        "Wexp": np.stack([np.concatenate([np.asarray(s)[None], np.asarray(r)]) for s, r in (
            (L0_ffn_Wg_s, L0_ffn_Wg_r), (L0_ffn_Wu_s, L0_ffn_Wu_r), (L0_ffn_Wd_s, L0_ffn_Wd_r))]),
        "Wrouter": L0_ffn_W_router,
    }
    arrays = {f"in_{n}": np.ascontiguousarray(a) for n, a in arrays.items()}
    nc = bacc.Bacc("TRN2", target_bir_lowering=False, num_devices=1)
    args = [nc.dram_tensor(n, a.shape, mybir.dt.from_np(a.dtype), kind="ExternalInput").ap() for n, a in arrays.items()]
    args.append(nc.dram_tensor("out", (TOK, D), F32, kind="ExternalOutput").ap())
    perceiver_kernel(nc, *args)
    r = run_bass_kernel_spmd(nc, [arrays], core_ids=[0])
    return np.asarray(r.results[0]["out"]).reshape(16, 64, D)
```
